# Optimizing a Trainium2 kernel written in Bass

```python
import numpy as np
import jax
import jax.numpy as jnp

def _softmax(x, axis=-1):
    return jax.nn.softmax(x, axis=axis)

def _gelu(x):
    return jax.nn.gelu(x, approximate=True)

def _silu(x):
    return jax.nn.silu(x)

def _sigmoid(x):
    return jax.nn.sigmoid(x)

def _layernorm(x, axis=-1, eps=1e-05):
    m = jnp.mean(x, axis=axis, keepdims=True)
    v = jnp.var(x, axis=axis, keepdims=True)
    return (x - m) / jnp.sqrt(v + eps)

def _scatter_add(tgt, idx, src, axis=0):
    return tgt.at[idx].add(src)

def _segment_sum(src, seg, n):
    return jax.ops.segment_sum(src, seg, n)
kernel_name = 'mk_gnn_ffn_d1_gnn_r8_8b1130'

def setup_inputs(seed: int=0):
    np.random.seed(seed)
    _w = jnp.asarray

    def _rec_inputs():
        import jax
        import jax.numpy as jnp
        _gk = jax.random.key(seed)
        x = -0.0003713 + 1 * jax.random.normal(jax.random.fold_in(_gk, 1), (12500, 256), jnp.float32)
        _s = jax.random.randint(jax.random.fold_in(_gk, 2), (100000,), 0, 12500, jnp.int32)
        _d = jax.random.randint(jax.random.fold_in(_gk, 3), (100000,), 0, 12500, jnp.int32)
        _loop = jnp.arange(12500, dtype=jnp.int32)
        src = jnp.concatenate([_s, _d, _loop])
        dst = jnp.concatenate([_d, _s, _loop])
        _o = jnp.argsort(dst, stable=True)
        src = src[_o]
        dst = dst[_o]
        edge_attr_3 = -1.09012e-05 + 0.99985 * jax.random.normal(jax.random.fold_in(_gk, 11), (212500, 3), jnp.float32)
        return (x, src, dst, edge_attr_3)
    x, src, dst, edge_attr_3 = _rec_inputs()

    def _L0_gnn_setup():
        import jax, jax.numpy as jnp
        import numpy as np
        N = 6250
        E = 50000
        IN = 256
        H = 8
        D = 32
        EF = 3
        key = jax.random.key(seed)
        ks = jax.random.split(key, 8)
        x = jax.random.normal(ks[0], (N, IN), dtype=jnp.float32)
        edge_index = jax.random.randint(ks[1], (2, E), 0, N, dtype=jnp.int64)
        edge_attr = jax.random.normal(ks[2], (E, EF), dtype=jnp.float32)
        W = jax.random.normal(ks[3], (H * D, IN), dtype=jnp.float32) * np.float32(np.sqrt(2.0 / (IN + H * D)))
        a_src = jax.random.normal(ks[4], (H, D), dtype=jnp.float32) * np.float32(np.sqrt(2.0 / (H + D)))
        a_dst = jax.random.normal(ks[5], (H, D), dtype=jnp.float32) * np.float32(np.sqrt(2.0 / (H + D)))
        edge_W = jax.random.normal(ks[6], (H * D, EF), dtype=jnp.float32) * np.float32(np.sqrt(2.0 / (EF + H * D)))
        edge_b = jnp.zeros((H * D,), dtype=jnp.float32)
        bias = jnp.zeros((H * D,), dtype=jnp.float32)
        return {'x': x, 'W': W, 'a_src': a_src, 'a_dst': a_dst, 'edge_W': edge_W, 'edge_b': edge_b, 'bias': bias, 'edge_attr': edge_attr, 'edge_index': edge_index}
    _L0_gnn_all = _L0_gnn_setup()
    _L0_gnn_in = {k: v for k, v in _L0_gnn_all.items() if k in ('W', 'a_src', 'a_dst', 'edge_W', 'edge_b', 'bias')}
    del _L0_gnn_all

    def _L0_ffn_setup():
        import math
        import jax, jax.numpy as jnp
        import numpy as np
        CAPACITY_FACTOR = 1.25
        key = jax.random.key(seed)
        ks = jax.random.split(key, 5)
        B, L, D, F, E = (8, 1024, 256, 1024, 8)
        h = jax.random.normal(ks[0], (B, L, D), dtype=jnp.float32)
        gate_w = jax.random.normal(ks[1], (D, E), dtype=jnp.float32) * 0.02
        gate_b = jnp.zeros((E,), dtype=jnp.float32)
        w1 = jax.random.normal(ks[2], (E, D, F), dtype=jnp.float32) * (1.0 / math.sqrt(D))
        b1 = jnp.zeros((E, F), dtype=jnp.float32)
        w2 = jax.random.normal(ks[3], (E, F, D), dtype=jnp.float32) * (1.0 / math.sqrt(F))
        b2 = jnp.zeros((E, D), dtype=jnp.float32)
        return {'h': h, 'gate_w': gate_w, 'gate_b': gate_b, 'w1': w1, 'b1': b1, 'w2': w2, 'b2': b2}
    _L0_ffn_all = _L0_ffn_setup()
    _L0_ffn_in = {k: v for k, v in _L0_ffn_all.items() if k in ('gate_w', 'gate_b', 'w1', 'b1', 'w2', 'b2')}
    del _L0_ffn_all
    return {'x': x, 'src': src, 'dst': dst, 'edge_attr_3': edge_attr_3, 'L0_gnn_W': _L0_gnn_in['W'], 'L0_gnn_a_src': _L0_gnn_in['a_src'], 'L0_gnn_a_dst': _L0_gnn_in['a_dst'], 'L0_gnn_edge_W': _L0_gnn_in['edge_W'], 'L0_gnn_edge_b': _L0_gnn_in['edge_b'], 'L0_gnn_bias': _L0_gnn_in['bias'], 'L0_ffn_gate_w': _L0_ffn_in['gate_w'], 'L0_ffn_gate_b': _L0_ffn_in['gate_b'], 'L0_ffn_w1': _L0_ffn_in['w1'], 'L0_ffn_b1': _L0_ffn_in['b1'], 'L0_ffn_w2': _L0_ffn_in['w2'], 'L0_ffn_b2': _L0_ffn_in['b2']}

def reference(x, src, dst, edge_attr_3, L0_gnn_W, L0_gnn_a_src, L0_gnn_a_dst, L0_gnn_edge_W, L0_gnn_edge_b, L0_gnn_bias, L0_ffn_gate_w, L0_ffn_gate_b, L0_ffn_w1, L0_ffn_b1, L0_ffn_w2, L0_ffn_b2):
    import jax
    import jax.numpy as jnp

    def _L0_gnn_ref(x, W, a_src, a_dst, edge_W, edge_b, bias, edge_attr, edge_index):
        import jax, jax.numpy as jnp
        import numpy as np
        N = 6250
        E = 50000
        IN = 256
        H = 8
        D = 32
        EF = 3
        n = x.shape[0]
        h = (x @ W.T).reshape(n, H, D)
        src, dst = (edge_index[0], edge_index[1])
        h_src = h[src]
        h_dst = h[dst]
        alpha = jnp.einsum('ehd,hd->eh', h_src, a_src) + jnp.einsum('ehd,hd->eh', h_dst, a_dst)
        enc = jax.nn.relu(edge_attr @ edge_W.T + edge_b).reshape(-1, H, D)
        alpha = alpha + jnp.sum(enc * h_dst, axis=-1)
        alpha = jnp.where(alpha >= 0, alpha, 0.2 * alpha)
        amax = jax.ops.segment_max(alpha, dst, num_segments=n)
        ex = jnp.exp(alpha - amax[dst])
        denom = jax.ops.segment_sum(ex, dst, num_segments=n)
        attn = ex / jnp.maximum(denom[dst], 1e-10)
        out = jax.ops.segment_sum(h_src * attn[..., None], dst, num_segments=n)
        return out.reshape(n, H * D) + bias

    def _L0_ffn_ref(h, gate_w, gate_b, w1, b1, w2, b2):
        import math
        import jax, jax.numpy as jnp
        import numpy as np
        CAPACITY_FACTOR = 1.25
        B, L, D = h.shape
        E = gate_w.shape[1]
        T = B * L
        C = max(1, math.ceil(CAPACITY_FACTOR * T / E))
        x = h.reshape(T, D)
        logits = x @ gate_w + gate_b
        probs = jax.nn.softmax(logits, axis=-1)
        idx = jnp.argmax(probs, axis=-1)
        prb = jnp.take_along_axis(probs, idx[:, None], axis=1)[:, 0]
        one_hot = jax.nn.one_hot(idx, E, dtype=jnp.float32)
        pos = (jnp.cumsum(one_hot, axis=0) * one_hot).sum(-1).astype(jnp.int32) - 1
        kept = pos < C
        pos_safe = jnp.where(kept, pos, C)
        buf = jnp.zeros((E, C, D), dtype=h.dtype).at[idx, pos_safe].set(x, mode='drop')
        hmid = jax.nn.relu(jnp.einsum('ecd,edf->ecf', buf, w1) + b1[:, None, :])
        ybuf = jnp.einsum('ecf,efd->ecd', hmid, w2) + b2[:, None, :]
        pos_g = jnp.minimum(pos, C - 1)
        y_tok = ybuf[idx, pos_g] * (prb * kept)[:, None]
        y = y_tok.reshape(B, L, D)
        y = jnp.nan_to_num(y, nan=0.0, posinf=10000.0, neginf=-10000.0)
        return y
    edge_index = jnp.stack([src, dst])
    x = x + _L0_gnn_ref(_layernorm(x, axis=-1), L0_gnn_W, L0_gnn_a_src, L0_gnn_a_dst, L0_gnn_edge_W, L0_gnn_edge_b, L0_gnn_bias, edge_attr_3, edge_index)
    x = x + _L0_ffn_ref(_layernorm(x, axis=-1)[None], L0_ffn_gate_w, L0_ffn_gate_b, L0_ffn_w1, L0_ffn_b1, L0_ffn_w2, L0_ffn_b2)[0]
    return x

_drawn_inputs = setup_inputs


def setup_inputs(seed=0):
    import zlib

    import numpy as np

    out = dict(_drawn_inputs(seed))
    spreads = {'L0_gnn_edge_b': (0.0, 0.1),
     'L0_gnn_bias': (0.0, 0.1),
     'L0_ffn_gate_b': (0.0, 0.1),
     'L0_ffn_b1': (0.0, 0.695),
     'L0_ffn_b2': (0.0, 0.491)}
    factors = {}
    for name, (base, spread) in spreads.items():
        noise = np.random.default_rng([zlib.crc32(name.encode()), seed]).standard_normal(out[name].shape)
        drawn = base * np.exp(spread * noise) if base else spread * noise
        out[name] = jnp.asarray(drawn.astype(out[name].dtype))
    for name, factor in factors.items():
        out[name] = (out[name] * factor).astype(out[name].dtype)
    return out
```

```python
from contextlib import ExitStack

import concourse.bass as bass
from concourse import mybir

P = 128
ALU = mybir.AluOpType
ACT = mybir.ActivationFunctionType
AX = mybir.AxisListType
F32 = mybir.dt.float32
BF16 = mybir.dt.bfloat16
I32 = mybir.dt.int32

N = 12500
E = 212500
IN = 256
H, D = 8, 32
HD = H * D
KC = IN // P
NB = -(-N // P)
NPAD = NB * P
G = 4
IE = G * P
BATCH = 3
RING = 3
ITEMS_NEEDED = -(-E // IE) + NB
NBATCH = -(-ITEMS_NEEDED // (BATCH * RING)) * RING
NITEM = NBATCH * BATCH
NCHUNK = -(-(E + IE + 2) // P)
EP = NCHUNK * P
DG = D + 1
ROW = H * DG
DG_MAX = H + 1
VD = HD + H
EA = 3
KE = 35
EPS = 1e-5
BIG = 1e30
SENTINEL = NPAD + 7
T = BATCH * G

X = 8
F = 1024
CAP = -(-5 * N // (4 * X))
NT = -(-N // P) + X - 1
DUMP = NPAD


def at_least(eng, sem, value):
    if not isinstance(value, int) or value > 0:
        eng.wait_ge(sem, value)


def there(index, count):
    return not isinstance(index, int) or 0 <= index < count


def run_steps(eng, step, first, head, tail, last, unroll):
    for s in range(first, head):
        step(s, s % unroll, s // unroll)
    if tail > head:
        with eng.Fori(head // unroll, tail // unroll) as q:
            for u in range(unroll):
                step(unroll * q + u, u, q)
    for s in range(tail, last):
        step(s, s % unroll, s // unroll)


class Space:

    def __init__(self, nc, ctx, prefix):
        self.nc, self.ctx, self.prefix = nc, ctx, prefix
        ctx.enter_context(nc.cleanup_on_exit())

    def sb(self, name, shape, dt=F32):
        return self.ctx.enter_context(self.nc.sbuf_tensor(self.prefix + name, shape, dt))

    def ps(self, name, shape, dt=F32):
        return self.ctx.enter_context(self.nc.psum_tensor(self.prefix + name, shape, dt))

    def sem(self, name):
        return self.nc.alloc_semaphore(self.prefix + name)


def make_identity(nc, pool, ident, cleared, ready):
    nc.gpsimd.memset(ident[:], 0.0).then_inc(cleared, 1)
    pool.wait_ge(cleared, 1)
    nc.gpsimd.affine_select(out=ident[:], in_=ident[:], compare_op=ALU.not_equal, fill=1.0, base=0,
                            pattern=[[-1, P]], channel_multiplier=1).then_inc(ready, 1)


def node_phase(nc, ident, x_pad, w_t, a_src, a_dst, src_table, dst_table):
    GW = HD + 2 * H
    with ExitStack() as ctx:
        m = Space(nc, ctx, "n_")
        waug = m.sb("waug", [P, KC, GW])
        arep = m.sb("arep", [P, 2, HD])
        prod = m.sb("prod", [P, KC, HD])
        x = [m.sb(f"x{u}", [P, IN]) for u in range(4)]
        stats = [m.sb(f"stats{u}", [P, 6]) for u in range(2)]
        mv = [m.sb(f"mv{u}", [P, 2]) for u in range(2)]
        veps = [m.sb(f"veps{u}", [P, 1]) for u in range(2)]
        std = [m.sb(f"std{u}", [P, 1]) for u in range(2)]
        rstd = [m.sb(f"rstd{u}", [P, 1]) for u in range(2)]
        xn = [m.sb(f"xn{u}", [P, IN]) for u in range(2)]
        xnt = [m.sb(f"xnt{u}", [P, KC, P]) for u in range(2)]
        srow = [m.sb(f"srow{u}", [P, H, DG]) for u in range(2)]
        drow = [m.sb(f"drow{u}", [P, 3, VD], BF16) for u in range(2)]
        rest = [m.sb(f"rest{u}", [P, VD]) for u in range(2)]
        tp = [m.ps(f"tp{u}", [P, 512]) for u in range(2)]
        gp = [m.ps(f"gp{u}", [P, 512]) for u in range(2)]

        weights_in = m.sem("weights_in")
        x_in = [m.sem(f"x_in{u}") for u in range(4)]
        srow_out = [m.sem(f"srow_out{u}") for u in range(2)]
        drow_out = [m.sem(f"drow_out{u}") for u in range(2)]
        ident_cleared = m.sem("ident_cleared")
        ident_ready = m.sem("ident_ready")
        prod_ready = m.sem("prod_ready")
        waug_ready = m.sem("waug_ready")
        stats_ready = m.sem("stats_ready")
        mv_ready = m.sem("mv_ready")
        var_ready = m.sem("var_ready")
        std_ready = m.sem("std_ready")
        rstd_ready = m.sem("rstd_ready")
        xn_ready = m.sem("xn_ready")
        tp_ready = m.sem("tp_ready")
        xnt_ready = m.sem("xnt_ready")
        gp_ready = m.sem("gp_ready")
        srow_ready = m.sem("srow_ready")
        rest_ready = m.sem("rest_ready")
        mid_ready = m.sem("mid_ready")
        lo_ready = m.sem("lo_ready")
        block = ctx.enter_context(nc.Block())

        def steps(eng, step):
            run_steps(eng, step, -2, 4, (NB - 4) // 4 * 4, NB + 1, 4)

        @block.sync
        def _(sp):
            for k in range(KC):
                sp.dma_start(waug[:, k, 0:HD], w_t[k * P:(k + 1) * P, :]).then_inc(weights_in, 16)
            sp.dma_start(arep[:, 0, :], a_dst.to_broadcast([P, HD])).then_inc(weights_in, 16)
            sp.dma_start(arep[:, 1, :], a_src.to_broadcast([P, HD])).then_inc(weights_in, 16)

            for b in range(2):
                sp.dma_start(x[b][:], x_pad[b * P:(b + 1) * P, :]).then_inc(x_in[b], 16)

            def step(s, u, q):
                if not isinstance(s, int) or s + 4 < NB:
                    w = (u + 4) % 4
                    at_least(sp, xn_ready, s + 1)
                    sp.dma_start(x[w][:], x_pad[bass.ds((s + 4) * P, P), :]).then_inc(x_in[w], 16)
                if there(s - 1, NB):
                    v = (u + 1) % 2
                    sp.wait_ge(srow_ready, s)
                    sp.dma_start(src_table[bass.ds((s - 1) * P, P), :],
                                 srow[v][:].rearrange("p h d -> p (h d)")).then_inc(srow_out[v], 16)
                    sp.wait_ge(lo_ready, s)
                    sp.dma_start(dst_table[bass.ds((s - 1) * P, P), :],
                                 drow[v][:].rearrange("p s v -> p (s v)")).then_inc(drow_out[v], 16)

            steps(sp, step)
            for u in range(2):
                sp.wait_ge(srow_out[u], 16 * NB // 2)
                sp.wait_ge(drow_out[u], 16 * NB // 2)

        @block.gpsimd
        def _(pool):
            make_identity(nc, pool, ident, ident_cleared, ident_ready)

        @block.tensor
        def _(pe):
            pe.wait_ge(ident_ready, 1)
            pe.wait_ge(waug_ready, KC * 2)

            def step(s, u, q):
                if not there(s, NB):
                    return
                v = u % 2
                pe.wait_ge(xn_ready, s + 1)
                at_least(pe, xnt_ready, s - 1)
                for k in range(KC):
                    ins = nc.tensor.transpose(tp[v][:, k * P:(k + 1) * P], xn[v][:, k * P:(k + 1) * P], ident[:])
                ins.then_inc(tp_ready, 1)
                pe.wait_ge(xnt_ready, s + 1)
                at_least(pe, rest_ready, s - 1)
                for k in range(KC):
                    ins = nc.tensor.matmul(gp[v][:, 0:GW], xnt[v][:, k, :], waug[:, k, :],
                                           start=(k == 0), stop=(k == KC - 1))
                ins.then_inc(gp_ready, 1)

            steps(pe, step)

        @block.vector
        def _(dve):
            dve.wait_ge(weights_in, 16 * (KC + 2))
            for s in range(2):
                for k in range(KC):
                    nc.vector.tensor_tensor(prod[:, k, :], waug[:, k, 0:HD], arep[:, s, :],
                                            ALU.mult).then_inc(prod_ready, 1)
                dve.wait_ge(prod_ready, KC * (s + 1))
                for k in range(KC):
                    nc.vector.tensor_reduce(waug[:, k, HD + s * H:HD + (s + 1) * H],
                                            prod[:, k, :].rearrange("p (h d) -> p h d", d=D),
                                            AX.X, ALU.add).then_inc(waug_ready, 1)
                dve.wait_ge(waug_ready, KC * (s + 1))

            def step(s, u, q):
                v, w = u % 2, (u + 1) % 2
                if there(s + 2, NB):
                    xs = (u + 2) % 4
                    dve.wait_ge(x_in[xs], 16 * (q + (u + 2) // 4 + 1))
                    nc.vector.bn_stats(stats[v][:], x[xs][:]).then_inc(stats_ready, 1)
                if there(s + 1, NB):
                    dve.wait_ge(std_ready, s + 2)
                    if there(s + 2, NB):
                        dve.wait_ge(stats_ready, s + 3)
                    nc.vector.reciprocal(rstd[w][:], std[w][:]).then_inc(rstd_ready, 1)
                if there(s + 2, NB):
                    if isinstance(s, int):
                        dve.wait_ge(stats_ready, s + 3)
                    nc.vector.bn_aggr(mv[v][:], stats[v][:]).then_inc(mv_ready, 1)
                if there(s + 1, NB):
                    dve.wait_ge(rstd_ready, s + 2)
                    at_least(dve, tp_ready, s)
                    xs = (u + 1) % 4
                    nc.vector.tensor_scalar(xn[w][:], x[xs][:], mv[w][:, 0:1], rstd[w][:], ALU.subtract,
                                            ALU.mult).then_inc(xn_ready, 1)
                if there(s + 2, NB):
                    dve.wait_ge(mv_ready, s + 3)
                    at_least(dve, std_ready, s + 1)
                    nc.vector.tensor_scalar_add(veps[v][:], mv[v][:, 1:2], EPS).then_inc(var_ready, 1)
                if there(s - 1, NB):
                    v = (u + 1) % 2
                    dve.wait_ge(srow_ready, s)
                    nc.vector.tensor_tensor(rest[v][:], gp[v][:, 0:VD], drow[v][:, 0, :],
                                            ALU.subtract).then_inc(rest_ready, 1)
                    dve.wait_ge(mid_ready, s)
                    nc.vector.tensor_tensor(drow[v][:, 2, :], rest[v][:], drow[v][:, 1, :],
                                            ALU.subtract).then_inc(lo_ready, 1)

            steps(dve, step)

        @block.scalar
        def _(act):
            def step(s, u, q):
                v = (u + 1) % 2
                if there(s + 2, NB):
                    act.wait_ge(var_ready, s + 3)
                    at_least(act, rstd_ready, s + 1)
                    nc.scalar.activation(std[u % 2][:], veps[u % 2][:], ACT.Sqrt).then_inc(std_ready, 1)
                if there(s, NB):
                    w = u % 2
                    act.wait_ge(tp_ready, s + 1)
                    at_least(act, gp_ready, s - 1)
                    nc.scalar.copy(xnt[w][:], tp[w][:, 0:IN].rearrange("p (k t) -> p k t", k=KC)).then_inc(
                        xnt_ready, 1)
                if there(s - 1, NB):
                    act.wait_ge(gp_ready, s)
                    at_least(act, drow_out[v], 16 * (2 * q + (u - 1) // 2))
                    at_least(act, srow_out[v], 16 * (2 * q + (u - 1) // 2))
                    nc.scalar.copy(drow[v][:, 0, :], gp[v][:, 0:VD])
                    nc.scalar.copy(srow[v][:, :, 0:D], gp[v][:, 0:HD].rearrange("p (h d) -> p h d", d=D))
                    nc.scalar.copy(srow[v][:, :, D], gp[v][:, VD:VD + H]).then_inc(srow_ready, 1)
                    act.wait_ge(rest_ready, s)
                    nc.scalar.copy(drow[v][:, 1, :], rest[v][:]).then_inc(mid_ready, 1)

            steps(act, step)


def setup_phase(nc, ident, tables, dst_heads, dst_chunks, edge_attr_t, edge_w_t, edge_b, edge_parts):
    item_edge, item_block, neg_node, wparts = tables
    COLS = EA * EP // P
    HALF = NITEM // 2
    with ExitStack() as ctx:
        m = Space(nc, ctx, "s_")
        heads_i = m.sb("heads_i", [P, NCHUNK], I32)
        heads = m.sb("heads", [P, NCHUNK])
        below = m.sb("below", [P, NCHUNK])
        thr_i = m.sb("thr_i", [P, 1], I32)
        thr = m.sb("thr", [P, 1])
        part_i = m.sb("part_i", [P, 1], I32)
        part = m.sb("part", [P, 1])
        num_i = m.sb("num_i", [P, NITEM], I32)
        num = m.sb("num", [P, NITEM])
        chunk = m.sb("chunk", [P, 1])
        chunk_i = m.sb("chunk_i", [P, 1], I32)
        rows_i = m.sb("rows_i", [P, P], I32)
        rows = m.sb("rows", [P, P])
        inside = m.sb("inside", [P, 1])
        first = m.sb("first", [P, 1])
        shifted = m.sb("shifted", [P, P])
        diff = m.sb("diff", [P, P])
        upto = m.sb("upto", [P, P])
        count = m.sb("count", [P, 1], I32)
        items_i = m.sb("items_i", [P, 1], I32)
        items = m.sb("items", [P, 1])
        ends = m.sb("ends", [P, 1])
        begins = m.sb("begins", [P, 1])
        base = m.sb("base", [P, 1])
        ones = m.sb("ones", [P, P])
        base_rep = m.sb("base_rep", [P, P])
        past = m.sb("past", [P, NITEM])
        at = m.sb("at", [P, NITEM])
        blk = m.sb("blk", [P, NITEM])
        edge = m.sb("edge", [P, NITEM])
        ea = m.sb("ea", [P, COLS])
        ea_rest = m.sb("ea_rest", [P, COLS])
        ea_part = [m.sb(f"ea_part{i}", [P, COLS], BF16) for i in range(3)]
        wf = m.sb("wf", [KE, HD])
        wrest = m.sb("wrest", [KE, HD])
        wpart = [m.sb(f"wpart{i}", [KE, HD], BF16) for i in range(3)]
        ps_small = m.ps("ps_small", [P, 512])
        ps_edge = [m.ps(f"ps_edge{i}", [P, 512]) for i in range(2)]
        ps_blk = [m.ps(f"ps_blk{i}", [P, 512]) for i in range(2)]

        heads_in = m.sem("heads_in")
        rows_in = m.sem("rows_in")
        ea_in = m.sem("ea_in")
        ea_out = m.sem("ea_out")
        w_in = m.sem("w_in")
        w_cleared = m.sem("w_cleared")
        w_out = m.sem("w_out")
        const_ready = m.sem("const_ready")
        cleared = m.sem("cleared")
        step = m.sem("step")
        chunk_ready = m.sem("chunk_ready")
        first_ready = m.sem("first_ready")
        count_ready = m.sem("count_ready")
        items_ready = m.sem("items_ready")
        ends_ready = m.sem("ends_ready")
        at_ready = m.sem("at_ready")
        spread = m.sem("spread")
        ea_step = m.sem("ea_step")
        ea_turn = m.sem("ea_turn")
        block = ctx.enter_context(nc.Block())

        @block.sync
        def _(sp):
            sp.dma_start(heads_i[:], dst_heads.to_broadcast([P, NCHUNK])).then_inc(heads_in, 16)
            flat = edge_attr_t.rearrange("k e -> (k e)").rearrange("(p c) -> p c", p=P)
            sp.dma_start(ea[:], flat).then_inc(ea_in, 16)
            sp.wait_ge(w_cleared, 2)
            for g in range(9):
                sp.dma_start(wf[EA * g:EA * (g + 1), :], edge_w_t).then_inc(w_in, 16)
            for j in range(3):
                sp.dma_start(wf[32 + j:33 + j, :], edge_b).then_inc(w_in, 16)
            sp.wait_ge(ea_step, 4)
            for j in range(3):
                sp.dma_start(wparts[9 * j:9 * j + 9, :], wpart[j][9 * j:9 * j + 9, :]).then_inc(w_out, 16)
                sp.dma_start(wparts[32 + j:33 + j, :], wpart[j][32 + j:33 + j, :]).then_inc(w_out, 16)
            sp.wait_ge(ea_step, 8)
            for j in range(3):
                for i in range(3):
                    rows_out = edge_parts[9 * j + EA * i:9 * j + EA * (i + 1), :]
                    sp.dma_start(rows_out.rearrange("k e -> (k e)").rearrange("(p c) -> p c", p=P),
                                 ea_part[i][:]).then_inc(ea_out, 16)
            sp.wait_ge(w_out, 6 * 16)
            sp.wait_ge(ea_out, 9 * 16)

        @block.gpsimd
        def _(pool):
            nc.gpsimd.iota(thr_i[:], pattern=[[0, 1]], base=0, channel_multiplier=P).then_inc(const_ready, 1)
            nc.gpsimd.iota(part_i[:], pattern=[[0, 1]], base=0, channel_multiplier=1).then_inc(const_ready, 1)
            nc.gpsimd.iota(num_i[:], pattern=[[1, NITEM]], base=0, channel_multiplier=0).then_inc(const_ready, 1)
            nc.gpsimd.memset(ones[:], 1.0).then_inc(cleared, 1)
            nc.gpsimd.memset(shifted[:], 0.0).then_inc(cleared, 1)
            pool.wait_ge(cleared, 2)
            nc.gpsimd.affine_select(out=shifted[:], in_=shifted[:], compare_op=ALU.not_equal, fill=1.0, base=-1,
                                    pattern=[[-1, P]], channel_multiplier=1).then_inc(const_ready, 1)
            nc.gpsimd.affine_select(out=upto[:], in_=ones[:], compare_op=ALU.is_ge, fill=0.0, base=0,
                                    pattern=[[1, P]], channel_multiplier=-1).then_inc(const_ready, 1)
            pool.wait_ge(chunk_ready, 1)
            nc.gpsimd.indirect_dma_start(out=rows_i[:], out_offset=None, in_=dst_chunks,
                                         in_offset=bass.IndirectOffsetOnAxis(ap=chunk_i[:, 0:1], axis=0)
                                         ).then_inc(rows_in, 16)
            pool.wait_ge(rows_in, 16)

        @block.tensor
        def _(pe):
            pe.wait_ge(first_ready, 2)
            nc.tensor.matmul(ps_small[:, 0:1], diff[:], first[:], start=True, stop=True).then_inc(count_ready, 1)
            pe.wait_ge(items_ready, 1)
            nc.tensor.matmul(ps_small[0:NB, 1:2], upto[0:NB, 0:NB], items[0:NB, :], start=True,
                             stop=True).then_inc(ends_ready, 1)
            pe.wait_ge(at_ready, 1)
            for i in range(2):
                cols = slice(HALF * i, HALF * (i + 1))
                nc.tensor.matmul(ps_edge[i][:, 0:HALF], base_rep[0:NB, :], at[0:NB, cols], start=True, stop=True)
                ins = nc.tensor.matmul(ps_blk[i][:, 0:HALF], ones[0:NB, :], past[0:NB, cols], start=True, stop=True)
            ins.then_inc(spread, 1)

        @block.vector
        def _(dve):
            done = [0]

            def link(ins):
                done[0] += 1
                ins.then_inc(step, 1)
                dve.wait_ge(step, done[0])

            v = nc.vector
            v.memset(wf[:], 0.0).then_inc(w_cleared, 1)
            v.memset(wparts[:], 0.0).then_inc(w_cleared, 1)
            dve.wait_ge(const_ready, 5)
            v.tensor_copy(thr[:], thr_i[:])
            v.tensor_copy(part[:], part_i[:])
            v.tensor_copy(num[:], num_i[:])
            dve.wait_ge(heads_in, 16)
            link(v.tensor_copy(heads[:], heads_i[:]))
            link(v.tensor_scalar(below[:], heads[:], thr[:], None, ALU.is_lt))
            link(v.tensor_reduce(chunk[:], below[:], AX.X, ALU.add))
            link(v.tensor_scalar(chunk[:], chunk[:], -1.0, 0.0, ALU.add, ALU.max))
            v.tensor_copy(chunk_i[:], chunk[:]).then_inc(chunk_ready, 1)
            dve.wait_ge(rows_in, 16)
            link(v.tensor_copy(rows[:], rows_i[:]))
            link(v.tensor_scalar(rows[:], rows[:], thr[:], None, ALU.is_lt))
            link(v.tensor_reduce(inside[:], rows[:], AX.X, ALU.add))
            v.scalar_tensor_tensor(out=first[:], in0=chunk[:], scalar=float(P), in1=inside[:], op0=ALU.mult,
                                   op1=ALU.add).then_inc(first_ready, 1)
            v.tensor_tensor(diff[:], shifted[:], ident[:], ALU.subtract).then_inc(first_ready, 1)
            dve.wait_ge(count_ready, 1)
            link(v.tensor_scalar(count[:], ps_small[:, 0:1], float(IE - 1), None, ALU.add))
            link(v.tensor_scalar(items_i[:], count[:], IE.bit_length() - 1, None, ALU.logical_shift_right))
            link(v.tensor_copy(items[:], items_i[:]))
            dve.sem_inc(items_ready, 1)
            dve.wait_ge(ends_ready, 1)
            dve.wait_ge(first_ready, 2)
            link(v.tensor_copy(ends[0:NB, :], ps_small[0:NB, 1:2]))
            link(v.tensor_tensor(begins[0:NB, :], ends[0:NB, :], items[0:NB, :], ALU.subtract))
            link(v.scalar_tensor_tensor(out=base[0:NB, :], in0=begins[0:NB, :], scalar=-float(IE),
                                        in1=first[0:NB, :], op0=ALU.mult, op1=ALU.add))
            link(v.tensor_scalar(base_rep[0:NB, :], ones[0:NB, :], base[0:NB, :], None, ALU.mult))
            link(v.tensor_scalar(past[0:NB, :], num[0:NB, :], ends[0:NB, :], None, ALU.is_ge))
            link(v.tensor_scalar(at[0:NB, :], num[0:NB, :], begins[0:NB, :], None, ALU.is_ge))
            v.tensor_tensor(at[0:NB, :], at[0:NB, :], past[0:NB, :], ALU.subtract).then_inc(at_ready, 1)
            dve.wait_ge(spread, 1)
            for i in range(2):
                cols = slice(HALF * i, HALF * (i + 1))
                link(v.scalar_tensor_tensor(out=edge[:, cols], in0=num[:, cols], scalar=float(IE),
                                            in1=ps_edge[i][:, 0:HALF], op0=ALU.mult, op1=ALU.add))
                link(v.tensor_scalar(blk[:, cols], ps_blk[i][:, 0:HALF], float(NB - 1), None, ALU.min))
            v.tensor_scalar(item_edge[:], edge[0:1, :], float(E), None, ALU.min)
            v.tensor_copy(item_block[:], blk[0:1, :])
            v.tensor_scalar(neg_node[:], blk[:], -float(P), part[:], ALU.mult, ALU.subtract)

            for turn, (whole, rest, parts, loaded, n) in enumerate(
                    [(wf, wrest, wpart, w_in, 12), (ea, ea_rest, ea_part, ea_in, 1)]):
                dve.wait_ge(ea_turn, 2 * turn + 1)
                v.tensor_tensor(rest[:], whole[:], parts[0][:], ALU.subtract).then_inc(ea_step, 1)
                dve.wait_ge(ea_turn, 2 * turn + 2)
                dve.wait_ge(ea_step, 4 * turn + 1)
                v.tensor_tensor(parts[2][:], rest[:], parts[1][:], ALU.subtract).then_inc(ea_step, 3)

        @block.scalar
        def _(act):
            for turn, (whole, rest, parts, loaded, n) in enumerate(
                    [(wf, wrest, wpart, w_in, 12), (ea, ea_rest, ea_part, ea_in, 1)]):
                act.wait_ge(loaded, 16 * n)
                nc.scalar.copy(parts[0][:], whole[:]).then_inc(ea_turn, 1)
                act.wait_ge(ea_step, 4 * turn + 1)
                nc.scalar.copy(parts[1][:], rest[:]).then_inc(ea_turn, 1)


def edge_phase(nc, ident, tables, acc, src_pad, dst_ext, edge_parts, src_table, dst_table):
    item_edge, item_block, neg_node, wparts = tables
    PR = BATCH * H
    FH = 2 * HD
    NHALF = T // 2
    with ExitStack() as ctx:
        m = Space(nc, ctx, "e_")
        idx = [m.sb(f"idx{u}", [P, T], I32) for u in range(RING)]
        rows = [m.sb(f"rows{u}", [P, T, H, DG]) for u in range(RING)]
        onehot_t = [m.sb(f"onehot_t{u}", [P, BATCH, G, P], BF16) for u in range(RING)]
        alpha = [m.sb(f"alpha{u}", [P, G, BATCH, H]) for u in range(RING)]
        fact = [m.sb(f"fact{u}", [P, BATCH, H]) for u in range(RING)]
        dst_row = [m.sb(f"dst_row{j}", [P, IE], I32) for j in range(BATCH)]
        parts = [m.sb(f"parts{j}", [P, 3, VD], BF16) for j in range(BATCH)]
        ea = [m.sb(f"ea{j}", [KE, IE], BF16) for j in range(BATCH)]
        distance = m.sb("distance", [P, IE])
        onehot = [m.sb(f"onehot{j}", [P, G, P]) for j in range(BATCH)]
        enc = [m.sb(f"enc{v}", [P, FH]) for v in range(2)]
        prod = [m.sb(f"prod{v}", [P, FH]) for v in range(2)]
        red = m.sb("red", [P, T, H])
        score = m.sb("score", [P, T, H])
        dst_here = m.sb("dst_here", [P, T], I32)
        dst_next = m.sb("dst_next", [P, T], I32)
        dst_seq = m.sb("dst_seq", [PR, IE + 1], I32)
        gap = m.sb("gap", [PR, IE])
        seq_max = m.sb("seq_max", [PR, IE])
        differs = m.sb("differs", [P, BATCH, G])
        final_edge = m.sb("final_edge", [P, G])
        last_max = m.sb("last_max", [P, BATCH, G, DG_MAX])
        absent = m.sb("absent", [P, BATCH])
        cand = m.sb("cand", [P, BATCH, H])
        node_max = m.sb("node_max", [P, NB * H])
        old_max = m.sb("old_max", [P, BATCH, H])
        new_max = m.sb("new_max", [P, BATCH, H])
        grown = m.sb("grown", [P, BATCH, H])
        max_rest = m.sb("max_rest", [P, BATCH * H])
        max_parts = m.sb("max_parts", [P, 3, BATCH * H], BF16)
        ident_b = m.sb("ident_b", [P, P], BF16)

        ps_enc = [m.ps(f"ps_enc{v}", [P, 512]) for v in range(2)]
        ps_dst = [m.ps(f"ps_dst{v}", [P, 512]) for v in range(2)]
        ps_seq = m.ps("ps_seq", [P, 512])
        ps_node = m.ps("ps_node", [P, 512])
        ps_back = ps_node[:, 0:G * PR].rearrange("p (g j h) -> p g j h", g=G, j=BATCH)
        ps_last = ps_node[:, 128:128 + BATCH * DG_MAX].rearrange("p (j h) -> p j h", j=BATCH)
        ps_ref = ps_node[:, 256:256 + T * H].rearrange("p (t h) -> p t h", t=T)
        ps_sum = m.ps("ps_sum", [P, 512])
        ps_score = ps_sum[:, 384:384 + T * H].rearrange("p (t h) -> p t h", t=T)
        ps_onehot = m.ps("ps_onehot", [P, G, P], BF16)

        s = m.sem
        ones_ready, idb_ready, cleared = s("ones_ready"), s("idb_ready"), s("cleared")
        rows_free, turns = s("rows_free"), s("turns")
        idx_in = [s(f"idx_in{u}") for u in range(RING)]
        gathered = [s(f"gathered{u}") for u in range(RING)]
        dst_row_in = [s(f"dst_row_in{j}") for j in range(BATCH)]
        parts_in = [s(f"parts_in{j}") for j in range(BATCH)]
        seq_in, here_in = s("seq_in"), s("here_in")
        distance_ready, onehot_t_ready = s("distance_ready"), s("onehot_t_ready")
        enc_ready, relu_ready, dst_ready, prod_ready, red_ready = (
            s("enc_ready"), s("relu_ready"), s("dst_ready"), s("prod_ready"), s("red_ready"))
        score_ready, score1_ready, score2_ready, alpha_ready = (
            s("score_ready"), s("score1_ready"), s("score2_ready"), s("alpha_ready"))
        seq_ready, diff_ready, gap_ready, scan_ready = s("seq_ready"), s("diff_ready"), s("gap_ready"), s("scan_ready")
        back_ready, differs_ready, flag_ready, last_max_ready = (
            s("back_ready"), s("differs_ready"), s("flag_ready"), s("last_max_ready"))
        turned_ready, onehot_ready = s("turned_ready"), s("onehot_ready")
        last_ready, absent_ready, cand_ready = s("last_ready"), s("absent_ready"), s("cand_ready")
        old_ready, new_ready, kept_ready, grown_ready, fact_ready = (
            s("old_ready"), s("new_ready"), s("kept_ready"), s("grown_ready"), s("fact_ready"))
        hi_ready, rest_ready, mid_ready, rest2_ready, split_ready = (
            s("hi_ready"), s("rest_ready"), s("mid_ready"), s("rest2_ready"), s("split_ready"))
        ref_ready, off_ready, arg_ready, exp_ready = s("ref_ready"), s("off_ready"), s("arg_ready"), s("exp_ready")
        weighted, summed, scaled, added = s("weighted"), s("summed"), s("scaled"), s("added")
        block = ctx.enter_context(nc.Block())

        def steps(eng, step, first=0):
            run_steps(eng, step, first, 2 * RING, NBATCH - RING, NBATCH + 2, RING)

        @block.sync
        def _(sp):
            def load_indices(k, j, u):
                e = sp.value_load(item_edge[0:1, bass.ds(BATCH * k + j, 1)], min_val=0, max_val=E)
                sp.dma_start(idx[u][:, G * j:G * (j + 1)],
                             src_pad[bass.ds(e, IE)].rearrange("(p g) -> p g", g=G)).then_inc(idx_in[u], 16)
                return e

            def load_item(k, j, e):
                b = sp.value_load(item_block[0:1, bass.ds(BATCH * k + j, 1)], min_val=0, max_val=NB - 1)
                at_least(sp, distance_ready, BATCH * (k - 1) + j + 1)
                sp.dma_start(dst_row[j][:], dst_ext[bass.ds(e + 1, IE)].rearrange("(a e) -> a e", a=1)
                             .to_broadcast([P, IE])).then_inc(dst_row_in[j], 16)
                at_least(sp, score_ready, BATCH * (k - 1) + j + 1)
                sp.sem_inc(turns, 1)
                sp.dma_start(ea[j][0:27, :], edge_parts[:, bass.ds(e, IE)]).then_inc(parts_in[j], 16)
                sp.dma_start(parts[j][:].rearrange("p s v -> p (s v)"),
                             dst_table[bass.ds(b * P, P), :]).then_inc(parts_in[j], 16)

            def load_order(k, j):
                e = sp.value_load(item_edge[0:1, bass.ds(BATCH * k + j, 1)], min_val=0, max_val=E)
                if j == 0:
                    at_least(sp, diff_ready, k)
                    sp.sem_inc(turns, 1)
                sp.dma_start(dst_seq[H * j:H * (j + 1), :], dst_ext[bass.ds(e, IE + 1)]
                             .rearrange("(a e) -> a e", a=1).to_broadcast([H, IE + 1])).then_inc(seq_in, 16)
                return e

            def load_neighbours(k, j, e):
                sp.dma_start(dst_here[:, G * j:G * (j + 1)],
                             dst_ext[bass.ds(e + 1, IE)].rearrange("(p g) -> p g", g=G)).then_inc(here_in, 16)
                sp.dma_start(dst_next[:, G * j:G * (j + 1)],
                             dst_ext[bass.ds(e + 2, IE)].rearrange("(p g) -> p g", g=G)).then_inc(here_in, 16)

            def step(k, u, q):
                w = (u + 1) % RING
                if there(k + 1, NBATCH):
                    e = [None] * BATCH
                    for j in range(BATCH):
                        if j == 0:
                            at_least(sp, gathered[w], 16 * T * (q + (u + 1) // RING))
                        e[j] = load_indices(k + 1, j, w)
                    for j in range(BATCH):
                        load_item(k + 1, j, e[j])
                if there(k, NBATCH):
                    e = [load_order(k, j) for j in range(BATCH)]
                    at_least(sp, differs_ready, k)
                    sp.sem_inc(turns, 1)
                    for j in range(BATCH):
                        load_neighbours(k, j, e[j])

            sp.wait_ge(ones_ready, BATCH)
            steps(sp, step, -1)

        @block.gpsimd
        def _(pool):
            def step(k, u, q):
                if not there(k, NBATCH):
                    return
                pool.wait_ge(idx_in[u], 16 * BATCH * (q + 1))
                for j in range(BATCH):
                    at_least(pool, summed, BATCH * (k - RING) + j + 1)
                    pool.sem_inc(rows_free, 1)
                    for g in range(G):
                        t = G * j + g
                        nc.gpsimd.indirect_dma_start(
                            out=rows[u][:, t].rearrange("p h d -> p (h d)"), out_offset=None, in_=src_table,
                            in_offset=bass.IndirectOffsetOnAxis(ap=idx[u][:, t:t + 1], axis=0)
                        ).then_inc(gathered[u], 16)

            steps(pool, step)

        @block.tensor
        def _(pe):
            def products(k, u, h):
                j, v = h // 2, h % 2
                if v == 0:
                    pe.wait_ge(parts_in[j], 32 * (k + 1))
                    pe.wait_ge(onehot_t_ready, BATCH * k + j + 1)
                at_least(pe, relu_ready, NHALF * k + h - 1)
                for t in range(2):
                    g = 2 * (h % 2) + t
                    ins = nc.tensor.matmul(ps_enc[v][:, t * HD:(t + 1) * HD], ea[j][:, g:IE:G], wparts[:],
                                           start=True, stop=True)
                ins.then_inc(enc_ready, 1)
                at_least(pe, prod_ready, NHALF * k + h - 1)
                for t in range(2):
                    g = 2 * (h % 2) + t
                    for part in range(3):
                        ins = nc.tensor.matmul(ps_dst[v][:, t * HD:(t + 1) * HD], onehot_t[u][:, j, g, :],
                                               parts[j][:, part, 0:HD], start=(part == 0), stop=(part == 2))
                ins.then_inc(dst_ready, 1)

            def dst_scores(k, u):
                at_least(pe, added, BATCH * (k - 1))
                for j in range(BATCH):
                    for g in range(G):
                        for part in range(3):
                            ins = nc.tensor.matmul(ps_score[:, G * j + g, :], onehot_t[u][:, j, g, :],
                                                   parts[j][:, part, HD:VD], start=(part == 0), stop=(part == 2))
                    ins.then_inc(score_ready, 1)

            def to_rows(k, u):
                pe.wait_ge(alpha_ready, k + 1)
                at_least(pe, scan_ready, k)
                for g in range(G):
                    ins = nc.tensor.transpose(ps_seq[0:PR, g:IE:G], alpha[u][:, g].rearrange("p j h -> p (j h)"),
                                              ident[:])
                ins.then_inc(seq_ready, 1)

            def to_edges(k, u):
                pe.wait_ge(scan_ready, k + 1)
                at_least(pe, off_ready, k)
                turn_onehot(k, u, 1)
                for g in range(G):
                    ins = nc.tensor.transpose(ps_back[:, g].rearrange("p j h -> p (j h)"), seq_max[:, g:IE:G],
                                              ident[0:PR, 0:PR])
                ins.then_inc(back_ready, 1)

            def turn_onehot(k, u, j):
                at_least(pe, onehot_ready, BATCH * k + j)
                for g in range(G):
                    ins = nc.tensor.transpose(ps_onehot[:, g, :], onehot_t[u][:, j, g, :], ident_b[:])
                ins.then_inc(turned_ready, 1)

            def node_maxima(k):
                pe.wait_ge(last_max_ready, k + 1)
                pe.wait_ge(onehot_ready, BATCH * (k + 1))
                for j in range(BATCH):
                    for g in range(G):
                        ins = nc.tensor.matmul(ps_last[:, j, :], onehot[j][:, g, :], last_max[:, j, g, :],
                                               start=(g == 0), stop=(g == G - 1))
                ins.then_inc(last_ready, 1)

            def references(k, u):
                pe.wait_ge(split_ready, k + 1)
                for j in range(BATCH):
                    for g in range(G):
                        for part in range(3):
                            ins = nc.tensor.matmul(ps_ref[:, G * j + g, :], onehot_t[u][:, j, g, :],
                                                   max_parts[:, part, H * j:H * (j + 1)],
                                                   start=(part == 0), stop=(part == 2))
                ins.then_inc(ref_ready, 1)

            def sums(k, u, j):
                pe.wait_ge(weighted, BATCH * k + j + 1)
                at_least(pe, added, BATCH * k + j)
                if j == 0 and there(k + 1, NBATCH):
                    pe.wait_ge(score1_ready, k + 2)
                for g in range(G):
                    ins = nc.tensor.matmul(ps_sum[:, 0:ROW], onehot[j][:, g, :],
                                           rows[u][:, G * j + g].rearrange("p h d -> p (h d)"),
                                           start=(g == 0), stop=(g == G - 1))
                ins.then_inc(summed, 1)

            def step(k, u, q):
                now, before, older = there(k, NBATCH), there(k - 1, NBATCH), there(k - 2, NBATCH)
                u1, u2 = (u - 1) % RING, (u - 2) % RING
                if now:
                    products(k, u, 0)
                if older:
                    sums(k - 2, u2, 0)
                if before:
                    to_rows(k - 1, u1)
                    turn_onehot(k - 1, u1, 0)
                if now:
                    products(k, u, 1)
                if older:
                    sums(k - 2, u2, 1)
                if before:
                    to_edges(k - 1, u1)
                if now:
                    products(k, u, 2)
                if older:
                    sums(k - 2, u2, 2)
                if before:
                    turn_onehot(k - 1, u1, 2)
                if now:
                    products(k, u, 3)
                if before:
                    node_maxima(k - 1)
                if now:
                    products(k, u, 4)
                    products(k, u, 5)
                if before:
                    references(k - 1, u1)
                if now:
                    dst_scores(k, u)

            pe.wait_ge(idb_ready, 1)
            steps(pe, step)

        @block.vector
        def _(dve):
            v = nc.vector

            def product(k, h):
                w = h % 2
                n = NHALF * k + h
                dve.wait_ge(relu_ready, n + 1)
                dve.wait_ge(dst_ready, n + 1)
                v.tensor_tensor(prod[w][:], ps_dst[w][:], enc[w][:], ALU.mult).then_inc(prod_ready, 1)
                if h == 0:
                    at_least(dve, alpha_ready, k)
                dve.wait_ge(prod_ready, n + 1)
                v.tensor_reduce(red[:, 2 * h:2 * h + 2, :],
                                prod[w][:].rearrange("p (t h d) -> p t h d", t=2, d=D),
                                AX.X, ALU.add).then_inc(red_ready, 1)

            def scores(k, u, q):
                dve.wait_ge(score_ready, BATCH * (k + 1))
                dve.wait_ge(red_ready, NHALF * (k + 1))
                v.tensor_tensor(score[:], ps_score[:], red[:], ALU.add).then_inc(score1_ready, 1)
                dve.wait_ge(gathered[u], 16 * T * (q + 1))
                dve.wait_ge(score1_ready, k + 1)
                v.tensor_tensor(red[:], score[:], rows[u][:, :, :, D], ALU.add).then_inc(score2_ready, 1)
                dve.wait_ge(score2_ready, k + 1)
                for j in range(BATCH):
                    r = red[:, G * j:G * (j + 1), :]
                    ins = v.scalar_tensor_tensor(out=alpha[u][:, :, j, :], in0=r, scalar=0.2, in1=r,
                                                 op0=ALU.mult, op1=ALU.max)
                ins.then_inc(alpha_ready, 1)

            def gaps(k):
                dve.wait_ge(seq_in, 16 * BATCH * (k + 1))
                at_least(dve, scan_ready, k)
                v.tensor_tensor(gap[:], dst_seq[:, 0:IE], dst_seq[:, 1:IE + 1], ALU.subtract).then_inc(diff_ready, 1)

            def scan(k):
                dve.wait_ge(seq_ready, k + 1)
                dve.wait_ge(gap_ready, k + 1)
                at_least(dve, back_ready, k)
                v.tensor_tensor_scan(seq_max[:], gap[:], ps_seq[0:PR, :], -BIG, ALU.add, ALU.max).then_inc(scan_ready, 1)

            def flags(k):
                dve.wait_ge(here_in, 32 * BATCH * (k + 1))
                v.tensor_tensor(differs[:].rearrange("p j g -> p (j g)"), dst_here[:], dst_next[:],
                                ALU.not_equal).then_inc(differs_ready, 1)
                dve.wait_ge(differs_ready, k + 1)
                at_least(dve, last_ready, k)
                v.tensor_tensor(last_max[:, :, :, H], differs[:],
                                final_edge[:].rearrange("p (a g) -> p a g", a=1).to_broadcast([P, BATCH, G]),
                                ALU.max).then_inc(flag_ready, 1)

            def last_maxima(k):
                dve.wait_ge(back_ready, k + 1)
                dve.wait_ge(flag_ready, k + 1)
                for j in range(BATCH):
                    ins = v.tensor_tensor(last_max[:, j, :, 0:H], ps_back[:, :, j, :],
                                          last_max[:, j, :, H:H + 1].to_broadcast([P, G, H]), ALU.mult)
                ins.then_inc(last_max_ready, 1)

            def running_maxima(k, u):
                dve.wait_ge(last_ready, k + 1)
                v.tensor_scalar(absent[:], ps_last[:, :, H], BIG, -BIG, ALU.mult, ALU.add).then_inc(absent_ready, 1)
                dve.wait_ge(absent_ready, k + 1)
                v.tensor_tensor(cand[:], ps_last[:, :, 0:H],
                                absent[:].rearrange("p (j a) -> p j a", a=1).to_broadcast([P, BATCH, H]),
                                ALU.add).then_inc(cand_ready, 1)
                dve.wait_ge(cand_ready, k + 1)
                for j in range(BATCH):
                    b = dve.value_load(item_block[0:1, bass.ds(BATCH * k + j, 1)], min_val=0, max_val=NB - 1)
                    here = node_max[:, bass.ds(b * H, H)]
                    n = BATCH * k + j
                    at_least(dve, kept_ready, n)
                    v.tensor_scalar(old_max[:, j, :], here, -BIG, None, ALU.max).then_inc(old_ready, 1)
                    v.tensor_tensor(new_max[:, j, :], here, cand[:, j, :], ALU.max).then_inc(new_ready, 1)
                    dve.wait_ge(old_ready, n + 1)
                    dve.wait_ge(new_ready, n + 1)
                    v.tensor_tensor(here, new_max[:, j, :], old_max[:, j, :], ALU.max).then_inc(kept_ready, 1)
                v.tensor_tensor(grown[:], old_max[:], new_max[:], ALU.subtract).then_inc(grown_ready, 1)
                flat = new_max[:].rearrange("p j h -> p (j h)")
                at_least(dve, ref_ready, k)
                v.tensor_copy(max_parts[:, 0, :], flat).then_inc(hi_ready, 1)
                dve.wait_ge(hi_ready, k + 1)
                v.tensor_tensor(max_rest[:], flat, max_parts[:, 0, :], ALU.subtract).then_inc(rest_ready, 1)
                dve.wait_ge(rest_ready, k + 1)
                v.tensor_copy(max_parts[:, 1, :], max_rest[:]).then_inc(mid_ready, 1)
                dve.wait_ge(mid_ready, k + 1)
                v.tensor_tensor(max_parts[:, 2, :], max_rest[:], max_parts[:, 1, :],
                                ALU.subtract).then_inc(split_ready, 1)

            def exponents(k, u):
                dve.wait_ge(ref_ready, k + 1)
                a = alpha[u][:]
                v.tensor_tensor(a, a, ps_ref[:].rearrange("p (j g) h -> p g j h", g=G),
                                ALU.subtract).then_inc(off_ready, 1)
                dve.wait_ge(off_ready, k + 1)
                v.tensor_scalar(a, a, 0.0, None, ALU.min).then_inc(arg_ready, 1)

            def weigh(k, u, j):
                dve.wait_ge(exp_ready, k + 1)
                r = rows[u][:, G * j:G * (j + 1)].rearrange("p g h d -> p (g h) d")
                v.tensor_tensor(r[:, :, 0:D], r[:, :, 0:D], r[:, :, D:DG].to_broadcast([P, G * H, D]),
                                ALU.mult).then_inc(weighted, 1)

            def accumulate(k, u, j):
                n = BATCH * k + j
                b = dve.value_load(item_block[0:1, bass.ds(n, 1)], min_val=0, max_val=NB - 1)
                here = acc[:, bass.ds(b * ROW, ROW)]
                by_head = here.rearrange("p (h d) -> p h d", d=DG)
                if j == 0:
                    dve.wait_ge(fact_ready, k + 1)
                at_least(dve, added, n)
                v.tensor_tensor(by_head, by_head, fact[u][:, j, :].rearrange("p (h a) -> p h a", a=1)
                                .to_broadcast([P, H, DG]), ALU.mult).then_inc(scaled, 1)
                dve.wait_ge(scaled, n + 1)
                dve.wait_ge(summed, n + 1)
                v.tensor_tensor(here, here, ps_sum[:, 0:ROW], ALU.add).then_inc(added, 1)

            def step(k, u, q):
                now, before, older = there(k, NBATCH), there(k - 1, NBATCH), there(k - 2, NBATCH)
                u1, u2 = (u - 1) % RING, (u - 2) % RING
                if now:
                    product(k, 0)
                if before:
                    gaps(k - 1)
                if older:
                    accumulate(k - 2, u2, 0)
                if before:
                    scan(k - 1)
                if now:
                    product(k, 1)
                if older:
                    accumulate(k - 2, u2, 1)
                if before:
                    flags(k - 1)
                    last_maxima(k - 1)
                if now:
                    product(k, 2)
                if older:
                    accumulate(k - 2, u2, 2)
                if now:
                    product(k, 3)
                if before:
                    running_maxima(k - 1, u1)
                if now:
                    product(k, 4)
                    product(k, 5)
                if before:
                    exponents(k - 1, u1)
                if now:
                    scores(k, u, q)
                if before:
                    for j in range(BATCH):
                        weigh(k - 1, u1, j)

            for j in range(BATCH):
                v.memset(ea[j][:], 1.0).then_inc(ones_ready, 1)
            v.tensor_copy(ident_b[:], ident[:]).then_inc(idb_ready, 1)
            v.memset(node_max[:], -BIG).then_inc(cleared, 1)
            v.memset(final_edge[:], 0.0).then_inc(cleared, 1)
            v.memset(acc[:], 0.0).then_inc(cleared, 1)
            dve.wait_ge(cleared, 3)
            v.tensor_copy(final_edge[:, G - 1:G], ident[:, P - 1:P]).then_inc(cleared, 1)
            dve.wait_ge(cleared, 4)
            steps(dve, step)

        @block.scalar
        def _(act):
            def place(k, u, j):
                n = BATCH * k + j
                act.wait_ge(dst_row_in[j], 16 * (k + 1))
                at_least(act, onehot_t_ready, n)
                nc.scalar.activation(distance[:], dst_row[j][:], ACT.Abs,
                                     bias=neg_node[:, bass.ds(n, 1)]).then_inc(distance_ready, 1)
                act.wait_ge(distance_ready, n + 1)
                if j == 0:
                    at_least(act, ref_ready, k - RING + 1)
                nc.scalar.activation(onehot_t[u][:, j], distance[:].rearrange("p (e g) -> p g e", g=G), ACT.Relu,
                                     bias=1.0, scale=-1.0).then_inc(onehot_t_ready, 1)

            def relu(k, h):
                w, n = h % 2, NHALF * k + h
                act.wait_ge(enc_ready, n + 1)
                at_least(act, prod_ready, n - 1)
                nc.scalar.activation(enc[w][:], ps_enc[w][:], ACT.Relu).then_inc(relu_ready, 1)

            def onehot_out(k, j):
                n = BATCH * k + j
                act.wait_ge(turned_ready, n + 1)
                at_least(act, summed, n - BATCH + 1)
                nc.scalar.copy(onehot[j][:], ps_onehot[:]).then_inc(onehot_ready, 1)

            def step(k, u, q):
                now, before = there(k, NBATCH), there(k - 1, NBATCH)
                u1 = (u - 1) % RING
                if now:
                    relu(k, 0)
                if before:
                    act.wait_ge(diff_ready, k)
                    nc.scalar.mul(gap[:], gap[:], BIG).then_inc(gap_ready, 1)
                    onehot_out(k - 1, 0)
                if now:
                    place(k, u, 1)
                    relu(k, 1)
                if before:
                    onehot_out(k - 1, 1)
                if now:
                    relu(k, 2)
                if before:
                    onehot_out(k - 1, 2)
                if now:
                    place(k, u, 2)
                    relu(k, 3)
                    relu(k, 4)
                if there(k + 1, NBATCH):
                    place(k + 1, (u + 1) % RING, 0)
                if before:
                    act.wait_ge(grown_ready, k)
                    at_least(act, added, BATCH * (k - 1 - RING + 1))
                    nc.scalar.activation(fact[u1][:], grown[:], ACT.Exp).then_inc(fact_ready, 1)
                if now:
                    relu(k, 5)
                if before:
                    act.wait_ge(arg_ready, k)
                    nc.scalar.activation(rows[u1][:, :, :, D].rearrange("p (j g) h -> p g j h", g=G),
                                         alpha[u1][:], ACT.Exp).then_inc(exp_ready, 1)

            place(0, 0, 0)
            steps(act, step)


def combine_phase(nc, ident, acc, keep, x_pad, bias, gate_w, gate_b, token_rows):
    logits, = keep
    with ExitStack() as ctx:
        m = Space(nc, ctx, "c_")
        bias_rep = m.sb("bias_rep", [P, HD])
        gw = m.sb("gw", [P, KC, X])
        gb = m.sb("gb", [P, X])
        x = [m.sb(f"x{u}", [P, HD]) for u in range(2)]
        den = [m.sb(f"den{u}", [P, H]) for u in range(2)]
        gnn = [m.sb(f"gnn{u}", [P, HD]) for u in range(2)]
        stats = [m.sb(f"stats{u}", [P, 6]) for u in range(2)]
        mv = [m.sb(f"mv{u}", [P, 2]) for u in range(2)]
        veps = [m.sb(f"veps{u}", [P, 1]) for u in range(2)]
        std = [m.sb(f"std{u}", [P, 1]) for u in range(2)]
        rstd = [m.sb(f"rstd{u}", [P, 1]) for u in range(2)]
        row = [m.sb(f"row{u}", [P, 2, HD]) for u in range(4)]
        xnt = [m.sb(f"xnt{u}", [P, KC, P]) for u in range(2)]
        tp = [m.ps(f"tp{u}", [P, 512]) for u in range(2)]
        gp = [m.ps(f"gp{u}", [P, 512]) for u in range(2)]

        const_in = m.sem("const_in")
        turns = m.sem("turns")
        x_in = [m.sem(f"x_in{u}") for u in range(2)]
        row_out = [m.sem(f"row_out{u}") for u in range(4)]
        den_ready, rden_ready, gnn_ready, biased, x1_ready = (
            m.sem("den_ready"), m.sem("rden_ready"), m.sem("gnn_ready"), m.sem("biased"), m.sem("x1_ready"))
        stats_ready, mv_ready, var_ready, std_ready, rstd_ready, row_ready = (
            m.sem("stats_ready"), m.sem("mv_ready"), m.sem("var_ready"), m.sem("std_ready"),
            m.sem("rstd_ready"), m.sem("row_ready"))
        tp_ready, xnt_ready, gp_ready, logits_ready = (
            m.sem("tp_ready"), m.sem("xnt_ready"), m.sem("gp_ready"), m.sem("logits_ready"))
        block = ctx.enter_context(nc.Block())

        def steps(eng, step):
            run_steps(eng, step, -1, 8, (NB - 4) // 4 * 4, NB + 1, 4)

        @block.sync
        def _(sp):
            sp.dma_start(bias_rep[:], bias.to_broadcast([P, HD])).then_inc(const_in, 16)
            sp.dma_start(gb[:], gate_b.to_broadcast([P, X])).then_inc(const_in, 16)
            for k in range(KC):
                sp.dma_start(gw[:, k, :], gate_w[k * P:(k + 1) * P, :]).then_inc(const_in, 16)
            sp.dma_start(x[0][:], x_pad[0:P, :]).then_inc(x_in[0], 16)
            sp.dma_start(x[1][:], x_pad[P:2 * P, :]).then_inc(x_in[1], 16)

            def step(s, u, q):
                w = (u + 1) % 2
                if not isinstance(s, int) or s + 3 < NB:
                    sp.wait_ge(x1_ready, s + 2)
                    sp.dma_start(x[w][:], x_pad[bass.ds((s + 3) * P, P), :]).then_inc(x_in[w], 16)
                if there(s, NB):
                    sp.wait_ge(row_ready, s + 1)
                    sp.dma_start(token_rows[bass.ds(s * P, P), :],
                                 row[u][:].rearrange("p a d -> p (a d)")).then_inc(row_out[u], 16)

            steps(sp, step)
            for u in range(4):
                sp.wait_ge(row_out[u], 16 * len(range(u, NB, 4)))

        @block.tensor
        def _(pe):
            pe.wait_ge(const_in, 16 * (2 + KC))

            def step(s, u, q):
                v = u % 2
                if there(s, NB):
                    pe.wait_ge(row_ready, s + 1)
                    at_least(pe, xnt_ready, s - 1)
                    for k in range(KC):
                        ins = nc.tensor.transpose(tp[v][:, k * P:(k + 1) * P], row[u][:, 0, k * P:(k + 1) * P],
                                                  ident[:])
                    ins.then_inc(tp_ready, 1)
                    pe.wait_ge(xnt_ready, s + 1)
                    at_least(pe, logits_ready, s - 1)
                    for k in range(KC):
                        ins = nc.tensor.matmul(gp[v][:, 0:X], xnt[v][:, k, :], gw[:, k, :],
                                               start=(k == 0), stop=(k == KC - 1))
                    ins.then_inc(gp_ready, 1)

            steps(pe, step)

        @block.vector
        def _(dve):
            v = nc.vector
            dve.wait_ge(const_in, 16 * (2 + KC))

            def step(s, u, q):
                w, w4 = (u + 1) % 2, (u + 1) % 4
                o = u % 2
                if there(s + 1, NB):
                    sums = acc[:, bass.ds((s + 1) * ROW, ROW)].rearrange("p (h d) -> p h d", d=DG)
                    at_least(dve, gnn_ready, s)
                    v.tensor_scalar(den[w][:], sums[:, :, D], 1e-10, None, ALU.max).then_inc(den_ready, 1)
                    dve.wait_ge(den_ready, s + 2)
                    v.reciprocal(den[w][:], den[w][:]).then_inc(rden_ready, 1)
                if there(s, NB):
                    dve.wait_ge(std_ready, s + 1)
                    v.reciprocal(rstd[o][:], std[o][:]).then_inc(rstd_ready, 1)
                if there(s + 1, NB):
                    dve.wait_ge(rden_ready, s + 2)
                    v.tensor_tensor(gnn[w][:].rearrange("p (h d) -> p h d", d=D), sums[:, :, 0:D],
                                    den[w][:].rearrange("p (h a) -> p h a", a=1).to_broadcast([P, H, D]),
                                    ALU.mult).then_inc(gnn_ready, 1)
                if there(s, NB):
                    dve.wait_ge(rstd_ready, s + 1)
                    v.tensor_scalar(row[u][:, 0, :], row[u][:, 1, :], mv[o][:, 0:1], rstd[o][:], ALU.subtract,
                                    ALU.mult).then_inc(row_ready, 1)
                if there(s + 1, NB):
                    dve.wait_ge(gnn_ready, s + 2)
                    v.tensor_tensor(gnn[w][:], gnn[w][:], bias_rep[:], ALU.add).then_inc(biased, 1)
                    dve.wait_ge(x_in[w], 16 * (2 * q + (u + 1) // 2 + 1))
                    at_least(dve, row_out[w4], 16 * (q + (u + 1) // 4))
                    at_least(dve, tp_ready, s - 2)
                    dve.wait_ge(biased, s + 2)
                    v.tensor_tensor(row[w4][:, 1, :], gnn[w][:], x[w][:], ALU.add).then_inc(x1_ready, 1)
                if there(s - 1, NB):
                    dve.wait_ge(gp_ready, s)
                    v.tensor_tensor(logits[:, bass.ds((s - 1) * X, X)], gp[w][:, 0:X], gb[:],
                                    ALU.add).then_inc(logits_ready, 1)
                if there(s + 1, NB):
                    dve.wait_ge(x1_ready, s + 2)
                    v.bn_stats(stats[w][:], row[w4][:, 1, :]).then_inc(stats_ready, 1)
                    dve.wait_ge(stats_ready, s + 2)
                    at_least(dve, row_ready, s)
                    dve.sem_inc(turns, 1)
                    v.bn_aggr(mv[w][:], stats[w][:]).then_inc(mv_ready, 1)
                    dve.wait_ge(mv_ready, s + 2)
                    v.tensor_scalar_add(veps[w][:], mv[w][:, 1:2], EPS).then_inc(var_ready, 1)

            steps(dve, step)

        @block.scalar
        def _(act):
            def step(s, u, q):
                w, o = (u + 1) % 2, u % 2
                if there(s + 1, NB):
                    act.wait_ge(var_ready, s + 2)
                    at_least(act, rstd_ready, s)
                    nc.scalar.activation(std[w][:], veps[w][:], ACT.Sqrt).then_inc(std_ready, 1)
                if there(s, NB):
                    act.wait_ge(tp_ready, s + 1)
                    at_least(act, gp_ready, s - 1)
                    nc.scalar.copy(xnt[o][:], tp[o][:, 0:HD].rearrange("p (k t) -> p k t", k=KC)).then_inc(
                        xnt_ready, 1)

            steps(act, step)


def route_phase(nc, keep, tables, slots, weights, weights_dram, token_rows):
    logits, = keep
    tile_expert, = tables
    w1s, w2s, b1r, b2r = weights
    w1, w2, b1, b2 = weights_dram
    NX = NB * X
    with ExitStack() as ctx:
        m = Space(nc, ctx, "r_")
        top = m.sb("top", [P, NB])
        shift = m.sb("shift", [P, NB, X])
        expo = m.sb("expo", [P, NB, X])
        total = m.sb("total", [P, NB])
        prob = m.sb("prob", [P, NB])
        ptop = m.sb("ptop", [P, NB])
        rank = shift
        rank_i = m.sb("rank_i", [P, X], I32)
        rank_f = m.sb("rank_f", [P, X])
        best = m.sb("best", [P, NB])
        hot = m.sb("hot", [P, NB, X])
        hot_b = m.sb("hot_b", [P, NB, X], BF16)
        node_i = m.sb("node_i", [P, NB], I32)
        node = m.sb("node", [P, NB])
        real = m.sb("real", [P, NB])
        ones_b = m.sb("ones_b", [P, P], BF16)
        before_b = m.sb("before_b", [P, P], BF16)
        part_i = m.sb("part_i", [P, 1], I32)
        part = m.sb("part", [P, 1])
        zeros = m.sb("zeros", [P, NB])
        tile_total = m.sb("tile_total", [P, X, NB])
        running = m.sb("running", [P, X, NB])
        pos = expo
        mine = shift
        position = m.sb("position", [P, NB])
        kept = m.sb("kept", [P, NB])
        tiles_f = m.sb("tiles_f", [P, X])
        tiles_i = m.sb("tiles_i", [P, X], I32)
        tiles = m.sb("tiles", [P, X])
        tile_end = m.sb("tile_end", [P, X])
        slot_base = m.sb("slot_base", [P, X])
        base = m.sb("base", [P, NB])
        slot_f = m.sb("slot_f", [P, NB])
        unreal = m.sb("unreal", [P, NB])
        dump = m.sb("dump", [P, 1])
        slot_i = m.sb("slot_i", [P, NB], I32)
        entry = m.sb("entry", [P, NB, 2])
        num_i = m.sb("num_i", [1, NT], I32)
        num = m.sb("num", [1, NT])
        expert = m.sb("expert", [1, NT])
        past = m.sb("past", [1, NT])
        empty = m.sb("empty", [P, NT + 1, 2])
        blank = m.sb("blank", [P, 2 * HD])
        ps_in = [m.ps(f"ps_in{i}", [P, 512]) for i in range(2)]
        ps_all = [m.ps(f"ps_all{i}", [P, 512]) for i in range(2)]

        const_ready = m.sem("const_ready")
        cleared = m.sem("cleared")
        step = m.sem("step")
        hot_ready = m.sem("hot_ready")
        counted = m.sem("counted")
        shift_ready = m.sem("shift_ready")
        exp_ready = m.sem("exp_ready")
        empty_ready = m.sem("empty_ready")
        empty_out = m.sem("empty_out")
        weights_in = m.sem("weights_in")
        entry_ready = m.sem("entry_ready")
        slots_out = m.sem("slots_out")
        block = ctx.enter_context(nc.Block())
        HALF = NX // 2
        FC = F // P

        @block.sync
        def _(sp):
            sp.wait_ge(empty_ready, 2)
            sp.dma_start(slots.rearrange("(t p) c -> p t c", p=P), empty[:]).then_inc(empty_out, 16)
            sp.dma_start(token_rows[NPAD:NPAD + P, :], blank[:]).then_inc(empty_out, 16)
            for x in range(X):
                sp.dma_start(w1s[:, x * KC * F:(x + 1) * KC * F].rearrange("p (k f) -> p k f", k=KC),
                             w1[x].rearrange("(k p) f -> p k f", p=P)).then_inc(weights_in, 16)
                sp.dma_start(w2s[:, x * FC * HD:(x + 1) * FC * HD].rearrange("p (c d) -> p c d", c=FC),
                             w2[x].rearrange("(c p) d -> p c d", p=P)).then_inc(weights_in, 16)
            sp.dma_start(b1r[:], b1.to_broadcast([P, X * F])).then_inc(weights_in, 16)
            sp.dma_start(b2r[:], b2.to_broadcast([P, X * HD])).then_inc(weights_in, 16)
            sp.wait_ge(empty_out, 32)
            sp.wait_ge(weights_in, 16 * (2 * X + 2))

        @block.gpsimd
        def _(pool):
            g = nc.gpsimd
            g.iota(node_i[:], pattern=[[P, NB]], base=0, channel_multiplier=1).then_inc(const_ready, 1)
            g.iota(rank_i[:], pattern=[[-1, X]], base=X, channel_multiplier=0).then_inc(const_ready, 1)
            g.iota(part_i[:], pattern=[[0, 1]], base=0, channel_multiplier=1).then_inc(const_ready, 1)
            g.iota(num_i[:], pattern=[[1, NT]], base=0, channel_multiplier=0).then_inc(const_ready, 1)
            g.memset(ones_b[:], 1.0).then_inc(cleared, 1)
            g.memset(zeros[:], 0.0).then_inc(const_ready, 1)
            pool.wait_ge(cleared, 1)
            g.affine_select(out=before_b[:], in_=ones_b[:], compare_op=ALU.is_gt, fill=0.0, base=0,
                            pattern=[[1, P]], channel_multiplier=-1).then_inc(const_ready, 1)
            pool.wait_ge(entry_ready, 1)
            pool.wait_ge(empty_out, 32)
            for b in range(NB):
                g.indirect_dma_start(out=slots, out_offset=bass.IndirectOffsetOnAxis(ap=slot_i[:, b:b + 1], axis=0),
                                     in_=entry[:, b, :], in_offset=None).then_inc(slots_out, 16)
            pool.wait_ge(slots_out, 16 * NB)

        @block.tensor
        def _(pe):
            pe.wait_ge(const_ready, 6)
            pe.wait_ge(hot_ready, 1)
            flat = hot_b[:].rearrange("p b x -> p (b x)")
            for i in range(2):
                nc.tensor.matmul(ps_in[i][:, 0:HALF], before_b[:], flat[:, HALF * i:HALF * (i + 1)],
                                 start=True, stop=True)
                ins = nc.tensor.matmul(ps_all[i][:, 0:HALF], ones_b[:], flat[:, HALF * i:HALF * (i + 1)],
                                       start=True, stop=True)
            ins.then_inc(counted, 1)

        @block.scalar
        def _(act):
            act.wait_ge(shift_ready, 1)
            nc.scalar.activation(expo[:], shift[:], ACT.Exp).then_inc(exp_ready, 1)

        @block.vector
        def _(dve):
            v = nc.vector
            done = [0]

            def link(ins):
                done[0] += 1
                ins.then_inc(step, 1)
                dve.wait_ge(step, done[0])

            def over_x(ap):
                return ap[:].rearrange("p (b a) -> p b a", a=1).to_broadcast([P, NB, X])

            def over_b(ap):
                return ap[:].rearrange("p (a x) -> p a x", a=1).to_broadcast([P, NB, X])

            dve.wait_ge(const_ready, 6)
            v.tensor_copy(node[:], node_i[:])
            v.tensor_copy(rank_f[:], rank_i[:])
            link(v.tensor_copy(part[:], part_i[:]))
            link(v.tensor_scalar(dump[:], part[:], float(DUMP), None, ALU.add))
            link(v.memset(empty[:], 0.0))
            v.memset(blank[:], 0.0).then_inc(empty_ready, 1)
            v.tensor_scalar(empty[:, :, 0], empty[:, :, 0], dump[:], None, ALU.add).then_inc(empty_ready, 1)
            lg = logits[:].rearrange("p (b x) -> p b x", x=X)
            link(v.tensor_reduce(top[:], lg, AX.X, ALU.max))
            v.tensor_tensor(shift[:], lg, over_x(top), ALU.subtract).then_inc(shift_ready, 1)
            dve.wait_ge(exp_ready, 1)
            link(v.tensor_reduce(total[:], expo[:], AX.X, ALU.add))
            link(v.reciprocal(total[:], total[:]))
            link(v.tensor_tensor(expo[:], expo[:], over_x(total), ALU.mult))
            link(v.tensor_reduce(ptop[:], expo[:], AX.X, ALU.max))
            link(v.tensor_tensor(hot[:], expo[:], over_x(ptop), ALU.is_equal))
            link(v.tensor_tensor(rank[:], hot[:], over_b(rank_f), ALU.mult))
            link(v.tensor_reduce(best[:], rank[:], AX.X, ALU.max))
            link(v.tensor_scalar(real[:], node[:], float(N), None, ALU.is_lt))
            link(v.tensor_tensor(hot[:], over_b(rank_f), over_x(best), ALU.is_equal))
            link(v.tensor_tensor(hot[:], hot[:], over_x(real), ALU.mult))
            v.tensor_copy(hot_b[:], hot[:]).then_inc(hot_ready, 1)
            dve.wait_ge(counted, 1)
            for i in range(2):
                half = slice(NB // 2 * i, NB // 2 * (i + 1))
                link(v.tensor_copy(tile_total[:, :, half].rearrange("p x b -> p b x"),
                                   ps_all[i][:, 0:HALF].rearrange("p (b x) -> p b x", x=X)))
            for x in range(X):
                link(v.tensor_tensor_scan(running[:, x, :], tile_total[:, x, :], zeros[:], 0.0, ALU.add, ALU.add))
            link(v.tensor_scalar(tiles_i[:], running[:, :, NB - 1], float(P - 1), None, ALU.add))
            link(v.tensor_scalar(tiles_i[:], tiles_i[:], P.bit_length() - 1, None, ALU.logical_shift_right))
            link(v.tensor_copy(tiles[:], tiles_i[:]))
            link(v.tensor_tensor_scan(tile_end[:], tiles[:], zeros[:, 0:X], 0.0, ALU.add, ALU.add))
            link(v.tensor_tensor(slot_base[:], tile_end[:], tiles[:], ALU.subtract))
            link(v.tensor_scalar(slot_base[:], slot_base[:], float(P), None, ALU.mult))
            link(v.tensor_tensor(running[:], running[:], tile_total[:], ALU.subtract))
            for i in range(2):
                half = slice(NB // 2 * i, NB // 2 * (i + 1))
                link(v.tensor_tensor(pos[:, half, :], ps_in[i][:, 0:HALF].rearrange("p (b x) -> p b x", x=X),
                                     running[:, :, half].rearrange("p x b -> p b x"), ALU.add))
            link(v.tensor_tensor(mine[:], pos[:], hot[:], ALU.mult))
            link(v.tensor_reduce(position[:], mine[:], AX.X, ALU.add))
            link(v.tensor_scalar(kept[:], position[:], float(CAP), None, ALU.is_lt))
            link(v.tensor_tensor(entry[:, :, 1], ptop[:], kept[:], ALU.mult))
            link(v.tensor_copy(entry[:, :, 0], node[:]))
            link(v.tensor_tensor(mine[:], hot[:], over_b(slot_base), ALU.mult))
            link(v.tensor_reduce(base[:], mine[:], AX.X, ALU.add))
            link(v.tensor_tensor(slot_f[:], position[:], base[:], ALU.add))
            link(v.tensor_scalar(unreal[:], real[:], -1.0, 1.0, ALU.mult, ALU.add))
            link(v.tensor_scalar(dump[:], part[:], float(NT * P), None, ALU.add))
            link(v.tensor_scalar(unreal[:], unreal[:], dump[:], None, ALU.mult))
            link(v.tensor_tensor(slot_f[:], slot_f[:], unreal[:], ALU.add))
            v.tensor_copy(slot_i[:], slot_f[:]).then_inc(entry_ready, 1)
            link(v.tensor_copy(num[:], num_i[:]))
            link(v.tensor_scalar(expert[:], num[:], tile_end[0:1, 0:1], None, ALU.is_ge))
            for x in range(1, X - 1):
                link(v.tensor_scalar(past[:], num[:], tile_end[0:1, x:x + 1], None, ALU.is_ge))
                link(v.tensor_tensor(expert[:], expert[:], past[:], ALU.add))
            link(v.tensor_copy(tile_expert[:], expert[:]))


def expert_phase(nc, ident, tables, weights, slots, token_rows, out):
    tile_expert, = tables
    w1s, w2s, b1r, b2r = weights
    FC = F // P
    UN = 3
    HB = 512
    with ExitStack() as ctx:
        m = Space(nc, ctx, "f_")
        entry = [m.sb(f"entry{u}", [P, 2]) for u in range(UN)]
        token = [m.sb(f"token{u}", [P, 1], I32) for u in range(UN)]
        row = [m.sb(f"row{u}", [P, 2, HD]) for u in range(UN)]
        xnt = [m.sb(f"xnt{u}", [P, KC, P]) for u in range(UN)]
        pre = m.sb("pre", [P, F])
        hid = m.sb("hid", [P, FC, P])
        y = m.sb("y", [P, HD])
        scaled = m.sb("scaled", [P, HD])
        is_number = m.sb("is_number", [P, HD], I32)
        is_plus = m.sb("is_plus", [P, HD], I32)
        is_minus = m.sb("is_minus", [P, HD], I32)
        plus = m.sb("plus", [P, HD])
        minus = m.sb("minus", [P, HD])
        clean = m.sb("clean", [P, HD])
        res = [m.sb(f"res{u}", [P, HD]) for u in range(UN)]
        ps_x = m.ps("ps_x", [P, 512])
        ps_h = [m.ps(f"ps_h{i}", [P, 512]) for i in range(2)]
        ps_t = [m.ps(f"ps_t{i}", [P, 512]) for i in range(2)]
        ps_y = [m.ps(f"ps_y{i}", [P, 512]) for i in range(2)]

        entry_in = [m.sem(f"entry_in{u}") for u in range(UN)]
        row_in = [m.sem(f"row_in{u}") for u in range(UN)]
        res_out = [m.sem(f"res_out{u}") for u in range(UN)]
        const_ready, turns, turns_v = m.sem("const_ready"), m.sem("turns"), m.sem("turns_v")
        token_ready, px_ready, xnt_ready = m.sem("token_ready"), m.sem("px_ready"), m.sem("xnt_ready")
        h_ready, pre_ready, t_ready, hid_ready = (
            m.sem("h_ready"), m.sem("pre_ready"), m.sem("t_ready"), m.sem("hid_ready"))
        y_ready, y_read, y_scaled, masks_ready, clean_step, res_ready = (
            m.sem("y_ready"), m.sem("y_read"), m.sem("y_scaled"), m.sem("masks_ready"), m.sem("clean_step"),
            m.sem("res_ready"))
        block = ctx.enter_context(nc.Block())

        def steps(eng, step):
            run_steps(eng, step, -3, 2 * UN, NT - UN, NT, UN)

        @block.sync
        def _(sp):
            def step(t, u, q):
                if there(t + 3, NT):
                    at_least(sp, res_ready, t + 1)
                    sp.dma_start(entry[u][:], slots[bass.ds((t + 3) * P, P), :]).then_inc(entry_in[u], 16)

            steps(sp, step)

        @block.gpsimd
        def _(pool):
            def step(t, u, q):
                w = (u + 2) % UN
                if there(t + 2, NT):
                    pool.wait_ge(token_ready, t + 3)
                    at_least(pool, res_ready, t)
                    pool.sem_inc(turns, 1)
                    nc.gpsimd.indirect_dma_start(
                        out=row[w][:].rearrange("p a d -> p (a d)"), out_offset=None, in_=token_rows,
                        in_offset=bass.IndirectOffsetOnAxis(ap=token[w][:, 0:1], axis=0)).then_inc(row_in[w], 16)
                if there(t, NT):
                    pool.wait_ge(res_ready, t + 1)
                    pool.sem_inc(turns, 1)
                    nc.gpsimd.indirect_dma_start(
                        out=out, out_offset=bass.IndirectOffsetOnAxis(ap=token[u][:, 0:1], axis=0),
                        in_=res[u][:], in_offset=None, bounds_check=N - 1, oob_is_err=False).then_inc(res_out[u], 16)

            steps(pool, step)
            for u in range(UN):
                pool.wait_ge(res_out[u], 16 * NT // UN)

        @block.tensor
        def _(pe):
            def step(t, u, q):
                w = (u + 1) % UN
                w2 = (u + 2) % UN
                if there(t, NT):
                    pe.wait_ge(pre_ready, 2 * (t + 1))
                    at_least(pe, hid_ready, 2 * t)
                    for c in range(FC):
                        ins = nc.tensor.transpose(ps_t[c // 4][:, (c % 4) * P:(c % 4 + 1) * P],
                                                  pre[:, c * P:(c + 1) * P], ident[:])
                        if c % 4 == 3:
                            ins.then_inc(t_ready, 1)
                if there(t + 1, NT):
                    x = pe.value_load(tile_expert[0:1, bass.ds(t + 1, 1)], min_val=0, max_val=X - 1)
                    pe.wait_ge(xnt_ready, t + 2)
                    at_least(pe, pre_ready, 2 * (t + 1))
                    for i in range(2):
                        for k in range(KC):
                            ins = nc.tensor.matmul(ps_h[i][:], xnt[w][:, k, :],
                                                   w1s[:, bass.ds(x * (KC * F) + (k * F + i * HB), HB)],
                                                   start=(k == 0), stop=(k == KC - 1))
                        ins.then_inc(h_ready, 1)
                if there(t, NT):
                    x = pe.value_load(tile_expert[0:1, bass.ds(t, 1)], min_val=0, max_val=X - 1)
                    pe.wait_ge(hid_ready, 2 * (t + 1))
                    at_least(pe, y_read, t)
                    for c in range(FC):
                        ins = nc.tensor.matmul(ps_y[0][:, 0:HD], hid[:, c, :],
                                               w2s[:, bass.ds(x * (FC * HD) + c * HD, HD)],
                                               start=(c == 0), stop=(c == FC - 1))
                    ins.then_inc(y_ready, 1)
                if there(t + 2, NT):
                    pe.wait_ge(row_in[w2], 16 * (q + (u + 2) // UN + 1))
                    at_least(pe, xnt_ready, t + 2)
                    for k in range(KC):
                        ins = nc.tensor.transpose(ps_x[:, k * P:(k + 1) * P], row[w2][:, 0, k * P:(k + 1) * P],
                                                  ident[:])
                    ins.then_inc(px_ready, 1)

            steps(pe, step)

        @block.scalar
        def _(act):
            def step(t, u, q):
                w2 = (u + 2) % UN
                if there(t, NT):
                    for i in range(2):
                        act.wait_ge(t_ready, 2 * t + i + 1)
                        at_least(act, y_ready, t)
                        nc.scalar.activation(hid[:, 4 * i:4 * (i + 1), :],
                                             ps_t[i][:].rearrange("p (c t) -> p c t", c=4),
                                             ACT.Relu).then_inc(hid_ready, 1)
                if there(t + 2, NT):
                    act.wait_ge(px_ready, t + 3)
                    at_least(act, h_ready, 2 * t)
                    nc.scalar.copy(xnt[w2][:], ps_x[:, 0:HD].rearrange("p (k t) -> p k t", k=KC)).then_inc(
                        xnt_ready, 1)

            steps(act, step)

        @block.vector
        def _(dve):
            v = nc.vector
            v.memset(plus[:], 1e4).then_inc(const_ready, 1)
            v.memset(minus[:], -1e4).then_inc(const_ready, 1)
            dve.wait_ge(const_ready, 2)

            def step(t, u, q):
                w = (u + 1) % UN
                w2 = (u + 2) % UN
                if there(t + 2, NT):
                    n = q + (u + 2) // UN
                    dve.wait_ge(entry_in[w2], 16 * (n + 1))
                    at_least(dve, res_out[w2], 16 * n)
                    v.tensor_copy(token[w2][:], entry[w2][:, 0:1]).then_inc(token_ready, 1)
                if there(t + 1, NT):
                    x = dve.value_load(tile_expert[0:1, bass.ds(t + 1, 1)], min_val=0, max_val=X - 1)
                    for i in range(2):
                        dve.wait_ge(h_ready, 2 * (t + 1) + i + 1)
                        at_least(dve, t_ready, 2 * t + 2)
                        v.tensor_tensor(pre[:, i * HB:(i + 1) * HB], ps_h[i][:],
                                        b1r[:, bass.ds(x * F + i * HB, HB)], ALU.add).then_inc(pre_ready, 1)
                if there(t, NT):
                    x = dve.value_load(tile_expert[0:1, bass.ds(t, 1)], min_val=0, max_val=X - 1)
                    dve.wait_ge(y_ready, t + 1)
                    v.tensor_tensor(y[:], ps_y[0][:, 0:HD], b2r[:, bass.ds(x * HD, HD)],
                                    ALU.add).then_inc(y_read, 1)
                    dve.wait_ge(y_read, t + 1)
                    v.tensor_scalar(scaled[:], y[:], entry[u][:, 1:2], None, ALU.mult).then_inc(y_scaled, 1)
                    v.memset(clean[:], 0.0).then_inc(masks_ready, 1)
                    dve.wait_ge(y_scaled, t + 1)
                    v.tensor_tensor(is_number[:], scaled[:], scaled[:], ALU.is_equal).then_inc(masks_ready, 1)
                    v.tensor_scalar(is_plus[:], scaled[:], float("inf"), None, ALU.is_equal).then_inc(masks_ready, 1)
                    v.tensor_scalar(is_minus[:], scaled[:], float("-inf"), None, ALU.is_equal).then_inc(masks_ready, 1)
                    dve.wait_ge(masks_ready, 4 * (t + 1))
                    dve.sem_inc(turns_v, 1)
                    v.copy_predicated(clean[:], is_number[:], scaled[:]).then_inc(clean_step, 1)
                    dve.wait_ge(clean_step, 3 * t + 1)
                    dve.sem_inc(turns_v, 1)
                    v.copy_predicated(clean[:], is_plus[:], plus[:]).then_inc(clean_step, 1)
                    dve.wait_ge(clean_step, 3 * t + 2)
                    dve.sem_inc(turns_v, 1)
                    v.copy_predicated(clean[:], is_minus[:], minus[:]).then_inc(clean_step, 1)
                    dve.wait_ge(row_in[u], 16 * (q + 1))
                    at_least(dve, res_out[u], 16 * q)
                    dve.wait_ge(clean_step, 3 * t + 3)
                    v.tensor_tensor(res[u][:], clean[:], row[u][:, 1, :], ALU.add).then_inc(res_ready, 1)

            steps(dve, step)


def gnn_then_experts(nc, x_pad, w_t, a_src, a_dst, dst_heads, dst_chunks, dst_ext, src_pad, edge_attr_t, edge_w_t,
                     edge_b, bias, gate_w, gate_b, w1, b1, w2, b2, out):
    src_table = nc.dram_tensor("src_table", (NPAD, ROW), F32, kind="Internal").ap()
    dst_table = nc.dram_tensor("dst_table", (NPAD, 3 * VD), BF16, kind="Internal").ap()
    edge_parts = nc.dram_tensor("edge_parts", (27, EP), BF16, kind="Internal").ap()
    token_rows = nc.dram_tensor("token_rows", (NPAD + P, 2 * HD), F32, kind="Internal").ap()
    slots = nc.dram_tensor("slots", ((NT + 1) * P, 2), F32, kind="Internal").ap()
    with ExitStack() as ctx:
        m = Space(nc, ctx, "")
        ident = m.sb("ident", [P, P])
        logits = m.sb("logits", [P, NB * X])
        tile_expert = m.sb("tile_expert", [1, NT], I32)
        node_phase(nc, ident, x_pad, w_t, a_src, a_dst, src_table, dst_table)
        with ExitStack() as edges:
            e = Space(nc, edges, "")
            tables = (e.sb("item_edge", [1, NITEM], I32), e.sb("item_block", [1, NITEM], I32),
                      e.sb("neg_node", [P, NITEM]), e.sb("wparts", [KE, HD], BF16))
            setup_phase(nc, ident, tables, dst_heads, dst_chunks, edge_attr_t, edge_w_t, edge_b, edge_parts)
            acc = e.sb("acc", [P, NB * ROW])
            edge_phase(nc, ident, tables, acc, src_pad, dst_ext, edge_parts, src_table, dst_table)
            combine_phase(nc, ident, acc, (logits,), x_pad, bias, gate_w, gate_b, token_rows)
        weights = (m.sb("w1s", [P, X * KC * F]), m.sb("w2s", [P, X * F // P * HD]), m.sb("b1r", [P, X * F]),
                   m.sb("b2r", [P, X * HD]))
        route_phase(nc, (logits,), (tile_expert,), slots, weights, (w1, w2, b1, b2), token_rows)
        expert_phase(nc, ident, (tile_expert,), weights, slots, token_rows, out)


def kernel(x, src, dst, edge_attr_3, L0_gnn_W, L0_gnn_a_src, L0_gnn_a_dst, L0_gnn_edge_W, L0_gnn_edge_b,
           L0_gnn_bias, L0_ffn_gate_w, L0_ffn_gate_b, L0_ffn_w1, L0_ffn_b1, L0_ffn_w2, L0_ffn_b2):
    import numpy as np
    import concourse.bacc as bacc
    from concourse.bass_utils import run_bass_kernel_spmd

    def padded(a, before, after, fill):
        a = np.asarray(a)
        wide = np.full(a.shape[:-1] + (before + a.shape[-1] + after,), fill, a.dtype)
        wide[..., before:before + a.shape[-1]] = a
        return wide

    x = np.asarray(x)
    x_pad = np.zeros((NPAD, IN), x.dtype)
    x_pad[:N] = x
    dst_pad = padded(dst, 0, EP - E, SENTINEL)
    layout = {
        "x_pad": x_pad,
        "w_t": np.asarray(L0_gnn_W).T,
        "a_src": np.asarray(L0_gnn_a_src).reshape(1, HD),
        "a_dst": np.asarray(L0_gnn_a_dst).reshape(1, HD),
        "dst_heads": dst_pad[::P].reshape(1, NCHUNK),
        "dst_chunks": dst_pad.reshape(NCHUNK, P),
        "dst_ext": padded(padded(dst, 1, 0, -1), 0, EP - E, SENTINEL),
        "src_pad": padded(src, 0, EP - E, 0),
        "edge_attr_t": padded(np.asarray(edge_attr_3).T, 0, EP - E, 0),
        "edge_w_t": np.asarray(L0_gnn_edge_W).T,
        "edge_b": np.asarray(L0_gnn_edge_b).reshape(1, HD),
        "bias": np.asarray(L0_gnn_bias).reshape(1, HD),
        "gate_w": np.asarray(L0_ffn_gate_w),
        "gate_b": np.asarray(L0_ffn_gate_b).reshape(1, X),
        "w1": np.asarray(L0_ffn_w1),
        "b1": np.asarray(L0_ffn_b1).reshape(1, X * F),
        "w2": np.asarray(L0_ffn_w2),
        "b2": np.asarray(L0_ffn_b2).reshape(1, X * HD),
    }
    nc = bacc.Bacc("TRN2", target_bir_lowering=False, num_devices=1)
    arrays, args = {}, {}
    for name, a in layout.items():
        a = np.ascontiguousarray(a)
        arrays["in_" + name] = a
        args[name] = nc.dram_tensor("in_" + name, a.shape, mybir.dt.from_np(a.dtype), kind="ExternalInput").ap()
    out = nc.dram_tensor("out_0", (N, HD), F32, kind="ExternalOutput").ap()
    gnn_then_experts(nc, out=out, **args)
    r = run_bass_kernel_spmd(nc, [arrays], core_ids=[0])
    return r.results[0]["out_0"]
```

```python
from contextlib import ExitStack

import concourse.bass as bass
from concourse import mybir

P = 128
ALU = mybir.AluOpType
ACT = mybir.ActivationFunctionType
AX = mybir.AxisListType
F32 = mybir.dt.float32
BF16 = mybir.dt.bfloat16
I32 = mybir.dt.int32

N = 12500
E = 212500
IN = 256
H, D = 8, 32
HD = H * D
KC = IN // P
NB = -(-N // P)
NPAD = NB * P
G = 4
IE = G * P
BATCH = 3
RING = 3
ITEMS_NEEDED = -(-E // IE) + NB
NBATCH = -(-ITEMS_NEEDED // (BATCH * RING)) * RING
NITEM = NBATCH * BATCH
NCHUNK = -(-(E + IE + 2) // P)
EP = NCHUNK * P
DG = D + 1
ROW = H * DG
DG_MAX = H + 1
VD = HD + H
EA = 3
KE = 35
EPS = 1e-5
BIG = 1e30
SENTINEL = NPAD + 7
T = BATCH * G

X = 8
F = 1024
CAP = -(-5 * N // (4 * X))
NT = -(-N // P) + X - 1
DUMP = NPAD


def at_least(eng, sem, value):
    if not isinstance(value, int) or value > 0:
        eng.wait_ge(sem, value)


def there(index, count):
    return not isinstance(index, int) or 0 <= index < count


def run_steps(eng, step, first, head, tail, last, unroll):
    for s in range(first, head):
        step(s, s % unroll, s // unroll)
    if tail > head:
        with eng.Fori(head // unroll, tail // unroll) as q:
            for u in range(unroll):
                step(unroll * q + u, u, q)
    for s in range(tail, last):
        step(s, s % unroll, s // unroll)


class Space:

    def __init__(self, nc, ctx, prefix):
        self.nc, self.ctx, self.prefix = nc, ctx, prefix
        ctx.enter_context(nc.cleanup_on_exit())

    def sb(self, name, shape, dt=F32):
        return self.ctx.enter_context(self.nc.sbuf_tensor(self.prefix + name, shape, dt))

    def ps(self, name, shape, dt=F32):
        return self.ctx.enter_context(self.nc.psum_tensor(self.prefix + name, shape, dt))

    def sem(self, name):
        return self.nc.alloc_semaphore(self.prefix + name)


def make_identity(nc, pool, ident, cleared, ready):
    nc.gpsimd.memset(ident[:], 0.0).then_inc(cleared, 1)
    pool.wait_ge(cleared, 1)
    nc.gpsimd.affine_select(out=ident[:], in_=ident[:], compare_op=ALU.not_equal, fill=1.0, base=0,
                            pattern=[[-1, P]], channel_multiplier=1).then_inc(ready, 1)


def node_phase(nc, ident, x_pad, w_t, a_src, a_dst, src_table, dst_table):
    GW = HD + 2 * H
    with ExitStack() as ctx:
        m = Space(nc, ctx, "n_")
        waug = m.sb("waug", [P, KC, GW])
        arep = m.sb("arep", [P, 2, HD])
        prod = m.sb("prod", [P, KC, HD])
        x = [m.sb(f"x{u}", [P, IN]) for u in range(4)]
        stats = [m.sb(f"stats{u}", [P, 6]) for u in range(2)]
        mv = [m.sb(f"mv{u}", [P, 2]) for u in range(2)]
        veps = [m.sb(f"veps{u}", [P, 1]) for u in range(2)]
        std = [m.sb(f"std{u}", [P, 1]) for u in range(2)]
        rstd = [m.sb(f"rstd{u}", [P, 1]) for u in range(2)]
        xn = [m.sb(f"xn{u}", [P, IN]) for u in range(2)]
        xnt = [m.sb(f"xnt{u}", [P, KC, P]) for u in range(2)]
        srow = [m.sb(f"srow{u}", [P, H, DG]) for u in range(2)]
        drow = [m.sb(f"drow{u}", [P, 3, VD], BF16) for u in range(2)]
        rest = [m.sb(f"rest{u}", [P, VD]) for u in range(2)]
        tp = [m.ps(f"tp{u}", [P, 512]) for u in range(2)]
        gp = [m.ps(f"gp{u}", [P, 512]) for u in range(2)]

        weights_in = m.sem("weights_in")
        x_in = [m.sem(f"x_in{u}") for u in range(4)]
        srow_out = [m.sem(f"srow_out{u}") for u in range(2)]
        drow_out = [m.sem(f"drow_out{u}") for u in range(2)]
        ident_cleared = m.sem("ident_cleared")
        ident_ready = m.sem("ident_ready")
        prod_ready = m.sem("prod_ready")
        waug_ready = m.sem("waug_ready")
        stats_ready = m.sem("stats_ready")
        mv_ready = m.sem("mv_ready")
        var_ready = m.sem("var_ready")
        std_ready = m.sem("std_ready")
        rstd_ready = m.sem("rstd_ready")
        xn_ready = m.sem("xn_ready")
        tp_ready = m.sem("tp_ready")
        xnt_ready = m.sem("xnt_ready")
        gp_ready = m.sem("gp_ready")
        srow_ready = m.sem("srow_ready")
        rest_ready = m.sem("rest_ready")
        mid_ready = m.sem("mid_ready")
        lo_ready = m.sem("lo_ready")
        block = ctx.enter_context(nc.Block())

        def steps(eng, step):
            run_steps(eng, step, -2, 4, (NB - 4) // 4 * 4, NB + 1, 4)

        @block.sync
        def _(sp):
            for k in range(KC):
                sp.dma_start(waug[:, k, 0:HD], w_t[k * P:(k + 1) * P, :]).then_inc(weights_in, 16)
            sp.dma_start(arep[:, 0, :], a_dst.to_broadcast([P, HD])).then_inc(weights_in, 16)
            sp.dma_start(arep[:, 1, :], a_src.to_broadcast([P, HD])).then_inc(weights_in, 16)

            for b in range(2):
                sp.dma_start(x[b][:], x_pad[b * P:(b + 1) * P, :]).then_inc(x_in[b], 16)

            def step(s, u, q):
                if not isinstance(s, int) or s + 4 < NB:
                    w = (u + 4) % 4
                    at_least(sp, xn_ready, s + 1)
                    sp.dma_start(x[w][:], x_pad[bass.ds((s + 4) * P, P), :]).then_inc(x_in[w], 16)
                if there(s - 1, NB):
                    v = (u + 1) % 2
                    sp.wait_ge(srow_ready, s)
                    sp.dma_start(src_table[bass.ds((s - 1) * P, P), :],
                                 srow[v][:].rearrange("p h d -> p (h d)")).then_inc(srow_out[v], 16)
                    sp.wait_ge(lo_ready, s)
                    sp.dma_start(dst_table[bass.ds((s - 1) * P, P), :],
                                 drow[v][:].rearrange("p s v -> p (s v)")).then_inc(drow_out[v], 16)

            steps(sp, step)
            for u in range(2):
                sp.wait_ge(srow_out[u], 16 * NB // 2)
                sp.wait_ge(drow_out[u], 16 * NB // 2)

        @block.gpsimd
        def _(pool):
            make_identity(nc, pool, ident, ident_cleared, ident_ready)

        @block.tensor
        def _(pe):
            pe.wait_ge(ident_ready, 1)
            pe.wait_ge(waug_ready, KC * 2)

            def step(s, u, q):
                if not there(s, NB):
                    return
                v = u % 2
                pe.wait_ge(xn_ready, s + 1)
                at_least(pe, xnt_ready, s - 1)
                for k in range(KC):
                    ins = nc.tensor.transpose(tp[v][:, k * P:(k + 1) * P], xn[v][:, k * P:(k + 1) * P], ident[:])
                ins.then_inc(tp_ready, 1)
                pe.wait_ge(xnt_ready, s + 1)
                at_least(pe, rest_ready, s - 1)
                for k in range(KC):
                    ins = nc.tensor.matmul(gp[v][:, 0:GW], xnt[v][:, k, :], waug[:, k, :],
                                           start=(k == 0), stop=(k == KC - 1))
                ins.then_inc(gp_ready, 1)

            steps(pe, step)

        @block.vector
        def _(dve):
            dve.wait_ge(weights_in, 16 * (KC + 2))
            for s in range(2):
                for k in range(KC):
                    nc.vector.tensor_tensor(prod[:, k, :], waug[:, k, 0:HD], arep[:, s, :],
                                            ALU.mult).then_inc(prod_ready, 1)
                dve.wait_ge(prod_ready, KC * (s + 1))
                for k in range(KC):
                    nc.vector.tensor_reduce(waug[:, k, HD + s * H:HD + (s + 1) * H],
                                            prod[:, k, :].rearrange("p (h d) -> p h d", d=D),
                                            AX.X, ALU.add).then_inc(waug_ready, 1)
                dve.wait_ge(waug_ready, KC * (s + 1))

            def step(s, u, q):
                v, w = u % 2, (u + 1) % 2
                if there(s + 2, NB):
                    xs = (u + 2) % 4
                    dve.wait_ge(x_in[xs], 16 * (q + (u + 2) // 4 + 1))
                    nc.vector.bn_stats(stats[v][:], x[xs][:]).then_inc(stats_ready, 1)
                if there(s + 1, NB):
                    dve.wait_ge(std_ready, s + 2)
                    if there(s + 2, NB):
                        dve.wait_ge(stats_ready, s + 3)
                    nc.vector.reciprocal(rstd[w][:], std[w][:]).then_inc(rstd_ready, 1)
                if there(s + 2, NB):
                    if isinstance(s, int):
                        dve.wait_ge(stats_ready, s + 3)
                    nc.vector.bn_aggr(mv[v][:], stats[v][:]).then_inc(mv_ready, 1)
                if there(s + 1, NB):
                    dve.wait_ge(rstd_ready, s + 2)
                    at_least(dve, tp_ready, s)
                    xs = (u + 1) % 4
                    nc.vector.tensor_scalar(xn[w][:], x[xs][:], mv[w][:, 0:1], rstd[w][:], ALU.subtract,
                                            ALU.mult).then_inc(xn_ready, 1)
                if there(s + 2, NB):
                    dve.wait_ge(mv_ready, s + 3)
                    at_least(dve, std_ready, s + 1)
                    nc.vector.tensor_scalar_add(veps[v][:], mv[v][:, 1:2], EPS).then_inc(var_ready, 1)
                if there(s - 1, NB):
                    v = (u + 1) % 2
                    dve.wait_ge(srow_ready, s)
                    nc.vector.tensor_tensor(rest[v][:], gp[v][:, 0:VD], drow[v][:, 0, :],
                                            ALU.subtract).then_inc(rest_ready, 1)
                    dve.wait_ge(mid_ready, s)
                    nc.vector.tensor_tensor(drow[v][:, 2, :], rest[v][:], drow[v][:, 1, :],
                                            ALU.subtract).then_inc(lo_ready, 1)

            steps(dve, step)

        @block.scalar
        def _(act):
            def step(s, u, q):
                v = (u + 1) % 2
                if there(s + 2, NB):
                    act.wait_ge(var_ready, s + 3)
                    at_least(act, rstd_ready, s + 1)
                    nc.scalar.activation(std[u % 2][:], veps[u % 2][:], ACT.Sqrt).then_inc(std_ready, 1)
                if there(s, NB):
                    w = u % 2
                    act.wait_ge(tp_ready, s + 1)
                    at_least(act, gp_ready, s - 1)
                    nc.scalar.copy(xnt[w][:], tp[w][:, 0:IN].rearrange("p (k t) -> p k t", k=KC)).then_inc(
                        xnt_ready, 1)
                if there(s - 1, NB):
                    act.wait_ge(gp_ready, s)
                    at_least(act, drow_out[v], 16 * (2 * q + (u - 1) // 2))
                    at_least(act, srow_out[v], 16 * (2 * q + (u - 1) // 2))
                    nc.scalar.copy(drow[v][:, 0, :], gp[v][:, 0:VD])
                    nc.scalar.copy(srow[v][:, :, 0:D], gp[v][:, 0:HD].rearrange("p (h d) -> p h d", d=D))
                    nc.scalar.copy(srow[v][:, :, D], gp[v][:, VD:VD + H]).then_inc(srow_ready, 1)
                    act.wait_ge(rest_ready, s)
                    nc.scalar.copy(drow[v][:, 1, :], rest[v][:]).then_inc(mid_ready, 1)

            steps(act, step)


def setup_phase(nc, ident, tables, dst_heads, dst_chunks, edge_attr_t, edge_w_t, edge_b, edge_parts):
    item_edge, item_block, neg_node, wparts = tables
    COLS = EA * EP // P
    HALF = NITEM // 2
    with ExitStack() as ctx:
        m = Space(nc, ctx, "s_")
        heads_i = m.sb("heads_i", [P, NCHUNK], I32)
        heads = m.sb("heads", [P, NCHUNK])
        below = m.sb("below", [P, NCHUNK])
        thr_i = m.sb("thr_i", [P, 1], I32)
        thr = m.sb("thr", [P, 1])
        part_i = m.sb("part_i", [P, 1], I32)
        part = m.sb("part", [P, 1])
        num_i = m.sb("num_i", [P, NITEM], I32)
        num = m.sb("num", [P, NITEM])
        chunk = m.sb("chunk", [P, 1])
        chunk_i = m.sb("chunk_i", [P, 1], I32)
        rows_i = m.sb("rows_i", [P, P], I32)
        rows = m.sb("rows", [P, P])
        inside = m.sb("inside", [P, 1])
        first = m.sb("first", [P, 1])
        shifted = m.sb("shifted", [P, P])
        diff = m.sb("diff", [P, P])
        upto = m.sb("upto", [P, P])
        count = m.sb("count", [P, 1], I32)
        items_i = m.sb("items_i", [P, 1], I32)
        items = m.sb("items", [P, 1])
        ends = m.sb("ends", [P, 1])
        begins = m.sb("begins", [P, 1])
        base = m.sb("base", [P, 1])
        ones = m.sb("ones", [P, P])
        base_rep = m.sb("base_rep", [P, P])
        past = m.sb("past", [P, NITEM])
        at = m.sb("at", [P, NITEM])
        blk = m.sb("blk", [P, NITEM])
        edge = m.sb("edge", [P, NITEM])
        ea = m.sb("ea", [P, COLS])
        ea_rest = m.sb("ea_rest", [P, COLS])
        ea_part = [m.sb(f"ea_part{i}", [P, COLS], BF16) for i in range(3)]
        wf = m.sb("wf", [KE, HD])
        wrest = m.sb("wrest", [KE, HD])
        wpart = [m.sb(f"wpart{i}", [KE, HD], BF16) for i in range(3)]
        ps_small = m.ps("ps_small", [P, 512])
        ps_edge = [m.ps(f"ps_edge{i}", [P, 512]) for i in range(2)]
        ps_blk = [m.ps(f"ps_blk{i}", [P, 512]) for i in range(2)]

        heads_in = m.sem("heads_in")
        rows_in = m.sem("rows_in")
        ea_in = m.sem("ea_in")
        ea_out = m.sem("ea_out")
        w_in = m.sem("w_in")
        w_cleared = m.sem("w_cleared")
        w_out = m.sem("w_out")
        const_ready = m.sem("const_ready")
        cleared = m.sem("cleared")
        step = m.sem("step")
        chunk_ready = m.sem("chunk_ready")
        first_ready = m.sem("first_ready")
        count_ready = m.sem("count_ready")
        items_ready = m.sem("items_ready")
        ends_ready = m.sem("ends_ready")
        at_ready = m.sem("at_ready")
        spread = m.sem("spread")
        ea_step = m.sem("ea_step")
        ea_turn = m.sem("ea_turn")
        block = ctx.enter_context(nc.Block())

        @block.sync
        def _(sp):
            sp.dma_start(heads_i[:], dst_heads.to_broadcast([P, NCHUNK])).then_inc(heads_in, 16)
            flat = edge_attr_t.rearrange("k e -> (k e)").rearrange("(p c) -> p c", p=P)
            sp.dma_start(ea[:], flat).then_inc(ea_in, 16)
            sp.wait_ge(w_cleared, 2)
            for g in range(9):
                sp.dma_start(wf[EA * g:EA * (g + 1), :], edge_w_t).then_inc(w_in, 16)
            for j in range(3):
                sp.dma_start(wf[32 + j:33 + j, :], edge_b).then_inc(w_in, 16)
            sp.wait_ge(ea_step, 4)
            for j in range(3):
                sp.dma_start(wparts[9 * j:9 * j + 9, :], wpart[j][9 * j:9 * j + 9, :]).then_inc(w_out, 16)
                sp.dma_start(wparts[32 + j:33 + j, :], wpart[j][32 + j:33 + j, :]).then_inc(w_out, 16)
            sp.wait_ge(ea_step, 8)
            for j in range(3):
                for i in range(3):
                    rows_out = edge_parts[9 * j + EA * i:9 * j + EA * (i + 1), :]
                    sp.dma_start(rows_out.rearrange("k e -> (k e)").rearrange("(p c) -> p c", p=P),
                                 ea_part[i][:]).then_inc(ea_out, 16)
            sp.wait_ge(w_out, 6 * 16)
            sp.wait_ge(ea_out, 9 * 16)

        @block.gpsimd
        def _(pool):
            nc.gpsimd.iota(thr_i[:], pattern=[[0, 1]], base=0, channel_multiplier=P).then_inc(const_ready, 1)
            nc.gpsimd.iota(part_i[:], pattern=[[0, 1]], base=0, channel_multiplier=1).then_inc(const_ready, 1)
            nc.gpsimd.iota(num_i[:], pattern=[[1, NITEM]], base=0, channel_multiplier=0).then_inc(const_ready, 1)
            nc.gpsimd.memset(ones[:], 1.0).then_inc(cleared, 1)
            nc.gpsimd.memset(shifted[:], 0.0).then_inc(cleared, 1)
            pool.wait_ge(cleared, 2)
            nc.gpsimd.affine_select(out=shifted[:], in_=shifted[:], compare_op=ALU.not_equal, fill=1.0, base=-1,
                                    pattern=[[-1, P]], channel_multiplier=1).then_inc(const_ready, 1)
            nc.gpsimd.affine_select(out=upto[:], in_=ones[:], compare_op=ALU.is_ge, fill=0.0, base=0,
                                    pattern=[[1, P]], channel_multiplier=-1).then_inc(const_ready, 1)
            pool.wait_ge(chunk_ready, 1)
            nc.gpsimd.indirect_dma_start(out=rows_i[:], out_offset=None, in_=dst_chunks,
                                         in_offset=bass.IndirectOffsetOnAxis(ap=chunk_i[:, 0:1], axis=0)
                                         ).then_inc(rows_in, 16)
            pool.wait_ge(rows_in, 16)

        @block.tensor
        def _(pe):
            pe.wait_ge(first_ready, 2)
            nc.tensor.matmul(ps_small[:, 0:1], diff[:], first[:], start=True, stop=True).then_inc(count_ready, 1)
            pe.wait_ge(items_ready, 1)
            nc.tensor.matmul(ps_small[0:NB, 1:2], upto[0:NB, 0:NB], items[0:NB, :], start=True,
                             stop=True).then_inc(ends_ready, 1)
            pe.wait_ge(at_ready, 1)
            for i in range(2):
                cols = slice(HALF * i, HALF * (i + 1))
                nc.tensor.matmul(ps_edge[i][:, 0:HALF], base_rep[0:NB, :], at[0:NB, cols], start=True, stop=True)
                ins = nc.tensor.matmul(ps_blk[i][:, 0:HALF], ones[0:NB, :], past[0:NB, cols], start=True, stop=True)
            ins.then_inc(spread, 1)

        @block.vector
        def _(dve):
            done = [0]

            def link(ins):
                done[0] += 1
                ins.then_inc(step, 1)
                dve.wait_ge(step, done[0])

            v = nc.vector
            v.memset(wf[:], 0.0).then_inc(w_cleared, 1)
            v.memset(wparts[:], 0.0).then_inc(w_cleared, 1)
            dve.wait_ge(const_ready, 5)
            v.tensor_copy(thr[:], thr_i[:])
            v.tensor_copy(part[:], part_i[:])
            v.tensor_copy(num[:], num_i[:])
            dve.wait_ge(heads_in, 16)
            link(v.tensor_copy(heads[:], heads_i[:]))
            link(v.tensor_scalar(below[:], heads[:], thr[:], None, ALU.is_lt))
            link(v.tensor_reduce(chunk[:], below[:], AX.X, ALU.add))
            link(v.tensor_scalar(chunk[:], chunk[:], -1.0, 0.0, ALU.add, ALU.max))
            v.tensor_copy(chunk_i[:], chunk[:]).then_inc(chunk_ready, 1)
            dve.wait_ge(rows_in, 16)
            link(v.tensor_copy(rows[:], rows_i[:]))
            link(v.tensor_scalar(rows[:], rows[:], thr[:], None, ALU.is_lt))
            link(v.tensor_reduce(inside[:], rows[:], AX.X, ALU.add))
            v.scalar_tensor_tensor(out=first[:], in0=chunk[:], scalar=float(P), in1=inside[:], op0=ALU.mult,
                                   op1=ALU.add).then_inc(first_ready, 1)
            v.tensor_tensor(diff[:], shifted[:], ident[:], ALU.subtract).then_inc(first_ready, 1)
            dve.wait_ge(count_ready, 1)
            link(v.tensor_scalar(count[:], ps_small[:, 0:1], float(IE - 1), None, ALU.add))
            link(v.tensor_scalar(items_i[:], count[:], IE.bit_length() - 1, None, ALU.logical_shift_right))
            link(v.tensor_copy(items[:], items_i[:]))
            dve.sem_inc(items_ready, 1)
            dve.wait_ge(ends_ready, 1)
            dve.wait_ge(first_ready, 2)
            link(v.tensor_copy(ends[0:NB, :], ps_small[0:NB, 1:2]))
            link(v.tensor_tensor(begins[0:NB, :], ends[0:NB, :], items[0:NB, :], ALU.subtract))
            link(v.scalar_tensor_tensor(out=base[0:NB, :], in0=begins[0:NB, :], scalar=-float(IE),
                                        in1=first[0:NB, :], op0=ALU.mult, op1=ALU.add))
            link(v.tensor_scalar(base_rep[0:NB, :], ones[0:NB, :], base[0:NB, :], None, ALU.mult))
            link(v.tensor_scalar(past[0:NB, :], num[0:NB, :], ends[0:NB, :], None, ALU.is_ge))
            link(v.tensor_scalar(at[0:NB, :], num[0:NB, :], begins[0:NB, :], None, ALU.is_ge))
            v.tensor_tensor(at[0:NB, :], at[0:NB, :], past[0:NB, :], ALU.subtract).then_inc(at_ready, 1)
            dve.wait_ge(spread, 1)
            for i in range(2):
                cols = slice(HALF * i, HALF * (i + 1))
                link(v.scalar_tensor_tensor(out=edge[:, cols], in0=num[:, cols], scalar=float(IE),
                                            in1=ps_edge[i][:, 0:HALF], op0=ALU.mult, op1=ALU.add))
                link(v.tensor_scalar(blk[:, cols], ps_blk[i][:, 0:HALF], float(NB - 1), None, ALU.min))
            v.tensor_scalar(item_edge[:], edge[0:1, :], float(E), None, ALU.min)
            v.tensor_copy(item_block[:], blk[0:1, :])
            v.tensor_scalar(neg_node[:], blk[:], -float(P), part[:], ALU.mult, ALU.subtract)

            for turn, (whole, rest, parts, loaded, n) in enumerate(
                    [(wf, wrest, wpart, w_in, 12), (ea, ea_rest, ea_part, ea_in, 1)]):
                dve.wait_ge(ea_turn, 2 * turn + 1)
                v.tensor_tensor(rest[:], whole[:], parts[0][:], ALU.subtract).then_inc(ea_step, 1)
                dve.wait_ge(ea_turn, 2 * turn + 2)
                dve.wait_ge(ea_step, 4 * turn + 1)
                v.tensor_tensor(parts[2][:], rest[:], parts[1][:], ALU.subtract).then_inc(ea_step, 3)

        @block.scalar
        def _(act):
            for turn, (whole, rest, parts, loaded, n) in enumerate(
                    [(wf, wrest, wpart, w_in, 12), (ea, ea_rest, ea_part, ea_in, 1)]):
                act.wait_ge(loaded, 16 * n)
                nc.scalar.copy(parts[0][:], whole[:]).then_inc(ea_turn, 1)
                act.wait_ge(ea_step, 4 * turn + 1)
                nc.scalar.copy(parts[1][:], rest[:]).then_inc(ea_turn, 1)


def edge_phase(nc, ident, tables, acc, edge_ends, dst_ext, edge_parts, src_table, dst_table):
    item_edge, item_block, neg_node, wparts = tables
    PR = BATCH * H
    FH = 2 * HD
    NHALF = T // 2
    with ExitStack() as ctx:
        m = Space(nc, ctx, "e_")
        ends = [m.sb(f"ends{u}", [P, T, 3], I32) for u in range(RING)]
        rows = [m.sb(f"rows{u}", [P, T, H, DG]) for u in range(RING)]
        onehot_t = [m.sb(f"onehot_t{u}", [P, BATCH, G, P], BF16) for u in range(RING)]
        alpha = [m.sb(f"alpha{u}", [P, G, BATCH, H]) for u in range(RING)]
        fact = [m.sb(f"fact{u}", [P, BATCH, H]) for u in range(RING)]
        dst_row = [m.sb(f"dst_row{j}", [P, IE], I32) for j in range(BATCH)]
        parts = [m.sb(f"parts{j}", [P, 3, VD], BF16) for j in range(BATCH)]
        ea = [m.sb(f"ea{j}", [KE, IE], BF16) for j in range(BATCH)]
        distance = m.sb("distance", [P, IE])
        onehot = [[m.sb(f"onehot{v}_{j}", [P, G, P]) for j in range(BATCH)] for v in range(2)]
        enc = [m.sb(f"enc{v}", [P, FH]) for v in range(2)]
        prod = [m.sb(f"prod{v}", [P, FH]) for v in range(2)]
        red = m.sb("red", [P, T, H])
        score = m.sb("score", [P, T, H])
        dst_seq = m.sb("dst_seq", [PR, IE + 1], I32)
        gap_i = m.sb("gap_i", [PR, IE], I32)
        gap = gap_i[:].bitcast(F32)
        seq_max = m.sb("seq_max", [PR, IE])
        differs = m.sb("differs", [P, BATCH, G])
        final_edge = m.sb("final_edge", [P, G])
        last_max = m.sb("last_max", [P, BATCH, G, DG_MAX])
        absent = m.sb("absent", [P, BATCH])
        node_max = m.sb("node_max", [P, NB * H])
        new_max = m.sb("new_max", [P, BATCH, H])
        grown = m.sb("grown", [P, BATCH, H])
        max_rest = m.sb("max_rest", [P, BATCH * H])
        max_parts = m.sb("max_parts", [P, 3, BATCH * H], BF16)
        ident_b = m.sb("ident_b", [P, P], BF16)

        ps_enc = [m.ps(f"ps_enc{v}", [P, 512]) for v in range(2)]
        ps_dst = [m.ps(f"ps_dst{v}", [P, 512]) for v in range(2)]
        ps_seq = m.ps("ps_seq", [P, 512])
        ps_node = m.ps("ps_node", [P, 512])
        ps_back = ps_node[:, 0:G * PR].rearrange("p (g j h) -> p g j h", g=G, j=BATCH)
        ps_last = ps_node[:, 128:128 + BATCH * DG_MAX].rearrange("p (j h) -> p j h", j=BATCH)
        ps_ref = ps_node[:, 256:256 + T * H].rearrange("p (t h) -> p t h", t=T)
        ps_sum = m.ps("ps_sum", [P, 512])
        ps_shared = m.ps("ps_shared", [P, 512])
        ps_onehot = ps_shared[:, 0:G * P // 2].bitcast(BF16).rearrange("p (g n) -> p g n", g=G)
        ps_score = ps_shared[:, 384:384 + T * H].rearrange("p (t h) -> p t h", t=T)

        s = m.sem
        ones_ready, idb_ready, cleared = s("ones_ready"), s("idb_ready"), s("cleared")
        rows_free, turns, turns_pe = s("rows_free"), s("turns"), s("turns_pe")
        ends_in = [s(f"ends_in{u}") for u in range(RING)]
        gathered = [s(f"gathered{u}") for u in range(RING)]
        dst_row_in = [s(f"dst_row_in{j}") for j in range(BATCH)]
        parts_in = [s(f"parts_in{j}") for j in range(BATCH)]
        seq_in = s("seq_in")
        distance_ready, onehot_t_ready = s("distance_ready"), s("onehot_t_ready")
        enc_ready, relu_ready, dst_ready, prod_ready, red_ready = (
            s("enc_ready"), s("relu_ready"), s("dst_ready"), s("prod_ready"), s("red_ready"))
        score_ready, score1_ready, score2_ready, alpha_ready = (
            s("score_ready"), s("score1_ready"), s("score2_ready"), s("alpha_ready"))
        seq_ready, diff_ready, gap_ready, scan_ready = s("seq_ready"), s("diff_ready"), s("gap_ready"), s("scan_ready")
        back_ready, differs_ready, flag_ready, last_max_ready = (
            s("back_ready"), s("differs_ready"), s("flag_ready"), s("last_max_ready"))
        turned_ready, onehot_ready = s("turned_ready"), s("onehot_ready")
        last_ready, absent_ready = s("last_ready"), s("absent_ready")
        new_ready, kept_ready, grown_ready, fact_ready = (
            s("new_ready"), s("kept_ready"), s("grown_ready"), s("fact_ready"))
        hi_ready, rest_ready, mid_ready, rest2_ready, split_ready = (
            s("hi_ready"), s("rest_ready"), s("mid_ready"), s("rest2_ready"), s("split_ready"))
        ref_ready, off_ready, arg_ready, exp_ready = s("ref_ready"), s("off_ready"), s("arg_ready"), s("exp_ready")
        weighted, pool_weighted, summed, scaled, added = (
            s("weighted"), s("pool_weighted"), s("summed"), s("scaled"), s("added"))
        block = ctx.enter_context(nc.Block())

        def steps(eng, step, first=0):
            def of_six(k, u, q):
                step(k, u % RING, 2 * q + u // RING, u % 2)

            run_steps(eng, of_six, first, 2 * RING, (NBATCH - RING) // (2 * RING) * 2 * RING, NBATCH + 2, 2 * RING)

        @block.sync
        def _(sp):
            def start(k, j):
                return sp.value_load(item_edge[0:1, bass.ds(BATCH * k + j, 1)], min_val=0, max_val=E)

            def load_ends(k, u, q):
                at_least(sp, flag_ready, k - RING + 1)
                sp.sem_inc(turns, 1)
                if not isinstance(q, int) or q > 0:
                    sp.wait_ge(gathered[u], 16 * T * q)
                sp.sem_inc(turns, 1)
                for j in range(BATCH):
                    e = start(k, j)
                    sp.dma_start(ends[u][:, G * j:G * (j + 1), :].rearrange("p g c -> p (g c)"),
                                 edge_ends[bass.ds(3 * e, 3 * IE)].rearrange("(p c) -> p c", p=P)
                                 ).then_inc(ends_in[u], 16)

            def load_dst_row(k, j):
                e = start(k, j)
                at_least(sp, distance_ready, BATCH * (k - 1) + j + 1)
                sp.dma_start(dst_row[j][:], dst_ext[bass.ds(e + 1, IE)].rearrange("(a e) -> a e", a=1)
                             .to_broadcast([P, IE])).then_inc(dst_row_in[j], 16)

            def load_item(k, j):
                e = start(k, j)
                b = sp.value_load(item_block[0:1, bass.ds(BATCH * k + j, 1)], min_val=0, max_val=NB - 1)
                at_least(sp, score_ready, BATCH * (k - 1) + j + 1)
                sp.sem_inc(turns, 1)
                sp.dma_start(ea[j][0:27, :], edge_parts[:, bass.ds(e, IE)]).then_inc(parts_in[j], 16)
                sp.dma_start(parts[j][:].rearrange("p s v -> p (s v)"),
                             dst_table[bass.ds(b * P, P), :]).then_inc(parts_in[j], 16)

            def load_order(k):
                at_least(sp, diff_ready, k)
                sp.sem_inc(turns, 1)
                for j in range(BATCH):
                    e = start(k, j)
                    sp.dma_start(dst_seq[H * j:H * (j + 1), :], dst_ext[bass.ds(e, IE + 1)]
                                 .rearrange("(a e) -> a e", a=1).to_broadcast([H, IE + 1])).then_inc(seq_in, 16)

            def step(k, u, q, v):
                ahead2, ahead1 = there(k + 2, NBATCH), there(k + 1, NBATCH)
                if ahead2:
                    load_dst_row(k + 2, 0)
                if ahead1:
                    load_item(k + 1, 0)
                if ahead2:
                    load_ends(k + 2, (u + 2) % RING, q + (u + 2) // RING)
                    load_dst_row(k + 2, 1)
                if ahead1:
                    load_order(k + 1)
                    load_item(k + 1, 1)
                if ahead2:
                    load_dst_row(k + 2, 2)
                if ahead1:
                    load_item(k + 1, 2)

            sp.wait_ge(ones_ready, BATCH)
            steps(sp, step, -2)

        @block.gpsimd
        def _(pool):
            def gather(k, u, q, j):
                if j == 0:
                    pool.wait_ge(ends_in[u], 16 * BATCH * (q + 1))
                at_least(pool, summed, BATCH * (k - RING) + j + 1)
                pool.sem_inc(rows_free, 1)
                for g in range(G):
                    t = G * j + g
                    nc.gpsimd.indirect_dma_start(
                        out=rows[u][:, t].rearrange("p h d -> p (h d)"), out_offset=None, in_=src_table,
                        in_offset=bass.IndirectOffsetOnAxis(ap=ends[u][:, t, 0:1], axis=0)
                    ).then_inc(gathered[u], 16)

            def gaps(k):
                pool.wait_ge(seq_in, 16 * BATCH * (k + 1))
                at_least(pool, scan_ready, k)
                nc.gpsimd.tensor_tensor(gap_i[:], dst_seq[:, 0:IE], dst_seq[:, 1:IE + 1],
                                        ALU.subtract).then_inc(diff_ready, 1)

            def weigh(k, u):
                pool.wait_ge(exp_ready, k + 1)
                r = rows[u][:, T - G:T].rearrange("p g h d -> p (g h) d")
                nc.gpsimd.tensor_tensor(r[:, :, 0:D], r[:, :, 0:D], r[:, :, D:DG].to_broadcast([P, G * H, D]),
                                        ALU.mult).then_inc(pool_weighted, 1)

            def step(k, u, q, v):
                w, qw = (u + 1) % RING, q + (u + 1) // RING
                ahead = there(k + 1, NBATCH)
                if there(k - 2, NBATCH):
                    weigh(k - 2, (u - 2) % RING)
                if there(k, NBATCH):
                    gaps(k)
                if ahead:
                    gather(k + 1, w, qw, 0)
                    gather(k + 1, w, qw, 1)
                    gather(k + 1, w, qw, 2)

            steps(pool, step, -1)

        @block.tensor
        def _(pe):
            def products(k, u, h):
                j, v = h // 2, h % 2
                if v == 0:
                    pe.wait_ge(parts_in[j], 32 * (k + 1))
                    pe.wait_ge(onehot_t_ready, BATCH * k + j + 1)
                at_least(pe, relu_ready, NHALF * k + h - 1)
                for t in range(2):
                    g = 2 * (h % 2) + t
                    ins = nc.tensor.matmul(ps_enc[v][:, t * HD:(t + 1) * HD], ea[j][:, g:IE:G], wparts[:],
                                           start=True, stop=True)
                ins.then_inc(enc_ready, 1)
                at_least(pe, prod_ready, NHALF * k + h - 1)
                for t in range(2):
                    g = 2 * (h % 2) + t
                    for part in range(3):
                        ins = nc.tensor.matmul(ps_dst[v][:, t * HD:(t + 1) * HD], onehot_t[u][:, j, g, :],
                                               parts[j][:, part, 0:HD], start=(part == 0), stop=(part == 2))
                ins.then_inc(dst_ready, 1)

            def dst_scores(k, u, j):
                at_least(pe, onehot_ready, BATCH * (k - 1) + min(j + 2, BATCH))
                for g in range(G):
                    for part in range(3):
                        ins = nc.tensor.matmul(ps_score[:, G * j + g, :], onehot_t[u][:, j, g, :],
                                               parts[j][:, part, HD:VD], start=(part == 0), stop=(part == 2))
                ins.then_inc(score_ready, 1)

            def to_rows(k, u):
                pe.wait_ge(alpha_ready, k + 1)
                at_least(pe, scan_ready, k)
                for g in range(G):
                    ins = nc.tensor.transpose(ps_seq[0:PR, g:IE:G], alpha[u][:, g].rearrange("p j h -> p (j h)"),
                                              ident[:])
                ins.then_inc(seq_ready, 1)

            def to_edges(k):
                pe.wait_ge(scan_ready, k + 1)
                at_least(pe, off_ready, k)
                pe.sem_inc(turns_pe, 1)
                for g in range(G):
                    ins = nc.tensor.transpose(ps_back[:, g].rearrange("p j h -> p (j h)"), seq_max[:, g:IE:G],
                                              ident[0:PR, 0:PR])
                ins.then_inc(back_ready, 1)

            def turn_onehot(k, u, j):
                at_least(pe, onehot_ready, BATCH * k + j)
                for g in range(G):
                    ins = nc.tensor.transpose(ps_onehot[:, g, :], onehot_t[u][:, j, g, :], ident_b[:])
                ins.then_inc(turned_ready, 1)

            def node_maxima(k, pair):
                pe.wait_ge(last_max_ready, k + 1)
                for j in range(BATCH):
                    pe.wait_ge(onehot_ready, BATCH * k + j + 1)
                    for g in range(G):
                        ins = nc.tensor.matmul(ps_last[:, j, :], onehot[pair][j][:, g, :], last_max[:, j, g, :],
                                               start=(g == 0), stop=(g == G - 1))
                ins.then_inc(last_ready, 1)

            def references(k, u):
                pe.wait_ge(split_ready, k + 1)
                for j in range(BATCH):
                    for g in range(G):
                        for part in range(3):
                            ins = nc.tensor.matmul(ps_ref[:, G * j + g, :], onehot_t[u][:, j, g, :],
                                                   max_parts[:, part, H * j:H * (j + 1)],
                                                   start=(part == 0), stop=(part == 2))
                ins.then_inc(ref_ready, 1)

            def sums(k, u, j, pair):
                if j < BATCH - 1:
                    pe.wait_ge(weighted, (BATCH - 1) * k + j + 1)
                else:
                    pe.wait_ge(pool_weighted, k + 1)
                at_least(pe, added, BATCH * k + j)
                for g in range(G):
                    ins = nc.tensor.matmul(ps_sum[:, 0:ROW], onehot[pair][j][:, g, :],
                                           rows[u][:, G * j + g].rearrange("p h d -> p (h d)"),
                                           start=(g == 0), stop=(g == G - 1))
                ins.then_inc(summed, 1)

            def step(k, u, q, v):
                now, before, older = there(k, NBATCH), there(k - 1, NBATCH), there(k - 2, NBATCH)
                u1, u2 = (u - 1) % RING, (u - 2) % RING
                other = 1 - v
                if now:
                    products(k, u, 0)
                if before:
                    to_rows(k - 1, u1)
                    turn_onehot(k - 1, u1, 0)
                if now:
                    products(k, u, 1)
                if before:
                    turn_onehot(k - 1, u1, 1)
                    to_edges(k - 1)
                if now:
                    dst_scores(k, u, 0)
                    products(k, u, 2)
                if before:
                    turn_onehot(k - 1, u1, 2)
                    node_maxima(k - 1, other)
                if now:
                    products(k, u, 3)
                if older:
                    sums(k - 2, u2, 0, v)
                if now:
                    dst_scores(k, u, 1)
                    products(k, u, 4)
                if older:
                    sums(k - 2, u2, 1, v)
                if now:
                    products(k, u, 5)
                if before:
                    references(k - 1, u1)
                if now:
                    dst_scores(k, u, 2)
                if older:
                    sums(k - 2, u2, 2, v)

            pe.wait_ge(idb_ready, 1)
            steps(pe, step)

        @block.vector
        def _(dve):
            v = nc.vector

            def multiply(k, h):
                n = NHALF * k + h
                dve.wait_ge(relu_ready, n + 1)
                dve.wait_ge(dst_ready, n + 1)
                v.tensor_tensor(prod[h % 2][:], ps_dst[h % 2][:], enc[h % 2][:], ALU.mult).then_inc(prod_ready, 1)

            def add_up(k, h):
                dve.wait_ge(prod_ready, NHALF * k + h + 1)
                v.tensor_reduce(red[:, 2 * h:2 * h + 2, :],
                                prod[h % 2][:].rearrange("p (t h d) -> p t h d", t=2, d=D),
                                AX.X, ALU.add).then_inc(red_ready, 1)

            def source_scores(k, u, q):
                dve.wait_ge(gathered[u], 16 * T * (q + 1))
                dve.wait_ge(red_ready, NHALF * (k + 1))
                v.tensor_tensor(score[:], rows[u][:, :, :, D], red[:], ALU.add).then_inc(score1_ready, 1)

            def destination_scores(k):
                dve.wait_ge(score_ready, BATCH * (k + 1))
                dve.wait_ge(score1_ready, k + 1)
                v.tensor_tensor(red[:], ps_score[:], score[:], ALU.add).then_inc(score2_ready, 1)

            def leaky_relu(k, u):
                dve.wait_ge(score2_ready, k + 1)
                for j in range(BATCH):
                    r = red[:, G * j:G * (j + 1), :]
                    ins = v.scalar_tensor_tensor(out=alpha[u][:, :, j, :], in0=r, scalar=0.2, in1=r,
                                                 op0=ALU.mult, op1=ALU.max)
                ins.then_inc(alpha_ready, 1)

            def scan(k):
                dve.wait_ge(seq_ready, k + 1)
                dve.wait_ge(gap_ready, k + 1)
                v.tensor_tensor_scan(seq_max[:], gap, ps_seq[0:PR, :], -BIG, ALU.add, ALU.max).then_inc(scan_ready, 1)

            def compare(k, u):
                v.tensor_tensor(differs[:].rearrange("p j g -> p (j g)"), ends[u][:, :, 1], ends[u][:, :, 2],
                                ALU.not_equal).then_inc(differs_ready, 1)

            def flags(k):
                dve.wait_ge(differs_ready, k + 1)
                v.tensor_tensor(last_max[:, :, :, H], differs[:],
                                final_edge[:].rearrange("p (a g) -> p a g", a=1).to_broadcast([P, BATCH, G]),
                                ALU.max).then_inc(flag_ready, 1)

            def last_maxima(k):
                dve.wait_ge(back_ready, k + 1)
                dve.wait_ge(flag_ready, k + 1)
                for j in range(BATCH):
                    ins = v.tensor_tensor(last_max[:, j, :, 0:H], ps_back[:, :, j, :],
                                          last_max[:, j, :, H:H + 1].to_broadcast([P, G, H]), ALU.mult)
                ins.then_inc(last_max_ready, 1)

            def block_of(n):
                return dve.value_load(item_block[0:1, bass.ds(n, 1)], min_val=0, max_val=NB - 1)

            def absences(k):
                dve.wait_ge(last_ready, k + 1)
                v.tensor_scalar(absent[:], ps_last[:, :, H], BIG, -BIG, ALU.mult, ALU.add).then_inc(absent_ready, 1)

            def new_maximum(k, j, block):
                here = node_max[:, bass.ds(block * H, H)]
                n = BATCH * k + j
                if j == 0:
                    dve.wait_ge(absent_ready, k + 1)
                    at_least(dve, fact_ready, k)
                at_least(dve, kept_ready, n)
                for out, op in ((grown[:, j, :], ALU.subtract), (new_max[:, j, :], ALU.max)):
                    v.scalar_tensor_tensor(out=out, in0=ps_last[:, j, 0:H], scalar=absent[:, j:j + 1],
                                           in1=here, op0=ALU.add, op1=op).then_inc(new_ready, 1)

            def keep_maximum(k, j, block):
                here = node_max[:, bass.ds(block * H, H)]
                dve.wait_ge(new_ready, 2 * (BATCH * k + j + 1))
                v.tensor_scalar(here, new_max[:, j, :], 0.0, None, ALU.add).then_inc(kept_ready, 1)

            flat = new_max[:].rearrange("p j h -> p (j h)")

            def high_part(k):
                dve.wait_ge(new_ready, 2 * BATCH * (k + 1))
                at_least(dve, ref_ready, k)
                v.tensor_copy(max_parts[:, 0, :], flat).then_inc(hi_ready, 1)

            def high_rest(k):
                dve.wait_ge(hi_ready, k + 1)
                v.tensor_tensor(max_rest[:], flat, max_parts[:, 0, :], ALU.subtract).then_inc(rest_ready, 1)

            def middle_part(k):
                dve.wait_ge(rest_ready, k + 1)
                v.tensor_copy(max_parts[:, 1, :], max_rest[:]).then_inc(mid_ready, 1)

            def low_part(k):
                dve.wait_ge(mid_ready, k + 1)
                v.tensor_tensor(max_parts[:, 2, :], max_rest[:], max_parts[:, 1, :],
                                ALU.subtract).then_inc(split_ready, 1)

            def below_maxima(k, u):
                dve.wait_ge(ref_ready, k + 1)
                v.tensor_tensor(alpha[u][:], ps_ref[:].rearrange("p (j g) h -> p g j h", g=G), alpha[u][:],
                                ALU.subtract).then_inc(off_ready, 1)

            def weigh(k, u, j):
                dve.wait_ge(exp_ready, k + 1)
                r = rows[u][:, G * j:G * (j + 1)].rearrange("p g h d -> p (g h) d")
                v.tensor_tensor(r[:, :, 0:D], r[:, :, 0:D], r[:, :, D:DG].to_broadcast([P, G * H, D]),
                                ALU.mult).then_inc(weighted, 1)

            def rescale(k, u, j, block):
                n = BATCH * k + j
                by_head = acc[:, bass.ds(block * ROW, ROW)].rearrange("p (h d) -> p h d", d=DG)
                if j == 0:
                    dve.wait_ge(fact_ready, k + 1)
                at_least(dve, added, n)
                v.tensor_tensor(by_head, by_head, fact[u][:, j, :].rearrange("p (h a) -> p h a", a=1)
                                .to_broadcast([P, H, DG]), ALU.mult).then_inc(scaled, 1)

            def accumulate(k, j, block):
                here = acc[:, bass.ds(block * ROW, ROW)]
                dve.wait_ge(scaled, BATCH * k + j + 1)
                dve.wait_ge(summed, BATCH * k + j + 1)
                v.tensor_tensor(here, here, ps_sum[:, 0:ROW], ALU.add).then_inc(added, 1)

            def step(k, u, q, pair):
                now, before, older = there(k, NBATCH), there(k - 1, NBATCH), there(k - 2, NBATCH)
                u1, u2 = (u - 1) % RING, (u - 2) % RING
                old, mid = [None] * BATCH, [None] * BATCH
                if now:
                    multiply(k, 0)
                if before:
                    compare(k - 1, u1)
                    scan(k - 1)
                    flags(k - 1)
                if now:
                    add_up(k, 0)
                if older:
                    old[0] = block_of(BATCH * (k - 2))
                if now:
                    multiply(k, 1)
                if before:
                    last_maxima(k - 1)
                if older:
                    rescale(k - 2, u2, 0, old[0])
                if now:
                    add_up(k, 1)
                if older:
                    weigh(k - 2, u2, 0)
                if before:
                    mid[0] = block_of(BATCH * (k - 1))
                if now:
                    multiply(k, 2)
                if older:
                    weigh(k - 2, u2, 1)
                if before:
                    mid[1] = block_of(BATCH * (k - 1) + 1)
                if now:
                    add_up(k, 2)
                if before:
                    absences(k - 1)
                    mid[2] = block_of(BATCH * (k - 1) + 2)
                    new_maximum(k - 1, 0, mid[0])
                if now:
                    multiply(k, 3)
                if before:
                    keep_maximum(k - 1, 0, mid[0])
                if older:
                    old[1] = block_of(BATCH * (k - 2) + 1)
                if now:
                    add_up(k, 3)
                if before:
                    new_maximum(k - 1, 1, mid[1])
                if older:
                    accumulate(k - 2, 0, old[0])
                if before:
                    keep_maximum(k - 1, 1, mid[1])
                if older:
                    rescale(k - 2, u2, 1, old[1])
                if before:
                    new_maximum(k - 1, 2, mid[2])
                if older:
                    old[2] = block_of(BATCH * (k - 2) + 2)
                if now:
                    multiply(k, 4)
                if before:
                    high_part(k - 1)
                    keep_maximum(k - 1, 2, mid[2])
                    high_rest(k - 1)
                if now:
                    add_up(k, 4)
                if before:
                    middle_part(k - 1)
                if older:
                    accumulate(k - 2, 1, old[1])
                if before:
                    low_part(k - 1)
                if now:
                    multiply(k, 5)
                if older:
                    rescale(k - 2, u2, 2, old[2])
                if now:
                    add_up(k, 5)
                if before:
                    below_maxima(k - 1, u1)
                if now:
                    source_scores(k, u, q)
                    destination_scores(k)
                    leaky_relu(k, u)
                if older:
                    accumulate(k - 2, 2, old[2])

            for j in range(BATCH):
                v.memset(ea[j][:], 1.0).then_inc(ones_ready, 1)
            v.tensor_copy(ident_b[:], ident[:]).then_inc(idb_ready, 1)
            v.memset(node_max[:], -BIG).then_inc(cleared, 1)
            v.memset(final_edge[:], 0.0).then_inc(cleared, 1)
            v.memset(acc[:], 0.0).then_inc(cleared, 1)
            dve.wait_ge(cleared, 3)
            v.tensor_copy(final_edge[:, G - 1:G], ident[:, P - 1:P]).then_inc(cleared, 1)
            dve.wait_ge(cleared, 4)
            steps(dve, step)

        @block.scalar
        def _(act):
            def place(k, u, j):
                n = BATCH * k + j
                act.wait_ge(dst_row_in[j], 16 * (k + 1))
                at_least(act, onehot_t_ready, n)
                nc.scalar.activation(distance[:], dst_row[j][:], ACT.Abs,
                                     bias=neg_node[:, bass.ds(n, 1)]).then_inc(distance_ready, 1)
                act.wait_ge(distance_ready, n + 1)
                if j == 0:
                    at_least(act, ref_ready, k - RING + 1)
                nc.scalar.activation(onehot_t[u][:, j], distance[:].rearrange("p (e g) -> p g e", g=G), ACT.Relu,
                                     bias=1.0, scale=-1.0).then_inc(onehot_t_ready, 1)

            def relu(k, h):
                w, n = h % 2, NHALF * k + h
                act.wait_ge(enc_ready, n + 1)
                at_least(act, prod_ready, n - 1)
                nc.scalar.activation(enc[w][:], ps_enc[w][:], ACT.Relu).then_inc(relu_ready, 1)

            def onehot_out(k, j, pair):
                n = BATCH * k + j
                act.wait_ge(turned_ready, n + 1)
                at_least(act, summed, n - 2 * BATCH + 1)
                nc.scalar.copy(onehot[pair][j][:], ps_onehot).then_inc(onehot_ready, 1)

            def step(k, u, q, v):
                now, before = there(k, NBATCH), there(k - 1, NBATCH)
                u1 = (u - 1) % RING
                w = (u + 1) % RING
                ahead = there(k + 1, NBATCH)
                other = 1 - v
                if now:
                    relu(k, 0)
                if before:
                    onehot_out(k - 1, 0, other)
                if now:
                    relu(k, 1)
                if before:
                    onehot_out(k - 1, 1, other)
                if now:
                    relu(k, 2)
                if before:
                    onehot_out(k - 1, 2, other)
                if ahead:
                    place(k + 1, w, 0)
                if now:
                    relu(k, 3)
                if ahead:
                    place(k + 1, w, 1)
                if now:
                    relu(k, 4)
                if ahead:
                    place(k + 1, w, 2)
                if now:
                    act.wait_ge(diff_ready, k + 1)
                    nc.scalar.mul(gap, gap_i[:], BIG).then_inc(gap_ready, 1)
                if before:
                    act.wait_ge(new_ready, 2 * BATCH * k)
                    nc.scalar.activation(grown[:], grown[:], ACT.Relu).then_inc(grown_ready, 1)
                    act.wait_ge(grown_ready, k)
                    at_least(act, added, BATCH * (k - 1 - RING + 1))
                    nc.scalar.activation(fact[u1][:], grown[:], ACT.Exp, scale=-1.0).then_inc(fact_ready, 1)
                if now:
                    relu(k, 5)
                if before:
                    act.wait_ge(off_ready, k)
                    nc.scalar.activation(alpha[u1][:], alpha[u1][:], ACT.Relu).then_inc(arg_ready, 1)
                    act.wait_ge(arg_ready, k)
                    nc.scalar.activation(rows[u1][:, :, :, D].rearrange("p (j g) h -> p g j h", g=G),
                                         alpha[u1][:], ACT.Exp, scale=-1.0).then_inc(exp_ready, 1)

            steps(act, step, -1)


def combine_phase(nc, ident, acc, keep, x_pad, bias, gate_w, gate_b, token_rows):
    logits, = keep
    with ExitStack() as ctx:
        m = Space(nc, ctx, "c_")
        bias_rep = m.sb("bias_rep", [P, HD])
        gw = m.sb("gw", [P, KC, X])
        gb = m.sb("gb", [P, X])
        x = [m.sb(f"x{u}", [P, HD]) for u in range(2)]
        den = [m.sb(f"den{u}", [P, H]) for u in range(2)]
        gnn = [m.sb(f"gnn{u}", [P, HD]) for u in range(2)]
        stats = [m.sb(f"stats{u}", [P, 6]) for u in range(2)]
        mv = [m.sb(f"mv{u}", [P, 2]) for u in range(2)]
        veps = [m.sb(f"veps{u}", [P, 1]) for u in range(2)]
        std = [m.sb(f"std{u}", [P, 1]) for u in range(2)]
        rstd = [m.sb(f"rstd{u}", [P, 1]) for u in range(2)]
        row = [m.sb(f"row{u}", [P, 2, HD]) for u in range(4)]
        xnt = [m.sb(f"xnt{u}", [P, KC, P]) for u in range(2)]
        tp = [m.ps(f"tp{u}", [P, 512]) for u in range(2)]
        gp = [m.ps(f"gp{u}", [P, 512]) for u in range(2)]

        const_in = m.sem("const_in")
        turns = m.sem("turns")
        x_in = [m.sem(f"x_in{u}") for u in range(2)]
        row_out = [m.sem(f"row_out{u}") for u in range(4)]
        den_ready, rden_ready, gnn_ready, biased, x1_ready = (
            m.sem("den_ready"), m.sem("rden_ready"), m.sem("gnn_ready"), m.sem("biased"), m.sem("x1_ready"))
        stats_ready, mv_ready, var_ready, std_ready, rstd_ready, row_ready = (
            m.sem("stats_ready"), m.sem("mv_ready"), m.sem("var_ready"), m.sem("std_ready"),
            m.sem("rstd_ready"), m.sem("row_ready"))
        tp_ready, xnt_ready, gp_ready, logits_ready = (
            m.sem("tp_ready"), m.sem("xnt_ready"), m.sem("gp_ready"), m.sem("logits_ready"))
        block = ctx.enter_context(nc.Block())

        def steps(eng, step):
            run_steps(eng, step, -1, 8, (NB - 4) // 4 * 4, NB + 1, 4)

        @block.sync
        def _(sp):
            sp.dma_start(bias_rep[:], bias.to_broadcast([P, HD])).then_inc(const_in, 16)
            sp.dma_start(gb[:], gate_b.to_broadcast([P, X])).then_inc(const_in, 16)
            for k in range(KC):
                sp.dma_start(gw[:, k, :], gate_w[k * P:(k + 1) * P, :]).then_inc(const_in, 16)
            sp.dma_start(x[0][:], x_pad[0:P, :]).then_inc(x_in[0], 16)
            sp.dma_start(x[1][:], x_pad[P:2 * P, :]).then_inc(x_in[1], 16)

            def step(s, u, q):
                w = (u + 1) % 2
                if not isinstance(s, int) or s + 3 < NB:
                    sp.wait_ge(x1_ready, s + 2)
                    sp.dma_start(x[w][:], x_pad[bass.ds((s + 3) * P, P), :]).then_inc(x_in[w], 16)
                if there(s, NB):
                    sp.wait_ge(row_ready, s + 1)
                    sp.dma_start(token_rows[bass.ds(s * P, P), :],
                                 row[u][:].rearrange("p a d -> p (a d)")).then_inc(row_out[u], 16)

            steps(sp, step)
            for u in range(4):
                sp.wait_ge(row_out[u], 16 * len(range(u, NB, 4)))

        @block.tensor
        def _(pe):
            pe.wait_ge(const_in, 16 * (2 + KC))

            def step(s, u, q):
                v = u % 2
                if there(s, NB):
                    pe.wait_ge(row_ready, s + 1)
                    at_least(pe, xnt_ready, s - 1)
                    for k in range(KC):
                        ins = nc.tensor.transpose(tp[v][:, k * P:(k + 1) * P], row[u][:, 0, k * P:(k + 1) * P],
                                                  ident[:])
                    ins.then_inc(tp_ready, 1)
                    pe.wait_ge(xnt_ready, s + 1)
                    at_least(pe, logits_ready, s - 1)
                    for k in range(KC):
                        ins = nc.tensor.matmul(gp[v][:, 0:X], xnt[v][:, k, :], gw[:, k, :],
                                               start=(k == 0), stop=(k == KC - 1))
                    ins.then_inc(gp_ready, 1)

            steps(pe, step)

        @block.vector
        def _(dve):
            v = nc.vector
            dve.wait_ge(const_in, 16 * (2 + KC))

            def step(s, u, q):
                w, w4 = (u + 1) % 2, (u + 1) % 4
                o = u % 2
                if there(s + 1, NB):
                    sums = acc[:, bass.ds((s + 1) * ROW, ROW)].rearrange("p (h d) -> p h d", d=DG)
                    at_least(dve, gnn_ready, s)
                    v.tensor_scalar(den[w][:], sums[:, :, D], 1e-10, None, ALU.max).then_inc(den_ready, 1)
                    dve.wait_ge(den_ready, s + 2)
                    v.reciprocal(den[w][:], den[w][:]).then_inc(rden_ready, 1)
                if there(s, NB):
                    dve.wait_ge(std_ready, s + 1)
                    v.reciprocal(rstd[o][:], std[o][:]).then_inc(rstd_ready, 1)
                if there(s + 1, NB):
                    dve.wait_ge(rden_ready, s + 2)
                    v.tensor_tensor(gnn[w][:].rearrange("p (h d) -> p h d", d=D), sums[:, :, 0:D],
                                    den[w][:].rearrange("p (h a) -> p h a", a=1).to_broadcast([P, H, D]),
                                    ALU.mult).then_inc(gnn_ready, 1)
                if there(s, NB):
                    dve.wait_ge(rstd_ready, s + 1)
                    v.tensor_scalar(row[u][:, 0, :], row[u][:, 1, :], mv[o][:, 0:1], rstd[o][:], ALU.subtract,
                                    ALU.mult).then_inc(row_ready, 1)
                if there(s + 1, NB):
                    dve.wait_ge(gnn_ready, s + 2)
                    v.tensor_tensor(gnn[w][:], gnn[w][:], bias_rep[:], ALU.add).then_inc(biased, 1)
                    dve.wait_ge(x_in[w], 16 * (2 * q + (u + 1) // 2 + 1))
                    at_least(dve, row_out[w4], 16 * (q + (u + 1) // 4))
                    at_least(dve, tp_ready, s - 2)
                    dve.wait_ge(biased, s + 2)
                    v.tensor_tensor(row[w4][:, 1, :], gnn[w][:], x[w][:], ALU.add).then_inc(x1_ready, 1)
                if there(s - 1, NB):
                    dve.wait_ge(gp_ready, s)
                    v.tensor_tensor(logits[:, bass.ds((s - 1) * X, X)], gp[w][:, 0:X], gb[:],
                                    ALU.add).then_inc(logits_ready, 1)
                if there(s + 1, NB):
                    dve.wait_ge(x1_ready, s + 2)
                    v.bn_stats(stats[w][:], row[w4][:, 1, :]).then_inc(stats_ready, 1)
                    dve.wait_ge(stats_ready, s + 2)
                    at_least(dve, row_ready, s)
                    dve.sem_inc(turns, 1)
                    v.bn_aggr(mv[w][:], stats[w][:]).then_inc(mv_ready, 1)
                    dve.wait_ge(mv_ready, s + 2)
                    v.tensor_scalar_add(veps[w][:], mv[w][:, 1:2], EPS).then_inc(var_ready, 1)

            steps(dve, step)

        @block.scalar
        def _(act):
            def step(s, u, q):
                w, o = (u + 1) % 2, u % 2
                if there(s + 1, NB):
                    act.wait_ge(var_ready, s + 2)
                    at_least(act, rstd_ready, s)
                    nc.scalar.activation(std[w][:], veps[w][:], ACT.Sqrt).then_inc(std_ready, 1)
                if there(s, NB):
                    act.wait_ge(tp_ready, s + 1)
                    at_least(act, gp_ready, s - 1)
                    nc.scalar.copy(xnt[o][:], tp[o][:, 0:HD].rearrange("p (k t) -> p k t", k=KC)).then_inc(
                        xnt_ready, 1)

            steps(act, step)


def route_phase(nc, keep, tables, slots, weights, weights_dram, token_rows):
    logits, = keep
    tile_expert, = tables
    w1s, w2s, b1r, b2r = weights
    w1, w2, b1, b2 = weights_dram
    NX = NB * X
    with ExitStack() as ctx:
        m = Space(nc, ctx, "r_")
        top = m.sb("top", [P, NB])
        shift = m.sb("shift", [P, NB, X])
        expo = m.sb("expo", [P, NB, X])
        total = m.sb("total", [P, NB])
        prob = m.sb("prob", [P, NB])
        ptop = m.sb("ptop", [P, NB])
        rank = shift
        rank_i = m.sb("rank_i", [P, X], I32)
        rank_f = m.sb("rank_f", [P, X])
        best = m.sb("best", [P, NB])
        hot = m.sb("hot", [P, NB, X])
        hot_b = m.sb("hot_b", [P, NB, X], BF16)
        node_i = m.sb("node_i", [P, NB], I32)
        node = m.sb("node", [P, NB])
        real = m.sb("real", [P, NB])
        ones_b = m.sb("ones_b", [P, P], BF16)
        before_b = m.sb("before_b", [P, P], BF16)
        part_i = m.sb("part_i", [P, 1], I32)
        part = m.sb("part", [P, 1])
        zeros = m.sb("zeros", [P, NB])
        tile_total = m.sb("tile_total", [P, X, NB])
        running = m.sb("running", [P, X, NB])
        pos = expo
        mine = shift
        position = m.sb("position", [P, NB])
        kept = m.sb("kept", [P, NB])
        tiles_f = m.sb("tiles_f", [P, X])
        tiles_i = m.sb("tiles_i", [P, X], I32)
        tiles = m.sb("tiles", [P, X])
        tile_end = m.sb("tile_end", [P, X])
        slot_base = m.sb("slot_base", [P, X])
        base = m.sb("base", [P, NB])
        slot_f = m.sb("slot_f", [P, NB])
        unreal = m.sb("unreal", [P, NB])
        dump = m.sb("dump", [P, 1])
        slot_i = m.sb("slot_i", [P, NB], I32)
        entry = m.sb("entry", [P, NB, 2])
        num_i = m.sb("num_i", [1, NT], I32)
        num = m.sb("num", [1, NT])
        expert = m.sb("expert", [1, NT])
        past = m.sb("past", [1, NT])
        empty = m.sb("empty", [P, NT + 1, 2])
        blank = m.sb("blank", [P, 2 * HD])
        ps_in = [m.ps(f"ps_in{i}", [P, 512]) for i in range(2)]
        ps_all = [m.ps(f"ps_all{i}", [P, 512]) for i in range(2)]

        const_ready = m.sem("const_ready")
        cleared = m.sem("cleared")
        step = m.sem("step")
        hot_ready = m.sem("hot_ready")
        counted = m.sem("counted")
        shift_ready = m.sem("shift_ready")
        exp_ready = m.sem("exp_ready")
        empty_ready = m.sem("empty_ready")
        empty_out = m.sem("empty_out")
        weights_in = m.sem("weights_in")
        entry_ready = m.sem("entry_ready")
        slots_out = m.sem("slots_out")
        block = ctx.enter_context(nc.Block())
        HALF = NX // 2
        FC = F // P

        @block.sync
        def _(sp):
            sp.wait_ge(empty_ready, 2)
            sp.dma_start(slots.rearrange("(t p) c -> p t c", p=P), empty[:]).then_inc(empty_out, 16)
            sp.dma_start(token_rows[NPAD:NPAD + P, :], blank[:]).then_inc(empty_out, 16)
            for x in range(X):
                sp.dma_start(w1s[:, x * KC * F:(x + 1) * KC * F].rearrange("p (k f) -> p k f", k=KC),
                             w1[x].rearrange("(k p) f -> p k f", p=P)).then_inc(weights_in, 16)
                sp.dma_start(w2s[:, x * FC * HD:(x + 1) * FC * HD].rearrange("p (c d) -> p c d", c=FC),
                             w2[x].rearrange("(c p) d -> p c d", p=P)).then_inc(weights_in, 16)
            sp.dma_start(b1r[:], b1.to_broadcast([P, X * F])).then_inc(weights_in, 16)
            sp.dma_start(b2r[:], b2.to_broadcast([P, X * HD])).then_inc(weights_in, 16)
            sp.wait_ge(empty_out, 32)
            sp.wait_ge(weights_in, 16 * (2 * X + 2))

        @block.gpsimd
        def _(pool):
            g = nc.gpsimd
            g.iota(node_i[:], pattern=[[P, NB]], base=0, channel_multiplier=1).then_inc(const_ready, 1)
            g.iota(rank_i[:], pattern=[[-1, X]], base=X, channel_multiplier=0).then_inc(const_ready, 1)
            g.iota(part_i[:], pattern=[[0, 1]], base=0, channel_multiplier=1).then_inc(const_ready, 1)
            g.iota(num_i[:], pattern=[[1, NT]], base=0, channel_multiplier=0).then_inc(const_ready, 1)
            g.memset(ones_b[:], 1.0).then_inc(cleared, 1)
            g.memset(zeros[:], 0.0).then_inc(const_ready, 1)
            pool.wait_ge(cleared, 1)
            g.affine_select(out=before_b[:], in_=ones_b[:], compare_op=ALU.is_gt, fill=0.0, base=0,
                            pattern=[[1, P]], channel_multiplier=-1).then_inc(const_ready, 1)
            pool.wait_ge(entry_ready, 1)
            pool.wait_ge(empty_out, 32)
            for b in range(NB):
                g.indirect_dma_start(out=slots, out_offset=bass.IndirectOffsetOnAxis(ap=slot_i[:, b:b + 1], axis=0),
                                     in_=entry[:, b, :], in_offset=None).then_inc(slots_out, 16)
            pool.wait_ge(slots_out, 16 * NB)

        @block.tensor
        def _(pe):
            pe.wait_ge(const_ready, 6)
            pe.wait_ge(hot_ready, 1)
            flat = hot_b[:].rearrange("p b x -> p (b x)")
            for i in range(2):
                nc.tensor.matmul(ps_in[i][:, 0:HALF], before_b[:], flat[:, HALF * i:HALF * (i + 1)],
                                 start=True, stop=True)
                ins = nc.tensor.matmul(ps_all[i][:, 0:HALF], ones_b[:], flat[:, HALF * i:HALF * (i + 1)],
                                       start=True, stop=True)
            ins.then_inc(counted, 1)

        @block.scalar
        def _(act):
            act.wait_ge(shift_ready, 1)
            nc.scalar.activation(expo[:], shift[:], ACT.Exp).then_inc(exp_ready, 1)

        @block.vector
        def _(dve):
            v = nc.vector
            done = [0]

            def link(ins):
                done[0] += 1
                ins.then_inc(step, 1)
                dve.wait_ge(step, done[0])

            def over_x(ap):
                return ap[:].rearrange("p (b a) -> p b a", a=1).to_broadcast([P, NB, X])

            def over_b(ap):
                return ap[:].rearrange("p (a x) -> p a x", a=1).to_broadcast([P, NB, X])

            dve.wait_ge(const_ready, 6)
            v.tensor_copy(node[:], node_i[:])
            v.tensor_copy(rank_f[:], rank_i[:])
            link(v.tensor_copy(part[:], part_i[:]))
            link(v.tensor_scalar(dump[:], part[:], float(DUMP), None, ALU.add))
            link(v.memset(empty[:], 0.0))
            v.memset(blank[:], 0.0).then_inc(empty_ready, 1)
            v.tensor_scalar(empty[:, :, 0], empty[:, :, 0], dump[:], None, ALU.add).then_inc(empty_ready, 1)
            lg = logits[:].rearrange("p (b x) -> p b x", x=X)
            link(v.tensor_reduce(top[:], lg, AX.X, ALU.max))
            v.tensor_tensor(shift[:], lg, over_x(top), ALU.subtract).then_inc(shift_ready, 1)
            dve.wait_ge(exp_ready, 1)
            link(v.tensor_reduce(total[:], expo[:], AX.X, ALU.add))
            link(v.reciprocal(total[:], total[:]))
            link(v.tensor_tensor(expo[:], expo[:], over_x(total), ALU.mult))
            link(v.tensor_reduce(ptop[:], expo[:], AX.X, ALU.max))
            link(v.tensor_tensor(hot[:], expo[:], over_x(ptop), ALU.is_equal))
            link(v.tensor_tensor(rank[:], hot[:], over_b(rank_f), ALU.mult))
            link(v.tensor_reduce(best[:], rank[:], AX.X, ALU.max))
            link(v.tensor_scalar(real[:], node[:], float(N), None, ALU.is_lt))
            link(v.tensor_tensor(hot[:], over_b(rank_f), over_x(best), ALU.is_equal))
            link(v.tensor_tensor(hot[:], hot[:], over_x(real), ALU.mult))
            v.tensor_copy(hot_b[:], hot[:]).then_inc(hot_ready, 1)
            dve.wait_ge(counted, 1)
            for i in range(2):
                half = slice(NB // 2 * i, NB // 2 * (i + 1))
                link(v.tensor_copy(tile_total[:, :, half].rearrange("p x b -> p b x"),
                                   ps_all[i][:, 0:HALF].rearrange("p (b x) -> p b x", x=X)))
            for x in range(X):
                link(v.tensor_tensor_scan(running[:, x, :], tile_total[:, x, :], zeros[:], 0.0, ALU.add, ALU.add))
            link(v.tensor_scalar(tiles_i[:], running[:, :, NB - 1], float(P - 1), None, ALU.add))
            link(v.tensor_scalar(tiles_i[:], tiles_i[:], P.bit_length() - 1, None, ALU.logical_shift_right))
            link(v.tensor_copy(tiles[:], tiles_i[:]))
            link(v.tensor_tensor_scan(tile_end[:], tiles[:], zeros[:, 0:X], 0.0, ALU.add, ALU.add))
            link(v.tensor_tensor(slot_base[:], tile_end[:], tiles[:], ALU.subtract))
            link(v.tensor_scalar(slot_base[:], slot_base[:], float(P), None, ALU.mult))
            link(v.tensor_tensor(running[:], running[:], tile_total[:], ALU.subtract))
            for i in range(2):
                half = slice(NB // 2 * i, NB // 2 * (i + 1))
                link(v.tensor_tensor(pos[:, half, :], ps_in[i][:, 0:HALF].rearrange("p (b x) -> p b x", x=X),
                                     running[:, :, half].rearrange("p x b -> p b x"), ALU.add))
            link(v.tensor_tensor(mine[:], pos[:], hot[:], ALU.mult))
            link(v.tensor_reduce(position[:], mine[:], AX.X, ALU.add))
            link(v.tensor_scalar(kept[:], position[:], float(CAP), None, ALU.is_lt))
            link(v.tensor_tensor(entry[:, :, 1], ptop[:], kept[:], ALU.mult))
            link(v.tensor_copy(entry[:, :, 0], node[:]))
            link(v.tensor_tensor(mine[:], hot[:], over_b(slot_base), ALU.mult))
            link(v.tensor_reduce(base[:], mine[:], AX.X, ALU.add))
            link(v.tensor_tensor(slot_f[:], position[:], base[:], ALU.add))
            link(v.tensor_scalar(unreal[:], real[:], -1.0, 1.0, ALU.mult, ALU.add))
            link(v.tensor_scalar(dump[:], part[:], float(NT * P), None, ALU.add))
            link(v.tensor_scalar(unreal[:], unreal[:], dump[:], None, ALU.mult))
            link(v.tensor_tensor(slot_f[:], slot_f[:], unreal[:], ALU.add))
            v.tensor_copy(slot_i[:], slot_f[:]).then_inc(entry_ready, 1)
            link(v.tensor_copy(num[:], num_i[:]))
            link(v.tensor_scalar(expert[:], num[:], tile_end[0:1, 0:1], None, ALU.is_ge))
            for x in range(1, X - 1):
                link(v.tensor_scalar(past[:], num[:], tile_end[0:1, x:x + 1], None, ALU.is_ge))
                link(v.tensor_tensor(expert[:], expert[:], past[:], ALU.add))
            link(v.tensor_copy(tile_expert[:], expert[:]))


def expert_phase(nc, ident, tables, weights, slots, token_rows, out):
    tile_expert, = tables
    w1s, w2s, b1r, b2r = weights
    FC = F // P
    UN = 3
    HB = 512
    with ExitStack() as ctx:
        m = Space(nc, ctx, "f_")
        entry = [m.sb(f"entry{u}", [P, 2]) for u in range(UN)]
        token = [m.sb(f"token{u}", [P, 1], I32) for u in range(UN)]
        row = [m.sb(f"row{u}", [P, 2, HD]) for u in range(UN)]
        xnt = [m.sb(f"xnt{u}", [P, KC, P]) for u in range(UN)]
        pre = m.sb("pre", [P, F])
        hid = m.sb("hid", [P, FC, P])
        y = m.sb("y", [P, HD])
        scaled = m.sb("scaled", [P, HD])
        is_number = m.sb("is_number", [P, HD], I32)
        is_plus = m.sb("is_plus", [P, HD], I32)
        is_minus = m.sb("is_minus", [P, HD], I32)
        plus = m.sb("plus", [P, HD])
        minus = m.sb("minus", [P, HD])
        clean = m.sb("clean", [P, HD])
        res = [m.sb(f"res{u}", [P, HD]) for u in range(UN)]
        ps_x = m.ps("ps_x", [P, 512])
        ps_h = [m.ps(f"ps_h{i}", [P, 512]) for i in range(2)]
        ps_t = [m.ps(f"ps_t{i}", [P, 512]) for i in range(2)]
        ps_y = [m.ps(f"ps_y{i}", [P, 512]) for i in range(2)]

        entry_in = [m.sem(f"entry_in{u}") for u in range(UN)]
        row_in = [m.sem(f"row_in{u}") for u in range(UN)]
        res_out = [m.sem(f"res_out{u}") for u in range(UN)]
        const_ready, turns, turns_v = m.sem("const_ready"), m.sem("turns"), m.sem("turns_v")
        token_ready, px_ready, xnt_ready = m.sem("token_ready"), m.sem("px_ready"), m.sem("xnt_ready")
        h_ready, pre_ready, t_ready, hid_ready = (
            m.sem("h_ready"), m.sem("pre_ready"), m.sem("t_ready"), m.sem("hid_ready"))
        y_ready, y_read, y_scaled, masks_ready, clean_step, res_ready = (
            m.sem("y_ready"), m.sem("y_read"), m.sem("y_scaled"), m.sem("masks_ready"), m.sem("clean_step"),
            m.sem("res_ready"))
        block = ctx.enter_context(nc.Block())

        def steps(eng, step):
            run_steps(eng, step, -3, 2 * UN, NT - UN, NT, UN)

        @block.sync
        def _(sp):
            def step(t, u, q):
                if there(t + 3, NT):
                    at_least(sp, res_ready, t + 1)
                    sp.dma_start(entry[u][:], slots[bass.ds((t + 3) * P, P), :]).then_inc(entry_in[u], 16)

            steps(sp, step)

        @block.gpsimd
        def _(pool):
            def step(t, u, q):
                w = (u + 2) % UN
                if there(t + 2, NT):
                    pool.wait_ge(token_ready, t + 3)
                    at_least(pool, res_ready, t)
                    pool.sem_inc(turns, 1)
                    nc.gpsimd.indirect_dma_start(
                        out=row[w][:].rearrange("p a d -> p (a d)"), out_offset=None, in_=token_rows,
                        in_offset=bass.IndirectOffsetOnAxis(ap=token[w][:, 0:1], axis=0)).then_inc(row_in[w], 16)
                if there(t, NT):
                    pool.wait_ge(res_ready, t + 1)
                    pool.sem_inc(turns, 1)
                    nc.gpsimd.indirect_dma_start(
                        out=out, out_offset=bass.IndirectOffsetOnAxis(ap=token[u][:, 0:1], axis=0),
                        in_=res[u][:], in_offset=None, bounds_check=N - 1, oob_is_err=False).then_inc(res_out[u], 16)

            steps(pool, step)
            for u in range(UN):
                pool.wait_ge(res_out[u], 16 * NT // UN)

        @block.tensor
        def _(pe):
            def step(t, u, q):
                w = (u + 1) % UN
                w2 = (u + 2) % UN
                if there(t, NT):
                    pe.wait_ge(pre_ready, 2 * (t + 1))
                    at_least(pe, hid_ready, 2 * t)
                    for c in range(FC):
                        ins = nc.tensor.transpose(ps_t[c // 4][:, (c % 4) * P:(c % 4 + 1) * P],
                                                  pre[:, c * P:(c + 1) * P], ident[:])
                        if c % 4 == 3:
                            ins.then_inc(t_ready, 1)
                if there(t + 1, NT):
                    x = pe.value_load(tile_expert[0:1, bass.ds(t + 1, 1)], min_val=0, max_val=X - 1)
                    pe.wait_ge(xnt_ready, t + 2)
                    at_least(pe, pre_ready, 2 * (t + 1))
                    for i in range(2):
                        for k in range(KC):
                            ins = nc.tensor.matmul(ps_h[i][:], xnt[w][:, k, :],
                                                   w1s[:, bass.ds(x * (KC * F) + (k * F + i * HB), HB)],
                                                   start=(k == 0), stop=(k == KC - 1))
                        ins.then_inc(h_ready, 1)
                if there(t, NT):
                    x = pe.value_load(tile_expert[0:1, bass.ds(t, 1)], min_val=0, max_val=X - 1)
                    pe.wait_ge(hid_ready, 2 * (t + 1))
                    at_least(pe, y_read, t)
                    for c in range(FC):
                        ins = nc.tensor.matmul(ps_y[0][:, 0:HD], hid[:, c, :],
                                               w2s[:, bass.ds(x * (FC * HD) + c * HD, HD)],
                                               start=(c == 0), stop=(c == FC - 1))
                    ins.then_inc(y_ready, 1)
                if there(t + 2, NT):
                    pe.wait_ge(row_in[w2], 16 * (q + (u + 2) // UN + 1))
                    at_least(pe, xnt_ready, t + 2)
                    for k in range(KC):
                        ins = nc.tensor.transpose(ps_x[:, k * P:(k + 1) * P], row[w2][:, 0, k * P:(k + 1) * P],
                                                  ident[:])
                    ins.then_inc(px_ready, 1)

            steps(pe, step)

        @block.scalar
        def _(act):
            def step(t, u, q):
                w2 = (u + 2) % UN
                if there(t, NT):
                    for i in range(2):
                        act.wait_ge(t_ready, 2 * t + i + 1)
                        at_least(act, y_ready, t)
                        nc.scalar.activation(hid[:, 4 * i:4 * (i + 1), :],
                                             ps_t[i][:].rearrange("p (c t) -> p c t", c=4),
                                             ACT.Relu).then_inc(hid_ready, 1)
                if there(t + 2, NT):
                    act.wait_ge(px_ready, t + 3)
                    at_least(act, h_ready, 2 * t)
                    nc.scalar.copy(xnt[w2][:], ps_x[:, 0:HD].rearrange("p (k t) -> p k t", k=KC)).then_inc(
                        xnt_ready, 1)

            steps(act, step)

        @block.vector
        def _(dve):
            v = nc.vector
            v.memset(plus[:], 1e4).then_inc(const_ready, 1)
            v.memset(minus[:], -1e4).then_inc(const_ready, 1)
            dve.wait_ge(const_ready, 2)

            def step(t, u, q):
                w = (u + 1) % UN
                w2 = (u + 2) % UN
                if there(t + 2, NT):
                    n = q + (u + 2) // UN
                    dve.wait_ge(entry_in[w2], 16 * (n + 1))
                    at_least(dve, res_out[w2], 16 * n)
                    v.tensor_copy(token[w2][:], entry[w2][:, 0:1]).then_inc(token_ready, 1)
                if there(t + 1, NT):
                    x = dve.value_load(tile_expert[0:1, bass.ds(t + 1, 1)], min_val=0, max_val=X - 1)
                    for i in range(2):
                        dve.wait_ge(h_ready, 2 * (t + 1) + i + 1)
                        at_least(dve, t_ready, 2 * t + 2)
                        v.tensor_tensor(pre[:, i * HB:(i + 1) * HB], ps_h[i][:],
                                        b1r[:, bass.ds(x * F + i * HB, HB)], ALU.add).then_inc(pre_ready, 1)
                if there(t, NT):
                    x = dve.value_load(tile_expert[0:1, bass.ds(t, 1)], min_val=0, max_val=X - 1)
                    dve.wait_ge(y_ready, t + 1)
                    v.tensor_tensor(y[:], ps_y[0][:, 0:HD], b2r[:, bass.ds(x * HD, HD)],
                                    ALU.add).then_inc(y_read, 1)
                    dve.wait_ge(y_read, t + 1)
                    v.tensor_scalar(scaled[:], y[:], entry[u][:, 1:2], None, ALU.mult).then_inc(y_scaled, 1)
                    v.memset(clean[:], 0.0).then_inc(masks_ready, 1)
                    dve.wait_ge(y_scaled, t + 1)
                    v.tensor_tensor(is_number[:], scaled[:], scaled[:], ALU.is_equal).then_inc(masks_ready, 1)
                    v.tensor_scalar(is_plus[:], scaled[:], float("inf"), None, ALU.is_equal).then_inc(masks_ready, 1)
                    v.tensor_scalar(is_minus[:], scaled[:], float("-inf"), None, ALU.is_equal).then_inc(masks_ready, 1)
                    dve.wait_ge(masks_ready, 4 * (t + 1))
                    dve.sem_inc(turns_v, 1)
                    v.copy_predicated(clean[:], is_number[:], scaled[:]).then_inc(clean_step, 1)
                    dve.wait_ge(clean_step, 3 * t + 1)
                    dve.sem_inc(turns_v, 1)
                    v.copy_predicated(clean[:], is_plus[:], plus[:]).then_inc(clean_step, 1)
                    dve.wait_ge(clean_step, 3 * t + 2)
                    dve.sem_inc(turns_v, 1)
                    v.copy_predicated(clean[:], is_minus[:], minus[:]).then_inc(clean_step, 1)
                    dve.wait_ge(row_in[u], 16 * (q + 1))
                    at_least(dve, res_out[u], 16 * q)
                    dve.wait_ge(clean_step, 3 * t + 3)
                    v.tensor_tensor(res[u][:], clean[:], row[u][:, 1, :], ALU.add).then_inc(res_ready, 1)

            steps(dve, step)


def gnn_then_experts(nc, x_pad, w_t, a_src, a_dst, dst_heads, dst_chunks, dst_ext, edge_ends, edge_attr_t, edge_w_t,
                     edge_b, bias, gate_w, gate_b, w1, b1, w2, b2, out):
    src_table = nc.dram_tensor("src_table", (NPAD, ROW), F32, kind="Internal").ap()
    dst_table = nc.dram_tensor("dst_table", (NPAD, 3 * VD), BF16, kind="Internal").ap()
    edge_parts = nc.dram_tensor("edge_parts", (27, EP), BF16, kind="Internal").ap()
    token_rows = nc.dram_tensor("token_rows", (NPAD + P, 2 * HD), F32, kind="Internal").ap()
    slots = nc.dram_tensor("slots", ((NT + 1) * P, 2), F32, kind="Internal").ap()
    with ExitStack() as ctx:
        m = Space(nc, ctx, "")
        ident = m.sb("ident", [P, P])
        logits = m.sb("logits", [P, NB * X])
        tile_expert = m.sb("tile_expert", [1, NT], I32)
        node_phase(nc, ident, x_pad, w_t, a_src, a_dst, src_table, dst_table)
        with ExitStack() as edges:
            e = Space(nc, edges, "")
            tables = (e.sb("item_edge", [1, NITEM], I32), e.sb("item_block", [1, NITEM], I32),
                      e.sb("neg_node", [P, NITEM]), e.sb("wparts", [KE, HD], BF16))
            setup_phase(nc, ident, tables, dst_heads, dst_chunks, edge_attr_t, edge_w_t, edge_b, edge_parts)
            acc = e.sb("acc", [P, NB * ROW])
            edge_phase(nc, ident, tables, acc, edge_ends, dst_ext, edge_parts, src_table, dst_table)
            combine_phase(nc, ident, acc, (logits,), x_pad, bias, gate_w, gate_b, token_rows)
        weights = (m.sb("w1s", [P, X * KC * F]), m.sb("w2s", [P, X * F // P * HD]), m.sb("b1r", [P, X * F]),
                   m.sb("b2r", [P, X * HD]))
        route_phase(nc, (logits,), (tile_expert,), slots, weights, (w1, w2, b1, b2), token_rows)
        expert_phase(nc, ident, (tile_expert,), weights, slots, token_rows, out)


def kernel(x, src, dst, edge_attr_3, L0_gnn_W, L0_gnn_a_src, L0_gnn_a_dst, L0_gnn_edge_W, L0_gnn_edge_b,
           L0_gnn_bias, L0_ffn_gate_w, L0_ffn_gate_b, L0_ffn_w1, L0_ffn_b1, L0_ffn_w2, L0_ffn_b2):
    import numpy as np
    import concourse.bacc as bacc
    from concourse.bass_utils import run_bass_kernel_spmd

    def padded(a, before, after, fill):
        a = np.asarray(a)
        wide = np.full(a.shape[:-1] + (before + a.shape[-1] + after,), fill, a.dtype)
        wide[..., before:before + a.shape[-1]] = a
        return wide

    dst = np.asarray(dst)
    x = np.asarray(x)
    x_pad = np.zeros((NPAD, IN), x.dtype)
    x_pad[:N] = x
    dst_pad = padded(dst, 0, EP - E, SENTINEL)
    layout = {
        "x_pad": x_pad,
        "w_t": np.asarray(L0_gnn_W).T,
        "a_src": np.asarray(L0_gnn_a_src).reshape(1, HD),
        "a_dst": np.asarray(L0_gnn_a_dst).reshape(1, HD),
        "dst_heads": dst_pad[::P].reshape(1, NCHUNK),
        "dst_chunks": dst_pad.reshape(NCHUNK, P),
        "dst_ext": padded(padded(dst, 1, 0, -1), 0, EP - E, SENTINEL),
        "edge_ends": np.stack([padded(src, 0, EP - E, 0), dst_pad, padded(dst[1:], 0, EP - E + 1, SENTINEL)],
                              axis=1).reshape(EP * 3),
        "edge_attr_t": padded(np.asarray(edge_attr_3).T, 0, EP - E, 0),
        "edge_w_t": np.asarray(L0_gnn_edge_W).T,
        "edge_b": np.asarray(L0_gnn_edge_b).reshape(1, HD),
        "bias": np.asarray(L0_gnn_bias).reshape(1, HD),
        "gate_w": np.asarray(L0_ffn_gate_w),
        "gate_b": np.asarray(L0_ffn_gate_b).reshape(1, X),
        "w1": np.asarray(L0_ffn_w1),
        "b1": np.asarray(L0_ffn_b1).reshape(1, X * F),
        "w2": np.asarray(L0_ffn_w2),
        "b2": np.asarray(L0_ffn_b2).reshape(1, X * HD),
    }
    nc = bacc.Bacc("TRN2", target_bir_lowering=False, num_devices=1)
    arrays, args = {}, {}
    for name, a in layout.items():
        a = np.ascontiguousarray(a)
        arrays["in_" + name] = a
        args[name] = nc.dram_tensor("in_" + name, a.shape, mybir.dt.from_np(a.dtype), kind="ExternalInput").ap()
    out = nc.dram_tensor("out_0", (N, HD), F32, kind="ExternalOutput").ap()
    gnn_then_experts(nc, out=out, **args)
    r = run_bass_kernel_spmd(nc, [arrays], core_ids=[0])
    return r.results[0]["out_0"]
```

```python
from contextlib import ExitStack

import concourse.bass as bass
from concourse import mybir

P = 128
ALU = mybir.AluOpType
ACT = mybir.ActivationFunctionType
AX = mybir.AxisListType
F32 = mybir.dt.float32
BF16 = mybir.dt.bfloat16
I32 = mybir.dt.int32

N = 12500
E = 212500
IN = 256
H, D = 8, 32
HD = H * D
KC = IN // P
NB = -(-N // P)
NPAD = NB * P
G = 4
IE = G * P
BATCH = 3
RING = 3
ITEMS_NEEDED = (E + NB * (IE - 1)) // IE
NBATCH = -(-ITEMS_NEEDED // BATCH)
NITEM = -(-NBATCH * BATCH // 2) * 2
NCHUNK = -(-(E + IE + 2) // P)
EP = NCHUNK * P
DG = D + 1
ROW = H * DG
DG_MAX = H + 1
VD = HD + H
EA = 3
KE = 35
EPS = 1e-5
BIG = 1e30
SENTINEL = NPAD + 7
T = BATCH * G

X = 8
F = 1024
CAP = -(-5 * N // (4 * X))
NT = -(-N // P) + X - 1
DUMP = NPAD


def at_least(eng, sem, value):
    if not isinstance(value, int) or value > 0:
        eng.wait_ge(sem, value)


def there(index, count):
    return not isinstance(index, int) or 0 <= index < count


def run_steps(eng, step, first, head, tail, last, unroll):
    for s in range(first, head):
        step(s, s % unroll, s // unroll)
    if tail > head:
        with eng.Fori(head // unroll, tail // unroll) as q:
            for u in range(unroll):
                step(unroll * q + u, u, q)
    for s in range(tail, last):
        step(s, s % unroll, s // unroll)


class Space:

    def __init__(self, nc, ctx, prefix):
        self.nc, self.ctx, self.prefix = nc, ctx, prefix
        ctx.enter_context(nc.cleanup_on_exit())

    def sb(self, name, shape, dt=F32):
        return self.ctx.enter_context(self.nc.sbuf_tensor(self.prefix + name, shape, dt))

    def ps(self, name, shape, dt=F32):
        return self.ctx.enter_context(self.nc.psum_tensor(self.prefix + name, shape, dt))

    def sem(self, name):
        return self.nc.alloc_semaphore(self.prefix + name)


def make_identity(nc, pool, ident, cleared, ready):
    nc.gpsimd.memset(ident[:], 0.0).then_inc(cleared, 1)
    pool.wait_ge(cleared, 1)
    nc.gpsimd.affine_select(out=ident[:], in_=ident[:], compare_op=ALU.not_equal, fill=1.0, base=0,
                            pattern=[[-1, P]], channel_multiplier=1).then_inc(ready, 1)


def node_phase(nc, ident, x_pad, w_t, a_src, a_dst, edge_attr_t, src_table, dst_table, edge_parts):
    GW = HD + 2 * H
    COLS = EA * EP // P
    with ExitStack() as ctx:
        m = Space(nc, ctx, "n_")
        waug = m.sb("waug", [P, KC, GW])
        arep = m.sb("arep", [P, 2, HD])
        prod = m.sb("prod", [P, KC, HD])
        x = [m.sb(f"x{u}", [P, IN]) for u in range(4)]
        stats = [m.sb(f"stats{u}", [P, 6]) for u in range(2)]
        mv = [m.sb(f"mv{u}", [P, 2]) for u in range(2)]
        veps = [m.sb(f"veps{u}", [P, 1]) for u in range(2)]
        std = [m.sb(f"std{u}", [P, 1]) for u in range(2)]
        rstd = [m.sb(f"rstd{u}", [P, 1]) for u in range(2)]
        xn = [m.sb(f"xn{u}", [P, IN]) for u in range(2)]
        xnt = [m.sb(f"xnt{u}", [P, KC, P]) for u in range(2)]
        srow = [m.sb(f"srow{u}", [P, H, DG]) for u in range(4)]
        drow = [m.sb(f"drow{u}", [P, 3, VD], BF16) for u in range(4)]
        rest = [m.sb(f"rest{u}", [P, VD]) for u in range(2)]
        ea = m.sb("ea", [P, COLS])
        ea_rest = m.sb("ea_rest", [P, COLS])
        ea_part = [m.sb(f"ea_part{i}", [P, COLS], BF16) for i in range(3)]
        tp = [m.ps(f"tp{u}", [P, 512]) for u in range(2)]
        gp = [m.ps(f"gp{u}", [P, 512]) for u in range(2)]

        ea_in, ea_out = m.sem("ea_in"), m.sem("ea_out")
        ea_high, ea_rest_ready, ea_middle, ea_low = (
            m.sem("ea_high"), m.sem("ea_rest_ready"), m.sem("ea_middle"), m.sem("ea_low"))
        weights_in = m.sem("weights_in")
        x_in = [m.sem(f"x_in{u}") for u in range(4)]
        srow_out = [m.sem(f"srow_out{u}") for u in range(4)]
        drow_out = [m.sem(f"drow_out{u}") for u in range(4)]
        ident_cleared = m.sem("ident_cleared")
        ident_ready = m.sem("ident_ready")
        prod_ready = m.sem("prod_ready")
        waug_ready = m.sem("waug_ready")
        stats_ready = m.sem("stats_ready")
        mv_ready = m.sem("mv_ready")
        var_ready = m.sem("var_ready")
        std_ready = m.sem("std_ready")
        rstd_ready = m.sem("rstd_ready")
        xn_ready = m.sem("xn_ready")
        tp_ready = m.sem("tp_ready")
        xnt_ready = m.sem("xnt_ready")
        gp_ready = m.sem("gp_ready")
        srow_ready = m.sem("srow_ready")
        rest_ready = m.sem("rest_ready")
        mid_ready = m.sem("mid_ready")
        lo_ready = m.sem("lo_ready")
        block = ctx.enter_context(nc.Block())

        def steps(eng, step):
            run_steps(eng, step, -2, 8, (NB - 4) // 4 * 4, NB + 2, 4)

        @block.sync
        def _(sp):
            for k in range(KC):
                sp.dma_start(waug[:, k, 0:HD], w_t[k * P:(k + 1) * P, :]).then_inc(weights_in, 16)
            sp.dma_start(arep[:, 0, :], a_dst.to_broadcast([P, HD])).then_inc(weights_in, 16)
            sp.dma_start(arep[:, 1, :], a_src.to_broadcast([P, HD])).then_inc(weights_in, 16)

            for b in range(2):
                sp.dma_start(x[b][:], x_pad[b * P:(b + 1) * P, :]).then_inc(x_in[b], 16)

            def step(s, u, q):
                if not isinstance(s, int) or s + 4 < NB:
                    w = (u + 4) % 4
                    at_least(sp, xn_ready, s + 1)
                    sp.dma_start(x[w][:], x_pad[bass.ds((s + 4) * P, P), :]).then_inc(x_in[w], 16)
                if there(s - 1, NB):
                    v = (u - 1) % 4
                    sp.wait_ge(srow_ready, s)
                    sp.dma_start(src_table[bass.ds((s - 1) * P, P), :],
                                 srow[v][:].rearrange("p h d -> p (h d)")).then_inc(srow_out[v], 16)
                if there(s - 2, NB):
                    v = (u - 2) % 4
                    sp.wait_ge(lo_ready, s - 1)
                    sp.dma_start(dst_table[bass.ds((s - 2) * P, P), :],
                                 drow[v][:].rearrange("p s v -> p (s v)")).then_inc(drow_out[v], 16)

            steps(sp, step)
            for u in range(4):
                sp.wait_ge(srow_out[u], 16 * len(range(u, NB, 4)))
                sp.wait_ge(drow_out[u], 16 * len(range(u, NB, 4)))

        @block.gpsimd
        def _(pool):
            nc.gpsimd.dma_start(ea[:], edge_attr_t.rearrange("k e -> (k e)").rearrange("(p c) -> p c", p=P)
                                ).then_inc(ea_in, 16)
            make_identity(nc, pool, ident, ident_cleared, ident_ready)
            for i, part_ready in enumerate((ea_high, ea_middle, ea_low)):
                pool.wait_ge(part_ready, 1)
                for j in range(3):
                    rows_out = edge_parts[9 * j + EA * i:9 * j + EA * (i + 1), :]
                    nc.gpsimd.dma_start(rows_out.rearrange("k e -> (k e)").rearrange("(p c) -> p c", p=P),
                                        ea_part[i][:]).then_inc(ea_out, 16)
            pool.wait_ge(ea_out, 9 * 16)

        @block.tensor
        def _(pe):
            pe.wait_ge(ident_ready, 1)
            pe.wait_ge(waug_ready, KC * 2)

            def step(s, u, q):
                v, w = u % 2, (u + 1) % 2
                if there(s + 1, NB):
                    pe.wait_ge(xn_ready, s + 2)
                    at_least(pe, xnt_ready, s)
                    for k in range(KC):
                        ins = nc.tensor.transpose(tp[w][:, k * P:(k + 1) * P], xn[w][:, k * P:(k + 1) * P], ident[:])
                    ins.then_inc(tp_ready, 1)
                if there(s, NB):
                    pe.wait_ge(xnt_ready, s + 1)
                    at_least(pe, rest_ready, s - 1)
                    for k in range(KC):
                        ins = nc.tensor.matmul(gp[v][:, 0:GW], xnt[v][:, k, :], waug[:, k, :],
                                               start=(k == 0), stop=(k == KC - 1))
                    ins.then_inc(gp_ready, 1)

            steps(pe, step)

        @block.vector
        def _(dve):
            dve.wait_ge(weights_in, 16 * (KC + 2))
            for s in range(2):
                for k in range(KC):
                    nc.vector.tensor_tensor(prod[:, k, :], waug[:, k, 0:HD], arep[:, s, :],
                                            ALU.mult).then_inc(prod_ready, 1)
                dve.wait_ge(prod_ready, KC * (s + 1))
                for k in range(KC):
                    nc.vector.tensor_reduce(waug[:, k, HD + s * H:HD + (s + 1) * H],
                                            prod[:, k, :].rearrange("p (h d) -> p h d", d=D),
                                            AX.X, ALU.add).then_inc(waug_ready, 1)
                dve.wait_ge(waug_ready, KC * (s + 1))

            def step(s, u, q):
                v, w = u % 2, (u + 1) % 2
                if isinstance(s, int) and s == 5:
                    dve.wait_ge(ea_high, 1)
                    nc.vector.tensor_tensor(ea_rest[:], ea[:], ea_part[0][:], ALU.subtract).then_inc(ea_rest_ready, 1)
                if isinstance(s, int) and s == 7:
                    dve.wait_ge(ea_rest_ready, 1)
                    dve.wait_ge(ea_middle, 1)
                    nc.vector.tensor_tensor(ea_part[2][:], ea_rest[:], ea_part[1][:], ALU.subtract).then_inc(ea_low, 1)
                if there(s + 2, NB):
                    xs = (u + 2) % 4
                    dve.wait_ge(x_in[xs], 16 * (q + (u + 2) // 4 + 1))
                    nc.vector.bn_stats(stats[v][:], x[xs][:]).then_inc(stats_ready, 1)
                if there(s + 1, NB):
                    dve.wait_ge(std_ready, s + 2)
                    if there(s + 2, NB):
                        dve.wait_ge(stats_ready, s + 3)
                    nc.vector.reciprocal(rstd[w][:], std[w][:]).then_inc(rstd_ready, 1)
                if there(s + 2, NB):
                    if isinstance(s, int):
                        dve.wait_ge(stats_ready, s + 3)
                    nc.vector.bn_aggr(mv[v][:], stats[v][:]).then_inc(mv_ready, 1)
                if there(s + 1, NB):
                    dve.wait_ge(rstd_ready, s + 2)
                    at_least(dve, tp_ready, s)
                    xs = (u + 1) % 4
                    nc.vector.tensor_scalar(xn[w][:], x[xs][:], mv[w][:, 0:1], rstd[w][:], ALU.subtract,
                                            ALU.mult).then_inc(xn_ready, 1)
                if there(s + 2, NB):
                    dve.wait_ge(mv_ready, s + 3)
                    at_least(dve, std_ready, s + 1)
                    nc.vector.tensor_scalar_add(veps[v][:], mv[v][:, 1:2], EPS).then_inc(var_ready, 1)
                if there(s - 1, NB):
                    dve.wait_ge(srow_ready, s)
                    at_least(dve, lo_ready, s - 2)
                    nc.vector.tensor_tensor(rest[w][:], gp[w][:, 0:VD], drow[(u - 1) % 4][:, 0, :],
                                            ALU.subtract).then_inc(rest_ready, 1)
                if there(s - 2, NB):
                    dve.wait_ge(mid_ready, s - 1)
                    nc.vector.tensor_tensor(drow[(u - 2) % 4][:, 2, :], rest[v][:], drow[(u - 2) % 4][:, 1, :],
                                            ALU.subtract).then_inc(lo_ready, 1)

            steps(dve, step)

        @block.scalar
        def _(act):
            def step(s, u, q):
                v, w4 = (u + 1) % 2, (u - 1) % 4
                if isinstance(s, int) and s == 4:
                    act.wait_ge(ea_in, 16)
                    nc.scalar.copy(ea_part[0][:], ea[:]).then_inc(ea_high, 1)
                if isinstance(s, int) and s == 6:
                    act.wait_ge(ea_rest_ready, 1)
                    nc.scalar.copy(ea_part[1][:], ea_rest[:]).then_inc(ea_middle, 1)
                if there(s - 1, NB):
                    act.wait_ge(gp_ready, s)
                    at_least(act, drow_out[w4], 16 * (q + (u - 1) // 4))
                    at_least(act, srow_out[w4], 16 * (q + (u - 1) // 4))
                    nc.scalar.copy(drow[w4][:, 0, :], gp[v][:, 0:VD])
                    nc.scalar.copy(srow[w4][:, :, 0:D], gp[v][:, 0:HD].rearrange("p (h d) -> p h d", d=D))
                    nc.scalar.copy(srow[w4][:, :, D], gp[v][:, VD:VD + H]).then_inc(srow_ready, 1)
                if there(s + 1, NB):
                    act.wait_ge(tp_ready, s + 2)
                    at_least(act, gp_ready, s)
                    nc.scalar.copy(xnt[v][:], tp[v][:, 0:IN].rearrange("p (k t) -> p k t", k=KC)).then_inc(
                        xnt_ready, 1)
                if there(s + 2, NB):
                    act.wait_ge(var_ready, s + 3)
                    at_least(act, rstd_ready, s + 1)
                    nc.scalar.activation(std[u % 2][:], veps[u % 2][:], ACT.Sqrt).then_inc(std_ready, 1)
                if there(s - 1, NB):
                    act.wait_ge(rest_ready, s)
                    nc.scalar.copy(drow[w4][:, 1, :], rest[v][:]).then_inc(mid_ready, 1)

            steps(act, step)


def setup_phase(nc, ident, tables, dst_heads, dst_chunks, dst_ext, edge_w_t, edge_b, edge_gaps):
    item_edge, item_block, neg_node, wparts = tables
    HALF = NITEM // 2
    with ExitStack() as ctx:
        m = Space(nc, ctx, "s_")
        heads_i = m.sb("heads_i", [P, NCHUNK], I32)
        heads = m.sb("heads", [P, NCHUNK])
        below = m.sb("below", [P, NCHUNK])
        thr_i = m.sb("thr_i", [P, 1], I32)
        thr = m.sb("thr", [P, 1])
        part_i = m.sb("part_i", [P, 1], I32)
        part = m.sb("part", [P, 1])
        num_i = m.sb("num_i", [P, NITEM], I32)
        num = m.sb("num", [P, NITEM])
        chunk = m.sb("chunk", [P, 1])
        chunk_i = m.sb("chunk_i", [P, 1], I32)
        rows_i = m.sb("rows_i", [P, P], I32)
        rows = m.sb("rows", [P, P])
        inside = m.sb("inside", [P, 1])
        first = m.sb("first", [P, 1])
        shifted = m.sb("shifted", [P, P])
        diff = m.sb("diff", [P, P])
        upto = m.sb("upto", [P, P])
        count = m.sb("count", [P, 1], I32)
        items_i = m.sb("items_i", [P, 1], I32)
        items = m.sb("items", [P, 1])
        ends = m.sb("ends", [P, 1])
        begins = m.sb("begins", [P, 1])
        base = m.sb("base", [P, 1])
        ones = m.sb("ones", [P, P])
        base_rep = m.sb("base_rep", [P, P])
        past = m.sb("past", [P, NITEM])
        at = m.sb("at", [P, NITEM])
        blk = m.sb("blk", [P, NITEM])
        edge = m.sb("edge", [P, NITEM])
        dst_here = m.sb("dst_here", [P, NCHUNK], I32)
        dst_next = m.sb("dst_next", [P, NCHUNK], I32)
        gap = m.sb("gap", [P, NCHUNK])
        wf = m.sb("wf", [KE, HD])
        wrest = m.sb("wrest", [KE, HD])
        wpart = [m.sb(f"wpart{i}", [KE, HD], BF16) for i in range(3)]
        ps_small = m.ps("ps_small", [P, 512])
        ps_edge = [m.ps(f"ps_edge{i}", [P, 512]) for i in range(2)]
        ps_blk = [m.ps(f"ps_blk{i}", [P, 512]) for i in range(2)]

        heads_in = m.sem("heads_in")
        rows_in = m.sem("rows_in")
        dst_in = m.sem("dst_in")
        diff_ready = m.sem("diff_ready")
        gap_ready = m.sem("gap_ready")
        gap_out = m.sem("gap_out")
        w_in = m.sem("w_in")
        w_cleared = m.sem("w_cleared")
        w_out = m.sem("w_out")
        const_ready = m.sem("const_ready")
        cleared = m.sem("cleared")
        step = m.sem("step")
        chunk_ready = m.sem("chunk_ready")
        first_ready = m.sem("first_ready")
        count_ready = m.sem("count_ready")
        items_ready = m.sem("items_ready")
        ends_ready = m.sem("ends_ready")
        at_ready = m.sem("at_ready")
        spread = m.sem("spread")
        w_high, w_rest_ready, w_middle, w_low = (
            m.sem("w_high"), m.sem("w_rest_ready"), m.sem("w_middle"), m.sem("w_low"))
        block = ctx.enter_context(nc.Block())

        @block.sync
        def _(sp):
            sp.dma_start(heads_i[:], dst_heads.to_broadcast([P, NCHUNK])).then_inc(heads_in, 16)
            for side, start in ((dst_here, 0), (dst_next, 1)):
                sp.dma_start(side[:], dst_ext[start:start + EP].rearrange("(p c) -> p c", p=P)).then_inc(dst_in, 16)
            sp.wait_ge(w_cleared, 2)
            for g in range(9):
                sp.dma_start(wf[EA * g:EA * (g + 1), :], edge_w_t).then_inc(w_in, 16)
            for j in range(3):
                sp.dma_start(wf[32 + j:33 + j, :], edge_b).then_inc(w_in, 16)
            sp.wait_ge(w_low, 1)
            for j in range(3):
                sp.dma_start(wparts[9 * j:9 * j + 9, :], wpart[j][9 * j:9 * j + 9, :]).then_inc(w_out, 16)
                sp.dma_start(wparts[32 + j:33 + j, :], wpart[j][32 + j:33 + j, :]).then_inc(w_out, 16)
            sp.wait_ge(gap_ready, 1)
            sp.dma_start(edge_gaps.rearrange("(p c) -> p c", p=P), gap[:]).then_inc(gap_out, 16)
            sp.wait_ge(w_out, 6 * 16)
            sp.wait_ge(gap_out, 16)

        @block.gpsimd
        def _(pool):
            nc.gpsimd.iota(thr_i[:], pattern=[[0, 1]], base=0, channel_multiplier=P).then_inc(const_ready, 1)
            nc.gpsimd.iota(part_i[:], pattern=[[0, 1]], base=0, channel_multiplier=1).then_inc(const_ready, 1)
            nc.gpsimd.iota(num_i[:], pattern=[[1, NITEM]], base=0, channel_multiplier=0).then_inc(const_ready, 1)
            nc.gpsimd.memset(ones[:], 1.0).then_inc(cleared, 1)
            nc.gpsimd.memset(shifted[:], 0.0).then_inc(cleared, 1)
            pool.wait_ge(cleared, 2)
            nc.gpsimd.affine_select(out=shifted[:], in_=shifted[:], compare_op=ALU.not_equal, fill=1.0, base=-1,
                                    pattern=[[-1, P]], channel_multiplier=1).then_inc(const_ready, 1)
            nc.gpsimd.affine_select(out=upto[:], in_=ones[:], compare_op=ALU.is_ge, fill=0.0, base=0,
                                    pattern=[[1, P]], channel_multiplier=-1).then_inc(const_ready, 1)
            pool.wait_ge(chunk_ready, 1)
            nc.gpsimd.indirect_dma_start(out=rows_i[:], out_offset=None, in_=dst_chunks,
                                         in_offset=bass.IndirectOffsetOnAxis(ap=chunk_i[:, 0:1], axis=0)
                                         ).then_inc(rows_in, 16)
            pool.wait_ge(rows_in, 16)

        @block.tensor
        def _(pe):
            pe.wait_ge(first_ready, 2)
            nc.tensor.matmul(ps_small[:, 0:1], diff[:], first[:], start=True, stop=True).then_inc(count_ready, 1)
            pe.wait_ge(items_ready, 1)
            nc.tensor.matmul(ps_small[0:NB, 1:2], upto[0:NB, 0:NB], items[0:NB, :], start=True,
                             stop=True).then_inc(ends_ready, 1)
            pe.wait_ge(at_ready, 1)
            for i in range(2):
                cols = slice(HALF * i, HALF * (i + 1))
                nc.tensor.matmul(ps_edge[i][:, 0:HALF], base_rep[0:NB, :], at[0:NB, cols], start=True, stop=True)
                ins = nc.tensor.matmul(ps_blk[i][:, 0:HALF], ones[0:NB, :], past[0:NB, cols], start=True, stop=True)
            ins.then_inc(spread, 1)

        @block.vector
        def _(dve):
            done = [0]

            def link(ins):
                done[0] += 1
                ins.then_inc(step, 1)
                dve.wait_ge(step, done[0])

            v = nc.vector
            v.memset(wf[:], 0.0).then_inc(w_cleared, 1)
            v.memset(wparts[:], 0.0).then_inc(w_cleared, 1)
            dve.wait_ge(const_ready, 5)
            v.tensor_copy(thr[:], thr_i[:])
            v.tensor_copy(part[:], part_i[:])
            v.tensor_copy(num[:], num_i[:])
            dve.wait_ge(heads_in, 16)
            link(v.tensor_copy(heads[:], heads_i[:]))
            link(v.tensor_scalar(below[:], heads[:], thr[:], None, ALU.is_lt))
            link(v.tensor_reduce(chunk[:], below[:], AX.X, ALU.add))
            link(v.tensor_scalar(chunk[:], chunk[:], -1.0, 0.0, ALU.add, ALU.max))
            v.tensor_copy(chunk_i[:], chunk[:]).then_inc(chunk_ready, 1)
            dve.wait_ge(rows_in, 16)
            link(v.tensor_copy(rows[:], rows_i[:]))
            link(v.tensor_scalar(rows[:], rows[:], thr[:], None, ALU.is_lt))
            link(v.tensor_reduce(inside[:], rows[:], AX.X, ALU.add))
            v.scalar_tensor_tensor(out=first[:], in0=chunk[:], scalar=float(P), in1=inside[:], op0=ALU.mult,
                                   op1=ALU.add).then_inc(first_ready, 1)
            v.tensor_tensor(diff[:], shifted[:], ident[:], ALU.subtract).then_inc(first_ready, 1)
            dve.wait_ge(count_ready, 1)
            link(v.tensor_scalar(count[:], ps_small[:, 0:1], float(IE - 1), None, ALU.add))
            link(v.tensor_scalar(items_i[:], count[:], IE.bit_length() - 1, None, ALU.logical_shift_right))
            link(v.tensor_copy(items[:], items_i[:]))
            dve.sem_inc(items_ready, 1)
            dve.wait_ge(ends_ready, 1)
            dve.wait_ge(first_ready, 2)
            link(v.tensor_copy(ends[0:NB, :], ps_small[0:NB, 1:2]))
            link(v.tensor_tensor(begins[0:NB, :], ends[0:NB, :], items[0:NB, :], ALU.subtract))
            link(v.scalar_tensor_tensor(out=base[0:NB, :], in0=begins[0:NB, :], scalar=-float(IE),
                                        in1=first[0:NB, :], op0=ALU.mult, op1=ALU.add))
            link(v.tensor_scalar(base_rep[0:NB, :], ones[0:NB, :], base[0:NB, :], None, ALU.mult))
            link(v.tensor_scalar(past[0:NB, :], num[0:NB, :], ends[0:NB, :], None, ALU.is_ge))
            link(v.tensor_scalar(at[0:NB, :], num[0:NB, :], begins[0:NB, :], None, ALU.is_ge))
            v.tensor_tensor(at[0:NB, :], at[0:NB, :], past[0:NB, :], ALU.subtract).then_inc(at_ready, 1)
            dve.wait_ge(spread, 1)
            for i in range(2):
                cols = slice(HALF * i, HALF * (i + 1))
                link(v.scalar_tensor_tensor(out=edge[:, cols], in0=num[:, cols], scalar=float(IE),
                                            in1=ps_edge[i][:, 0:HALF], op0=ALU.mult, op1=ALU.add))
                link(v.tensor_scalar(blk[:, cols], ps_blk[i][:, 0:HALF], float(NB - 1), None, ALU.min))
            v.tensor_scalar(item_edge[:], edge[0:1, :], float(E), None, ALU.min)
            v.tensor_copy(item_block[:], blk[0:1, :])
            dve.wait_ge(dst_in, 32)
            v.tensor_tensor(gap[:], dst_here[:], dst_next[:], ALU.subtract).then_inc(diff_ready, 1)
            v.tensor_scalar(neg_node[:], blk[:], -float(P), part[:], ALU.mult, ALU.subtract)

            dve.wait_ge(w_high, 1)
            v.tensor_tensor(wrest[:], wf[:], wpart[0][:], ALU.subtract).then_inc(w_rest_ready, 1)
            dve.wait_ge(w_rest_ready, 1)
            dve.wait_ge(w_middle, 1)
            v.tensor_tensor(wpart[2][:], wrest[:], wpart[1][:], ALU.subtract).then_inc(w_low, 1)

        @block.scalar
        def _(act):
            act.wait_ge(w_in, 16 * 12)
            nc.scalar.copy(wpart[0][:], wf[:]).then_inc(w_high, 1)
            act.wait_ge(w_rest_ready, 1)
            nc.scalar.copy(wpart[1][:], wrest[:]).then_inc(w_middle, 1)
            act.wait_ge(diff_ready, 1)
            nc.scalar.mul(gap[:], gap[:], BIG).then_inc(gap_ready, 1)


def edge_phase(nc, ident, tables, acc, edge_ends, dst_ext, edge_gaps, edge_parts, src_table, dst_table):
    item_edge, item_block, neg_node, wparts = tables
    PR = BATCH * H
    FH = 2 * HD
    NHALF = T // 2
    with ExitStack() as ctx:
        m = Space(nc, ctx, "e_")
        ends = [m.sb(f"ends{u}", [P, T, 3], I32) for u in range(RING)]
        rows = [m.sb(f"rows{u}", [P, T, H, DG]) for u in range(RING)]
        onehot_t = [m.sb(f"onehot_t{u}", [P, BATCH, G, P], BF16) for u in range(RING)]
        alpha = [m.sb(f"alpha{u}", [P, G, BATCH, H]) for u in range(RING)]
        fact = [m.sb(f"fact{u}", [P, BATCH, H]) for u in range(RING)]
        dst_row = [m.sb(f"dst_row{j}", [P, IE], I32) for j in range(BATCH)]
        parts = [m.sb(f"parts{j}", [P, 3, VD], BF16) for j in range(BATCH)]
        ea = [m.sb(f"ea{j}", [KE, IE], BF16) for j in range(BATCH)]
        distance = m.sb("distance", [P, IE])
        onehot = [[m.sb(f"onehot{v}_{j}", [P, G, P]) for j in range(BATCH)] for v in range(2)]
        enc = [m.sb(f"enc{v}", [P, FH]) for v in range(2)]
        prod = [m.sb(f"prod{v}", [P, FH]) for v in range(2)]
        red = m.sb("red", [P, T, H])
        score = m.sb("score", [P, T, H])
        gap = m.sb("gap", [PR, IE])
        seq_max = m.sb("seq_max", [PR, IE])
        differs = m.sb("differs", [P, BATCH, G])
        final_edge = m.sb("final_edge", [P, G])
        last_max = m.sb("last_max", [P, BATCH, G, DG_MAX])
        absent = m.sb("absent", [P, BATCH])
        node_max = m.sb("node_max", [P, NB * H])
        new_max = m.sb("new_max", [P, BATCH, H])
        grown = m.sb("grown", [P, BATCH, H])
        max_rest = m.sb("max_rest", [P, BATCH * H])
        max_parts = m.sb("max_parts", [P, 3, BATCH * H], BF16)
        ident_b = m.sb("ident_b", [P, P], BF16)

        ps_enc = [m.ps(f"ps_enc{v}", [P, 512]) for v in range(2)]
        ps_dst = [m.ps(f"ps_dst{v}", [P, 512]) for v in range(2)]
        ps_seq = m.ps("ps_seq", [P, 512])
        ps_node = m.ps("ps_node", [P, 512])
        ps_back = ps_node[:, 0:G * PR].rearrange("p (g j h) -> p g j h", g=G, j=BATCH)
        ps_last = ps_node[:, 128:128 + BATCH * DG_MAX].rearrange("p (j h) -> p j h", j=BATCH)
        ps_ref = ps_node[:, 256:256 + T * H].rearrange("p (t h) -> p t h", t=T)
        ps_sum = m.ps("ps_sum", [P, 512])
        ps_shared = m.ps("ps_shared", [P, 512])
        ps_onehot = ps_shared[:, 0:G * P // 2].bitcast(BF16).rearrange("p (g n) -> p g n", g=G)
        ps_score = ps_shared[:, 384:384 + T * H].rearrange("p (t h) -> p t h", t=T)

        s = m.sem
        ones_ready, idb_ready, cleared = s("ones_ready"), s("idb_ready"), s("cleared")
        rows_free, turns, turns_pe = s("rows_free"), s("turns"), s("turns_pe")
        ends_in = [s(f"ends_in{u}") for u in range(RING)]
        gathered = [s(f"gathered{u}") for u in range(RING)]
        dst_row_in = [s(f"dst_row_in{j}") for j in range(BATCH)]
        parts_in = [s(f"parts_in{j}") for j in range(BATCH)]
        gap_in = s("gap_in")
        distance_ready, onehot_t_ready = s("distance_ready"), s("onehot_t_ready")
        enc_ready, relu_ready, dst_ready, prod_ready, red_ready = (
            s("enc_ready"), s("relu_ready"), s("dst_ready"), s("prod_ready"), s("red_ready"))
        score_ready, score1_ready, score2_ready, alpha_ready = (
            s("score_ready"), s("score1_ready"), s("score2_ready"), s("alpha_ready"))
        seq_ready, scan_ready = s("seq_ready"), s("scan_ready")
        back_ready, differs_ready, flag_ready, last_max_ready = (
            s("back_ready"), s("differs_ready"), s("flag_ready"), s("last_max_ready"))
        turned_ready, onehot_ready = s("turned_ready"), s("onehot_ready")
        last_ready, absent_ready = s("last_ready"), s("absent_ready")
        new_ready, kept_ready, grown_ready, fact_ready = (
            s("new_ready"), s("kept_ready"), s("grown_ready"), s("fact_ready"))
        hi_ready, rest_ready, mid_ready, split_ready = (
            s("hi_ready"), s("rest_ready"), s("mid_ready"), s("split_ready"))
        ref_ready, off_ready, arg_ready, exp_ready = s("ref_ready"), s("off_ready"), s("arg_ready"), s("exp_ready")
        weighted, pool_weighted, summed, scaled, added = (
            s("weighted"), s("pool_weighted"), s("summed"), s("scaled"), s("added"))
        block = ctx.enter_context(nc.Block())

        class Batch:

            def __init__(self, k, u, q, lag):
                self.k = k - lag
                self.q = 2 * q + (u - lag) // RING
                self.u = (u - lag) % RING
                self.v = (u - lag) % 2
                self.there = there(self.k, NBATCH)
                self.blocks = [None] * BATCH

        def steps(eng, step):
            def of_six(k, u, q):
                step(*(Batch(k, u, q, lag) for lag in range(-2, 4)))

            run_steps(eng, of_six, -2, 2 * RING, (NBATCH - RING) // (2 * RING) * 2 * RING, NBATCH + 3, 2 * RING)

        @block.sync
        def _(sp):
            def start(k, j):
                return sp.value_load(item_edge[0:1, bass.ds(BATCH * k + j, 1)], min_val=0, max_val=E)

            def load_ends(k, u, q):
                at_least(sp, flag_ready, k - RING + 1)
                sp.sem_inc(turns, 1)
                if not isinstance(q, int) or q > 0:
                    sp.wait_ge(gathered[u], 16 * T * q)
                sp.sem_inc(turns, 1)
                for j in range(BATCH):
                    e = start(k, j)
                    sp.dma_start(ends[u][:, G * j:G * (j + 1), :].rearrange("p g c -> p (g c)"),
                                 edge_ends[bass.ds(3 * e, 3 * IE)].rearrange("(p c) -> p c", p=P)
                                 ).then_inc(ends_in[u], 16)

            def load_dst_row(k, j):
                e = start(k, j)
                at_least(sp, distance_ready, BATCH * (k - 1) + j + 1)
                sp.dma_start(dst_row[j][:], dst_ext[bass.ds(e + 1, IE)].rearrange("(a e) -> a e", a=1)
                             .to_broadcast([P, IE])).then_inc(dst_row_in[j], 16)

            def load_item(k, j):
                e = start(k, j)
                b = sp.value_load(item_block[0:1, bass.ds(BATCH * k + j, 1)], min_val=0, max_val=NB - 1)
                at_least(sp, score_ready, BATCH * (k - 1) + j + 1)
                sp.sem_inc(turns, 1)
                sp.dma_start(ea[j][0:27, :], edge_parts[:, bass.ds(e, IE)]).then_inc(parts_in[j], 16)
                sp.dma_start(parts[j][:].rearrange("p s v -> p (s v)"),
                             dst_table[bass.ds(b * P, P), :]).then_inc(parts_in[j], 16)

            def load_gaps(k):
                at_least(sp, scan_ready, k)
                sp.sem_inc(turns, 1)
                for j in range(BATCH):
                    e = start(k, j)
                    sp.dma_start(gap[H * j:H * (j + 1), :], edge_gaps[bass.ds(e, IE)]
                                 .rearrange("(a e) -> a e", a=1).to_broadcast([H, IE])).then_inc(gap_in, 16)

            def step(later, ahead, now, before, older, oldest):
                if later.there:
                    load_dst_row(later.k, 1)
                if ahead.there:
                    load_item(ahead.k, 1)
                if later.there:
                    load_dst_row(later.k, 0)
                if now.there:
                    load_gaps(now.k)
                if later.there:
                    load_dst_row(later.k, 2)
                if ahead.there:
                    load_item(ahead.k, 2)
                if later.there:
                    load_item(later.k, 0)
                    load_ends(later.k, later.u, later.q)

            sp.wait_ge(ones_ready, BATCH)
            steps(sp, step)

        @block.gpsimd
        def _(pool):
            def gather(k, u, q, j):
                if j == 0:
                    pool.wait_ge(ends_in[u], 16 * BATCH * (q + 1))
                at_least(pool, summed, BATCH * (k - RING) + j + 1)
                pool.sem_inc(rows_free, 1)
                for g in range(G):
                    t = G * j + g
                    nc.gpsimd.indirect_dma_start(
                        out=rows[u][:, t].rearrange("p h d -> p (h d)"), out_offset=None, in_=src_table,
                        in_offset=bass.IndirectOffsetOnAxis(ap=ends[u][:, t, 0:1], axis=0)
                    ).then_inc(gathered[u], 16)

            def weigh(k, u):
                pool.wait_ge(exp_ready, k + 1)
                r = rows[u][:, T - G:T].rearrange("p g h d -> p (g h) d")
                nc.gpsimd.tensor_tensor(r[:, :, 0:D], r[:, :, 0:D], r[:, :, D:DG].to_broadcast([P, G * H, D]),
                                        ALU.mult).then_inc(pool_weighted, 1)

            def step(later, ahead, now, before, older, oldest):
                if now.there:
                    gather(now.k, now.u, now.q, 0)
                    gather(now.k, now.u, now.q, 1)
                if older.there:
                    weigh(older.k, older.u)
                if now.there:
                    gather(now.k, now.u, now.q, 2)

            steps(pool, step)

        @block.tensor
        def _(pe):
            def products(k, u, h):
                j, v = h // 2, h % 2
                if v == 0:
                    pe.wait_ge(parts_in[j], 32 * (k + 1))
                    pe.wait_ge(onehot_t_ready, BATCH * k + j + 1)
                at_least(pe, relu_ready, NHALF * k + h - 1)
                for t in range(2):
                    g = 2 * (h % 2) + t
                    ins = nc.tensor.matmul(ps_enc[v][:, t * HD:(t + 1) * HD], ea[j][:, g:IE:G], wparts[:],
                                           start=True, stop=True)
                ins.then_inc(enc_ready, 1)
                at_least(pe, prod_ready, NHALF * k + h - 1)
                for t in range(2):
                    g = 2 * (h % 2) + t
                    for part in range(3):
                        ins = nc.tensor.matmul(ps_dst[v][:, t * HD:(t + 1) * HD], onehot_t[u][:, j, g, :],
                                               parts[j][:, part, 0:HD], start=(part == 0), stop=(part == 2))
                ins.then_inc(dst_ready, 1)

            def dst_scores(k, u, j, turned):
                at_least(pe, onehot_ready, BATCH * (k - 1) + turned)
                for g in range(G):
                    for part in range(3):
                        ins = nc.tensor.matmul(ps_score[:, G * j + g, :], onehot_t[u][:, j, g, :],
                                               parts[j][:, part, HD:VD], start=(part == 0), stop=(part == 2))
                ins.then_inc(score_ready, 1)

            def to_rows(k, u):
                pe.wait_ge(alpha_ready, k + 1)
                at_least(pe, scan_ready, k)
                for g in range(G):
                    ins = nc.tensor.transpose(ps_seq[0:PR, g:IE:G], alpha[u][:, g].rearrange("p j h -> p (j h)"),
                                              ident[:])
                ins.then_inc(seq_ready, 1)

            def to_edges(k):
                pe.wait_ge(scan_ready, k + 1)
                at_least(pe, off_ready, k)
                pe.sem_inc(turns_pe, 1)
                for g in range(G):
                    ins = nc.tensor.transpose(ps_back[:, g].rearrange("p j h -> p (j h)"), seq_max[:, g:IE:G],
                                              ident[0:PR, 0:PR])
                ins.then_inc(back_ready, 1)

            def turn_onehot(k, u, j):
                at_least(pe, onehot_ready, BATCH * k + j)
                for g in range(G):
                    ins = nc.tensor.transpose(ps_onehot[:, g, :], onehot_t[u][:, j, g, :], ident_b[:])
                ins.then_inc(turned_ready, 1)

            def node_maxima(k, j, pair):
                if j == 0:
                    pe.wait_ge(last_max_ready, k + 1)
                pe.wait_ge(onehot_ready, BATCH * k + j + 1)
                for g in range(G):
                    ins = nc.tensor.matmul(ps_last[:, j, :], onehot[pair][j][:, g, :], last_max[:, j, g, :],
                                           start=(g == 0), stop=(g == G - 1))
                if j == BATCH - 1:
                    ins.then_inc(last_ready, 1)

            def references(k, u):
                pe.wait_ge(split_ready, k + 1)
                for j in range(BATCH):
                    for g in range(G):
                        for part in range(3):
                            ins = nc.tensor.matmul(ps_ref[:, G * j + g, :], onehot_t[u][:, j, g, :],
                                                   max_parts[:, part, H * j:H * (j + 1)],
                                                   start=(part == 0), stop=(part == 2))
                ins.then_inc(ref_ready, 1)

            def sums(k, u, j, pair):
                if j < BATCH - 1:
                    pe.wait_ge(weighted, (BATCH - 1) * k + j + 1)
                else:
                    pe.wait_ge(pool_weighted, k + 1)
                at_least(pe, added, BATCH * k + j)
                for g in range(G):
                    ins = nc.tensor.matmul(ps_sum[:, 0:ROW], onehot[pair][j][:, g, :],
                                           rows[u][:, G * j + g].rearrange("p h d -> p (h d)"),
                                           start=(g == 0), stop=(g == G - 1))
                ins.then_inc(summed, 1)

            def step(later, ahead, now, before, older, oldest):
                if before.there:
                    to_rows(before.k, before.u)
                    turn_onehot(before.k, before.u, 0)
                if now.there:
                    products(now.k, now.u, 1)
                    dst_scores(now.k, now.u, 0, 1)
                if before.there:
                    turn_onehot(before.k, before.u, 1)
                    to_edges(before.k)
                if now.there:
                    products(now.k, now.u, 2)
                if before.there:
                    turn_onehot(before.k, before.u, 2)
                if now.there:
                    products(now.k, now.u, 3)
                if before.there:
                    node_maxima(before.k, 0, before.v)
                    node_maxima(before.k, 1, before.v)
                    node_maxima(before.k, 2, before.v)
                if older.there:
                    sums(older.k, older.u, 0, older.v)
                if now.there:
                    dst_scores(now.k, now.u, 1, 3)
                    products(now.k, now.u, 4)
                if older.there:
                    sums(older.k, older.u, 1, older.v)
                if now.there:
                    products(now.k, now.u, 5)
                    dst_scores(now.k, now.u, 2, 3)
                if before.there:
                    references(before.k, before.u)
                if older.there:
                    sums(older.k, older.u, 2, older.v)
                if ahead.there:
                    products(ahead.k, ahead.u, 0)

            pe.wait_ge(idb_ready, 1)
            steps(pe, step)

        @block.vector
        def _(dve):
            v = nc.vector

            def multiply(k, h):
                n = NHALF * k + h
                dve.wait_ge(relu_ready, n + 1)
                dve.wait_ge(dst_ready, n + 1)
                v.tensor_tensor(prod[h % 2][:], ps_dst[h % 2][:], enc[h % 2][:], ALU.mult).then_inc(prod_ready, 1)

            def add_up(k, h):
                dve.wait_ge(prod_ready, NHALF * k + h + 1)
                if h == 0:
                    at_least(dve, score1_ready, k)
                v.tensor_reduce(red[:, 2 * h:2 * h + 2, :],
                                prod[h % 2][:].rearrange("p (t h d) -> p t h d", t=2, d=D),
                                AX.X, ALU.add).then_inc(red_ready, 1)

            def source_scores(k, u, q):
                dve.wait_ge(gathered[u], 16 * T * (q + 1))
                dve.wait_ge(red_ready, NHALF * (k + 1))
                v.tensor_tensor(score[:], rows[u][:, :, :, D], red[:], ALU.add).then_inc(score1_ready, 1)

            def destination_scores(k, u):
                dve.wait_ge(score_ready, BATCH * (k + 1))
                dve.wait_ge(score1_ready, k + 1)
                v.tensor_tensor(alpha[u][:], ps_score.rearrange("p (j g) h -> p g j h", g=G),
                                score[:].rearrange("p (j g) h -> p g j h", g=G), ALU.add).then_inc(score2_ready, 1)

            def leaky_relu(k, u):
                dve.wait_ge(score2_ready, k + 1)
                a = alpha[u][:].rearrange("p g j h -> p (g j h)")
                v.scalar_tensor_tensor(out=a, in0=a, scalar=0.2, in1=a, op0=ALU.mult,
                                       op1=ALU.max).then_inc(alpha_ready, 1)

            def scan(k):
                dve.wait_ge(seq_ready, k + 1)
                dve.wait_ge(gap_in, 16 * BATCH * (k + 1))
                v.tensor_tensor_scan(seq_max[:], gap[:], ps_seq[0:PR, :], -BIG, ALU.add, ALU.max).then_inc(scan_ready, 1)

            def compare(k, u):
                v.tensor_tensor(differs[:].rearrange("p j g -> p (j g)"), ends[u][:, :, 1], ends[u][:, :, 2],
                                ALU.not_equal).then_inc(differs_ready, 1)

            def flags(k):
                dve.wait_ge(differs_ready, k + 1)
                v.tensor_tensor(last_max[:, :, :, H], differs[:],
                                final_edge[:].rearrange("p (a g) -> p a g", a=1).to_broadcast([P, BATCH, G]),
                                ALU.max).then_inc(flag_ready, 1)

            def last_maxima(k):
                dve.wait_ge(back_ready, k + 1)
                dve.wait_ge(flag_ready, k + 1)
                v.tensor_tensor(last_max[:, :, :, 0:H], ps_back.rearrange("p g j h -> p j g h"),
                                last_max[:, :, :, H:H + 1].to_broadcast([P, BATCH, G, H]),
                                ALU.mult).then_inc(last_max_ready, 1)

            def absences(k):
                dve.wait_ge(last_ready, k + 1)
                v.tensor_scalar(absent[:], ps_last[:, :, H], BIG, -BIG, ALU.mult, ALU.add).then_inc(absent_ready, 1)

            def load_block(k, j, blocks):
                if blocks[j] is None:
                    blocks[j] = dve.value_load(item_block[0:1, bass.ds(BATCH * k + j, 1)], min_val=0, max_val=NB - 1)

            def new_maximum(k, j, blocks):
                load_block(k, j, blocks)
                here = node_max[:, bass.ds(blocks[j] * H, H)]
                n = BATCH * k + j
                if j == 0:
                    dve.wait_ge(absent_ready, k + 1)
                    at_least(dve, fact_ready, k)
                at_least(dve, kept_ready, n)
                for out, op in ((grown[:, j, :], ALU.subtract), (new_max[:, j, :], ALU.max)):
                    v.scalar_tensor_tensor(out=out, in0=ps_last[:, j, 0:H], scalar=absent[:, j:j + 1],
                                           in1=here, op0=ALU.add, op1=op).then_inc(new_ready, 1)

            def keep_maximum(k, j, blocks):
                load_block(k, j, blocks)
                here = node_max[:, bass.ds(blocks[j] * H, H)]
                dve.wait_ge(new_ready, 2 * (BATCH * k + j + 1))
                v.tensor_scalar(here, new_max[:, j, :], 0.0, None, ALU.add).then_inc(kept_ready, 1)

            flat = new_max[:].rearrange("p j h -> p (j h)")

            def high_part(k):
                dve.wait_ge(new_ready, 2 * BATCH * (k + 1))
                at_least(dve, ref_ready, k)
                v.tensor_copy(max_parts[:, 0, :], flat).then_inc(hi_ready, 1)

            def high_rest(k):
                dve.wait_ge(hi_ready, k + 1)
                v.tensor_tensor(max_rest[:], flat, max_parts[:, 0, :], ALU.subtract).then_inc(rest_ready, 1)

            def middle_part(k):
                dve.wait_ge(rest_ready, k + 1)
                v.tensor_copy(max_parts[:, 1, :], max_rest[:]).then_inc(mid_ready, 1)

            def low_part(k):
                dve.wait_ge(mid_ready, k + 1)
                v.tensor_tensor(max_parts[:, 2, :], max_rest[:], max_parts[:, 1, :],
                                ALU.subtract).then_inc(split_ready, 1)

            def below_maxima(k, u):
                dve.wait_ge(ref_ready, k + 1)
                v.tensor_tensor(alpha[u][:], ps_ref[:].rearrange("p (j g) h -> p g j h", g=G), alpha[u][:],
                                ALU.subtract).then_inc(off_ready, 1)

            def weigh(k, u, j):
                dve.wait_ge(exp_ready, k + 1)
                r = rows[u][:, G * j:G * (j + 1)].rearrange("p g h d -> p (g h) d")
                v.tensor_tensor(r[:, :, 0:D], r[:, :, 0:D], r[:, :, D:DG].to_broadcast([P, G * H, D]),
                                ALU.mult).then_inc(weighted, 1)

            def rescale(k, u, j, blocks):
                n = BATCH * k + j
                load_block(k, j, blocks)
                by_head = acc[:, bass.ds(blocks[j] * ROW, ROW)].rearrange("p (h d) -> p h d", d=DG)
                if j == 0:
                    dve.wait_ge(fact_ready, k + 1)
                at_least(dve, added, n)
                v.tensor_tensor(by_head, by_head, fact[u][:, j, :].rearrange("p (h a) -> p h a", a=1)
                                .to_broadcast([P, H, DG]), ALU.mult).then_inc(scaled, 1)

            def accumulate(k, j, blocks):
                load_block(k, j, blocks)
                here = acc[:, bass.ds(blocks[j] * ROW, ROW)]
                dve.wait_ge(scaled, BATCH * k + j + 1)
                dve.wait_ge(summed, BATCH * k + j + 1)
                v.tensor_tensor(here, here, ps_sum[:, 0:ROW], ALU.add).then_inc(added, 1)

            def step(later, ahead, now, before, older, oldest):
                if now.there:
                    multiply(now.k, 0)
                if older.there:
                    load_block(older.k, 0, older.blocks)
                if before.there:
                    scan(before.k)
                    compare(before.k, before.u)
                if now.there:
                    add_up(now.k, 0)
                if older.there:
                    rescale(older.k, older.u, 0, older.blocks)
                if before.there:
                    flags(before.k)
                    load_block(before.k, 1, before.blocks)
                if now.there:
                    multiply(now.k, 1)
                if before.there:
                    last_maxima(before.k)
                if now.there:
                    add_up(now.k, 1)
                if older.there:
                    weigh(older.k, older.u, 0)
                if before.there:
                    load_block(before.k, 0, before.blocks)
                if now.there:
                    multiply(now.k, 2)
                if older.there:
                    weigh(older.k, older.u, 1)
                if before.there:
                    load_block(before.k, 2, before.blocks)
                    absences(before.k)
                if now.there:
                    add_up(now.k, 2)
                if before.there:
                    new_maximum(before.k, 0, before.blocks)
                if now.there:
                    multiply(now.k, 3)
                if before.there:
                    keep_maximum(before.k, 0, before.blocks)
                if older.there:
                    load_block(older.k, 1, older.blocks)
                if now.there:
                    add_up(now.k, 3)
                if before.there:
                    new_maximum(before.k, 1, before.blocks)
                if older.there:
                    accumulate(older.k, 0, older.blocks)
                if before.there:
                    keep_maximum(before.k, 1, before.blocks)
                if older.there:
                    rescale(older.k, older.u, 1, older.blocks)
                if before.there:
                    new_maximum(before.k, 2, before.blocks)
                    high_part(before.k)
                if now.there:
                    multiply(now.k, 4)
                if before.there:
                    keep_maximum(before.k, 2, before.blocks)
                    high_rest(before.k)
                if now.there:
                    add_up(now.k, 4)
                if before.there:
                    middle_part(before.k)
                if older.there:
                    accumulate(older.k, 1, older.blocks)
                    load_block(older.k, 2, older.blocks)
                if before.there:
                    low_part(before.k)
                if now.there:
                    multiply(now.k, 5)
                    add_up(now.k, 5)
                if older.there:
                    rescale(older.k, older.u, 2, older.blocks)
                if now.there:
                    source_scores(now.k, now.u, now.q)
                    destination_scores(now.k, now.u)
                    leaky_relu(now.k, now.u)
                if older.there:
                    accumulate(older.k, 2, older.blocks)
                if before.there:
                    below_maxima(before.k, before.u)

            for j in range(BATCH):
                v.memset(ea[j][:], 1.0).then_inc(ones_ready, 1)
            v.tensor_copy(ident_b[:], ident[:]).then_inc(idb_ready, 1)
            v.memset(node_max[:], -BIG).then_inc(cleared, 1)
            v.memset(final_edge[:], 0.0).then_inc(cleared, 1)
            v.memset(acc[:], 0.0).then_inc(cleared, 1)
            dve.wait_ge(cleared, 3)
            v.tensor_copy(final_edge[:, G - 1:G], ident[:, P - 1:P]).then_inc(cleared, 1)
            dve.wait_ge(cleared, 4)
            steps(dve, step)

        @block.scalar
        def _(act):
            def place(k, u, j):
                n = BATCH * k + j
                act.wait_ge(dst_row_in[j], 16 * (k + 1))
                at_least(act, onehot_t_ready, n)
                nc.scalar.activation(distance[:], dst_row[j][:], ACT.Abs,
                                     bias=neg_node[:, bass.ds(n, 1)]).then_inc(distance_ready, 1)
                act.wait_ge(distance_ready, n + 1)
                if j == 0:
                    at_least(act, ref_ready, k - RING + 1)
                nc.scalar.activation(onehot_t[u][:, j], distance[:].rearrange("p (e g) -> p g e", g=G), ACT.Relu,
                                     bias=1.0, scale=-1.0).then_inc(onehot_t_ready, 1)

            def relu(k, h):
                w, n = h % 2, NHALF * k + h
                act.wait_ge(enc_ready, n + 1)
                at_least(act, prod_ready, n - 1)
                nc.scalar.activation(enc[w][:], ps_enc[w][:], ACT.Relu).then_inc(relu_ready, 1)

            def onehot_out(k, j, pair):
                n = BATCH * k + j
                act.wait_ge(turned_ready, n + 1)
                at_least(act, summed, n - 2 * BATCH + 1)
                nc.scalar.copy(onehot[pair][j][:], ps_onehot).then_inc(onehot_ready, 1)

            def growth(k, u):
                act.wait_ge(new_ready, 2 * BATCH * (k + 1))
                nc.scalar.activation(grown[:], grown[:], ACT.Relu).then_inc(grown_ready, 1)
                act.wait_ge(grown_ready, k + 1)
                at_least(act, added, BATCH * (k - RING + 1))
                nc.scalar.activation(fact[u][:], grown[:], ACT.Exp, scale=-1.0).then_inc(fact_ready, 1)

            def from_zero(k, u):
                act.wait_ge(off_ready, k + 1)
                nc.scalar.activation(alpha[u][:], alpha[u][:], ACT.Relu).then_inc(arg_ready, 1)

            def exponentials(k, u):
                act.wait_ge(arg_ready, k + 1)
                nc.scalar.activation(rows[u][:, :, :, D].rearrange("p (j g) h -> p g j h", g=G),
                                     alpha[u][:], ACT.Exp, scale=-1.0).then_inc(exp_ready, 1)

            def step(later, ahead, now, before, older, oldest):
                if older.there:
                    growth(older.k, older.u)
                    from_zero(older.k, older.u)
                if before.there:
                    onehot_out(before.k, 0, before.v)
                if older.there:
                    exponentials(older.k, older.u)
                if now.there:
                    relu(now.k, 1)
                if before.there:
                    onehot_out(before.k, 1, before.v)
                if now.there:
                    relu(now.k, 2)
                if before.there:
                    onehot_out(before.k, 2, before.v)
                if ahead.there:
                    place(ahead.k, ahead.u, 0)
                    place(ahead.k, ahead.u, 1)
                if now.there:
                    relu(now.k, 3)
                    relu(now.k, 4)
                    relu(now.k, 5)
                if ahead.there:
                    place(ahead.k, ahead.u, 2)
                    relu(ahead.k, 0)

            steps(act, step)


def combine_phase(nc, ident, acc, keep, x_pad, bias, gate_w, gate_b, token_rows):
    logits, = keep
    with ExitStack() as ctx:
        m = Space(nc, ctx, "c_")
        bias_rep = m.sb("bias_rep", [P, HD])
        gw = m.sb("gw", [P, KC, X])
        gb = m.sb("gb", [P, X])
        x = [m.sb(f"x{u}", [P, HD]) for u in range(2)]
        xb = [m.sb(f"xb{u}", [P, HD]) for u in range(2)]
        den = m.sb("den", [P, NB, H])
        gnn = [m.sb(f"gnn{u}", [P, HD]) for u in range(2)]
        stats = [m.sb(f"stats{u}", [P, 6]) for u in range(2)]
        mv = [m.sb(f"mv{u}", [P, 2]) for u in range(2)]
        veps = [m.sb(f"veps{u}", [P, 1]) for u in range(2)]
        std = [m.sb(f"std{u}", [P, 1]) for u in range(2)]
        rstd = [m.sb(f"rstd{u}", [P, 1]) for u in range(2)]
        row = [m.sb(f"row{u}", [P, 2, HD]) for u in range(4)]
        xnt = [m.sb(f"xnt{u}", [P, KC, P]) for u in range(2)]
        tp = [m.ps(f"tp{u}", [P, 512]) for u in range(2)]
        gp = [m.ps(f"gp{u}", [P, 512]) for u in range(2)]

        const_in = m.sem("const_in")
        turns = m.sem("turns")
        x_in = [m.sem(f"x_in{u}") for u in range(2)]
        row_out = [m.sem(f"row_out{u}") for u in range(4)]
        den_ready, rden_ready, gnn_ready, biased, x1_ready = (
            m.sem("den_ready"), m.sem("rden_ready"), m.sem("gnn_ready"), m.sem("biased"), m.sem("x1_ready"))
        stats_ready, mv_ready, var_ready, std_ready, rstd_ready, row_ready = (
            m.sem("stats_ready"), m.sem("mv_ready"), m.sem("var_ready"), m.sem("std_ready"),
            m.sem("rstd_ready"), m.sem("row_ready"))
        tp_ready, xnt_ready, gp_ready, logits_ready = (
            m.sem("tp_ready"), m.sem("xnt_ready"), m.sem("gp_ready"), m.sem("logits_ready"))
        block = ctx.enter_context(nc.Block())

        def steps(eng, step):
            run_steps(eng, step, -2, 8, (NB - 4) // 4 * 4, NB + 2, 4)

        @block.sync
        def _(sp):
            sp.dma_start(bias_rep[:], bias.to_broadcast([P, HD])).then_inc(const_in, 16)
            sp.dma_start(gb[:], gate_b.to_broadcast([P, X])).then_inc(const_in, 16)
            for k in range(KC):
                sp.dma_start(gw[:, k, :], gate_w[k * P:(k + 1) * P, :]).then_inc(const_in, 16)
            sp.dma_start(x[0][:], x_pad[0:P, :]).then_inc(x_in[0], 16)
            sp.dma_start(x[1][:], x_pad[P:2 * P, :]).then_inc(x_in[1], 16)

            def step(s, u, q):
                if not isinstance(s, int) or s + 4 < NB:
                    sp.wait_ge(biased, s + 3)
                    sp.dma_start(x[u % 2][:], x_pad[bass.ds((s + 4) * P, P), :]).then_inc(x_in[u % 2], 16)
                if there(s, NB):
                    sp.wait_ge(row_ready, s + 1)
                    sp.dma_start(token_rows[bass.ds(s * P, P), :],
                                 row[u][:].rearrange("p a d -> p (a d)")).then_inc(row_out[u], 16)

            steps(sp, step)
            for u in range(4):
                sp.wait_ge(row_out[u], 16 * len(range(u, NB, 4)))

        @block.gpsimd
        def _(pool):
            pool.wait_ge(const_in, 16 * (2 + KC))

            def step(s, u, q):
                w = u % 2
                if there(s + 2, NB):
                    pool.wait_ge(x_in[w], 16 * (2 * q + (u + 2) // 2 + 1))
                    at_least(pool, x1_ready, s + 1)
                    nc.gpsimd.tensor_tensor(xb[w][:], x[w][:], bias_rep[:], ALU.add).then_inc(biased, 1)

            steps(pool, step)

        @block.tensor
        def _(pe):
            pe.wait_ge(const_in, 16 * (2 + KC))

            def step(s, u, q):
                v, w = u % 2, (u - 1) % 2
                if there(s - 1, NB):
                    pe.wait_ge(xnt_ready, s)
                    at_least(pe, logits_ready, s - 2)
                    for k in range(KC):
                        ins = nc.tensor.matmul(gp[w][:, 0:X], xnt[w][:, k, :], gw[:, k, :],
                                               start=(k == 0), stop=(k == KC - 1))
                    ins.then_inc(gp_ready, 1)
                if there(s, NB):
                    pe.wait_ge(row_ready, s + 1)
                    at_least(pe, xnt_ready, s - 1)
                    for k in range(KC):
                        ins = nc.tensor.transpose(tp[v][:, k * P:(k + 1) * P], row[u][:, 0, k * P:(k + 1) * P],
                                                  ident[:])
                    ins.then_inc(tp_ready, 1)

            steps(pe, step)

        @block.vector
        def _(dve):
            v = nc.vector
            dve.wait_ge(const_in, 16 * (2 + KC))
            all_sums = acc[:].rearrange("p (b h d) -> p b h d", h=H, d=DG)
            v.tensor_scalar(den[:], all_sums[:, :, :, D], 1e-10, None, ALU.max).then_inc(den_ready, 1)
            dve.wait_ge(den_ready, 1)
            v.reciprocal(den[:], den[:]).then_inc(rden_ready, 1)
            dve.wait_ge(rden_ready, 1)

            def step(s, u, q):
                even, odd, new = u % 2, (u + 1) % 2, (u + 2) % 4
                coming, middle, now = there(s + 2, NB), there(s + 1, NB), there(s, NB)
                if coming:
                    sums = acc[:, bass.ds((s + 2) * ROW, ROW)].rearrange("p (h d) -> p h d", d=DG)
                    at_least(dve, x1_ready, s + 1)
                    v.tensor_tensor(gnn[even][:].rearrange("p (h d) -> p h d", d=D), sums[:, :, 0:D],
                                    den[:].rearrange("p b h -> p (b h)")[:, bass.ds((s + 2) * H, H)]
                                    .rearrange("p (h a) -> p h a", a=1).to_broadcast([P, H, D]),
                                    ALU.mult).then_inc(gnn_ready, 1)
                if middle:
                    dve.wait_ge(stats_ready, s + 2)
                    at_least(dve, row_ready, s)
                    dve.sem_inc(turns, 1)
                    v.bn_aggr(mv[odd][:], stats[odd][:]).then_inc(mv_ready, 1)
                if coming:
                    at_least(dve, row_out[new], 16 * (q + (u + 2) // 4))
                    at_least(dve, tp_ready, s - 1)
                    dve.wait_ge(biased, s + 3)
                    dve.wait_ge(gnn_ready, s + 3)
                    v.tensor_tensor(row[new][:, 1, :], gnn[even][:], xb[even][:], ALU.add).then_inc(x1_ready, 1)
                if middle:
                    dve.wait_ge(mv_ready, s + 2)
                    at_least(dve, std_ready, s)
                    v.tensor_scalar_add(veps[odd][:], mv[odd][:, 1:2], EPS).then_inc(var_ready, 1)
                if now:
                    dve.wait_ge(std_ready, s + 1)
                    v.reciprocal(rstd[even][:], std[even][:]).then_inc(rstd_ready, 1)
                if coming:
                    dve.wait_ge(x1_ready, s + 3)
                    v.bn_stats(stats[even][:], row[new][:, 1, :]).then_inc(stats_ready, 1)
                if now:
                    dve.wait_ge(rstd_ready, s + 1)
                    v.tensor_scalar(row[u][:, 0, :], row[u][:, 1, :], mv[even][:, 0:1], rstd[even][:], ALU.subtract,
                                    ALU.mult).then_inc(row_ready, 1)
                if there(s - 2, NB):
                    dve.wait_ge(gp_ready, s - 1)
                    v.tensor_tensor(logits[:, bass.ds((s - 2) * X, X)], gp[even][:, 0:X], gb[:],
                                    ALU.add).then_inc(logits_ready, 1)

            steps(dve, step)

        @block.scalar
        def _(act):
            def step(s, u, q):
                w, o = (u + 1) % 2, u % 2
                if there(s + 1, NB):
                    act.wait_ge(var_ready, s + 2)
                    at_least(act, rstd_ready, s)
                    nc.scalar.activation(std[w][:], veps[w][:], ACT.Sqrt).then_inc(std_ready, 1)
                if there(s, NB):
                    act.wait_ge(tp_ready, s + 1)
                    at_least(act, gp_ready, s - 1)
                    nc.scalar.copy(xnt[o][:], tp[o][:, 0:HD].rearrange("p (k t) -> p k t", k=KC)).then_inc(
                        xnt_ready, 1)

            steps(act, step)


def route_phase(nc, keep, tables, slots, weights, weights_dram, token_rows):
    logits, = keep
    tile_expert, = tables
    w1s, w2s, b1r, b2r = weights
    w1, w2, b1, b2 = weights_dram
    NX = NB * X
    with ExitStack() as ctx:
        m = Space(nc, ctx, "r_")
        top = m.sb("top", [P, NB])
        shift = m.sb("shift", [P, NB, X])
        expo = m.sb("expo", [P, NB, X])
        total = m.sb("total", [P, NB])
        ptop = m.sb("ptop", [P, NB])
        rank = shift
        rank_i = m.sb("rank_i", [P, X], I32)
        rank_f = m.sb("rank_f", [P, X])
        best = m.sb("best", [P, NB])
        hot = m.sb("hot", [P, NB, X])
        hot_b = m.sb("hot_b", [P, NB, X], BF16)
        node_i = m.sb("node_i", [P, NB], I32)
        node = m.sb("node", [P, NB])
        real = m.sb("real", [P, NB])
        ones_b = m.sb("ones_b", [P, P], BF16)
        before_b = m.sb("before_b", [P, P], BF16)
        part_i = m.sb("part_i", [P, 1], I32)
        part = m.sb("part", [P, 1])
        zeros = m.sb("zeros", [P, NB])
        tile_total = m.sb("tile_total", [P, X, NB])
        running = m.sb("running", [P, X, NB])
        pos = expo
        mine = shift
        position = m.sb("position", [P, NB])
        kept = m.sb("kept", [P, NB])
        tiles_i = m.sb("tiles_i", [P, X], I32)
        tiles = m.sb("tiles", [P, X])
        tile_end = m.sb("tile_end", [P, X])
        slot_base = m.sb("slot_base", [P, X])
        base = m.sb("base", [P, NB])
        slot_f = m.sb("slot_f", [P, NB])
        unreal = m.sb("unreal", [P, NB])
        dump = m.sb("dump", [P, 1])
        slot_i = m.sb("slot_i", [P, NB], I32)
        entry = m.sb("entry", [P, NB, 2])
        num_i = m.sb("num_i", [1, NT], I32)
        num = m.sb("num", [1, NT])
        expert = m.sb("expert", [1, NT])
        past = m.sb("past", [1, NT])
        empty = m.sb("empty", [P, NT + 1, 2])
        blank = m.sb("blank", [P, 2 * HD])
        ps_in = [m.ps(f"ps_in{i}", [P, 512]) for i in range(2)]
        ps_all = [m.ps(f"ps_all{i}", [P, 512]) for i in range(2)]

        const_ready = m.sem("const_ready")
        cleared = m.sem("cleared")
        step = m.sem("step")
        hot_ready = m.sem("hot_ready")
        counted = m.sem("counted")
        shift_ready = m.sem("shift_ready")
        exp_ready = m.sem("exp_ready")
        empty_ready = m.sem("empty_ready")
        empty_out = m.sem("empty_out")
        weights_in = m.sem("weights_in")
        entry_ready = m.sem("entry_ready")
        slots_out = m.sem("slots_out")
        block = ctx.enter_context(nc.Block())
        HALF = NX // 2
        FC = F // P

        @block.sync
        def _(sp):
            sp.wait_ge(empty_ready, 2)
            sp.dma_start(slots.rearrange("(t p) c -> p t c", p=P), empty[:]).then_inc(empty_out, 16)
            sp.dma_start(token_rows[NPAD:NPAD + P, :], blank[:]).then_inc(empty_out, 16)
            for x in range(X):
                sp.dma_start(w1s[:, x * KC * F:(x + 1) * KC * F].rearrange("p (k f) -> p k f", k=KC),
                             w1[x].rearrange("(k p) f -> p k f", p=P)).then_inc(weights_in, 16)
                sp.dma_start(w2s[:, x * FC * HD:(x + 1) * FC * HD].rearrange("p (c d) -> p c d", c=FC),
                             w2[x].rearrange("(c p) d -> p c d", p=P)).then_inc(weights_in, 16)
            sp.dma_start(b1r[:], b1.to_broadcast([P, X * F])).then_inc(weights_in, 16)
            sp.dma_start(b2r[:], b2.to_broadcast([P, X * HD])).then_inc(weights_in, 16)
            sp.wait_ge(empty_out, 32)
            sp.wait_ge(weights_in, 16 * (2 * X + 2))

        @block.gpsimd
        def _(pool):
            g = nc.gpsimd
            g.iota(node_i[:], pattern=[[P, NB]], base=0, channel_multiplier=1).then_inc(const_ready, 1)
            g.iota(rank_i[:], pattern=[[-1, X]], base=X, channel_multiplier=0).then_inc(const_ready, 1)
            g.iota(part_i[:], pattern=[[0, 1]], base=0, channel_multiplier=1).then_inc(const_ready, 1)
            g.iota(num_i[:], pattern=[[1, NT]], base=0, channel_multiplier=0).then_inc(const_ready, 1)
            g.memset(ones_b[:], 1.0).then_inc(cleared, 1)
            g.memset(zeros[:], 0.0).then_inc(const_ready, 1)
            pool.wait_ge(cleared, 1)
            g.affine_select(out=before_b[:], in_=ones_b[:], compare_op=ALU.is_gt, fill=0.0, base=0,
                            pattern=[[1, P]], channel_multiplier=-1).then_inc(const_ready, 1)
            pool.wait_ge(entry_ready, 1)
            pool.wait_ge(empty_out, 32)
            for b in range(NB):
                g.indirect_dma_start(out=slots, out_offset=bass.IndirectOffsetOnAxis(ap=slot_i[:, b:b + 1], axis=0),
                                     in_=entry[:, b, :], in_offset=None).then_inc(slots_out, 16)
            pool.wait_ge(slots_out, 16 * NB)

        @block.tensor
        def _(pe):
            pe.wait_ge(const_ready, 6)
            pe.wait_ge(hot_ready, 1)
            flat = hot_b[:].rearrange("p b x -> p (b x)")
            for i in range(2):
                nc.tensor.matmul(ps_in[i][:, 0:HALF], before_b[:], flat[:, HALF * i:HALF * (i + 1)],
                                 start=True, stop=True)
                ins = nc.tensor.matmul(ps_all[i][:, 0:HALF], ones_b[:], flat[:, HALF * i:HALF * (i + 1)],
                                       start=True, stop=True)
            ins.then_inc(counted, 1)

        @block.scalar
        def _(act):
            act.wait_ge(shift_ready, 1)
            nc.scalar.activation(expo[:], shift[:], ACT.Exp).then_inc(exp_ready, 1)

        @block.vector
        def _(dve):
            v = nc.vector
            done = [0]

            def link(ins):
                done[0] += 1
                ins.then_inc(step, 1)
                dve.wait_ge(step, done[0])

            def over_x(ap):
                return ap[:].rearrange("p (b a) -> p b a", a=1).to_broadcast([P, NB, X])

            def over_b(ap):
                return ap[:].rearrange("p (a x) -> p a x", a=1).to_broadcast([P, NB, X])

            dve.wait_ge(const_ready, 6)
            v.tensor_copy(node[:], node_i[:])
            v.tensor_copy(rank_f[:], rank_i[:])
            link(v.tensor_copy(part[:], part_i[:]))
            link(v.tensor_scalar(dump[:], part[:], float(DUMP), None, ALU.add))
            link(v.memset(empty[:], 0.0))
            v.memset(blank[:], 0.0).then_inc(empty_ready, 1)
            v.tensor_scalar(empty[:, :, 0], empty[:, :, 0], dump[:], None, ALU.add).then_inc(empty_ready, 1)
            lg = logits[:].rearrange("p (b x) -> p b x", x=X)
            link(v.tensor_reduce(top[:], lg, AX.X, ALU.max))
            v.tensor_tensor(shift[:], lg, over_x(top), ALU.subtract).then_inc(shift_ready, 1)
            dve.wait_ge(exp_ready, 1)
            link(v.tensor_reduce(total[:], expo[:], AX.X, ALU.add))
            link(v.reciprocal(total[:], total[:]))
            link(v.tensor_tensor(expo[:], expo[:], over_x(total), ALU.mult))
            link(v.tensor_reduce(ptop[:], expo[:], AX.X, ALU.max))
            link(v.tensor_tensor(hot[:], expo[:], over_x(ptop), ALU.is_equal))
            link(v.tensor_tensor(rank[:], hot[:], over_b(rank_f), ALU.mult))
            link(v.tensor_reduce(best[:], rank[:], AX.X, ALU.max))
            link(v.tensor_scalar(real[:], node[:], float(N), None, ALU.is_lt))
            link(v.tensor_tensor(hot[:], over_b(rank_f), over_x(best), ALU.is_equal))
            link(v.tensor_tensor(hot[:], hot[:], over_x(real), ALU.mult))
            v.tensor_copy(hot_b[:], hot[:]).then_inc(hot_ready, 1)
            dve.wait_ge(counted, 1)
            for i in range(2):
                half = slice(NB // 2 * i, NB // 2 * (i + 1))
                link(v.tensor_copy(tile_total[:, :, half].rearrange("p x b -> p b x"),
                                   ps_all[i][:, 0:HALF].rearrange("p (b x) -> p b x", x=X)))
            for x in range(X):
                link(v.tensor_tensor_scan(running[:, x, :], tile_total[:, x, :], zeros[:], 0.0, ALU.add, ALU.add))
            link(v.tensor_scalar(tiles_i[:], running[:, :, NB - 1], float(P - 1), None, ALU.add))
            link(v.tensor_scalar(tiles_i[:], tiles_i[:], P.bit_length() - 1, None, ALU.logical_shift_right))
            link(v.tensor_copy(tiles[:], tiles_i[:]))
            link(v.tensor_tensor_scan(tile_end[:], tiles[:], zeros[:, 0:X], 0.0, ALU.add, ALU.add))
            link(v.tensor_tensor(slot_base[:], tile_end[:], tiles[:], ALU.subtract))
            link(v.tensor_scalar(slot_base[:], slot_base[:], float(P), None, ALU.mult))
            link(v.tensor_tensor(running[:], running[:], tile_total[:], ALU.subtract))
            for i in range(2):
                half = slice(NB // 2 * i, NB // 2 * (i + 1))
                link(v.tensor_tensor(pos[:, half, :], ps_in[i][:, 0:HALF].rearrange("p (b x) -> p b x", x=X),
                                     running[:, :, half].rearrange("p x b -> p b x"), ALU.add))
            link(v.tensor_tensor(mine[:], pos[:], hot[:], ALU.mult))
            link(v.tensor_reduce(position[:], mine[:], AX.X, ALU.add))
            link(v.tensor_scalar(kept[:], position[:], float(CAP), None, ALU.is_lt))
            link(v.tensor_tensor(entry[:, :, 1], ptop[:], kept[:], ALU.mult))
            link(v.tensor_copy(entry[:, :, 0], node[:]))
            link(v.tensor_tensor(mine[:], hot[:], over_b(slot_base), ALU.mult))
            link(v.tensor_reduce(base[:], mine[:], AX.X, ALU.add))
            link(v.tensor_tensor(slot_f[:], position[:], base[:], ALU.add))
            link(v.tensor_scalar(unreal[:], real[:], -1.0, 1.0, ALU.mult, ALU.add))
            link(v.tensor_scalar(dump[:], part[:], float(NT * P), None, ALU.add))
            link(v.tensor_scalar(unreal[:], unreal[:], dump[:], None, ALU.mult))
            link(v.tensor_tensor(slot_f[:], slot_f[:], unreal[:], ALU.add))
            v.tensor_copy(slot_i[:], slot_f[:]).then_inc(entry_ready, 1)
            link(v.tensor_copy(num[:], num_i[:]))
            link(v.tensor_scalar(expert[:], num[:], tile_end[0:1, 0:1], None, ALU.is_ge))
            for x in range(1, X - 1):
                link(v.tensor_scalar(past[:], num[:], tile_end[0:1, x:x + 1], None, ALU.is_ge))
                link(v.tensor_tensor(expert[:], expert[:], past[:], ALU.add))
            link(v.tensor_copy(tile_expert[:], expert[:]))


def expert_phase(nc, ident, tables, weights, slots, token_rows, out):
    tile_expert, = tables
    w1s, w2s, b1r, b2r = weights
    FC = F // P
    UN = 4
    HB = 512
    with ExitStack() as ctx:
        m = Space(nc, ctx, "f_")
        entry = [m.sb(f"entry{u}", [P, 2]) for u in range(UN)]
        token = [m.sb(f"token{u}", [P, 1], I32) for u in range(UN)]
        row = [m.sb(f"row{u}", [P, 2, HD]) for u in range(UN)]
        xnt = [m.sb(f"xnt{u}", [P, KC, P]) for u in range(UN)]
        pre = m.sb("pre", [P, F])
        hid = m.sb("hid", [P, FC, P])
        y = m.sb("y", [P, HD])
        scaled = m.sb("scaled", [P, HD])
        is_number = m.sb("is_number", [P, HD], I32)
        is_plus = m.sb("is_plus", [P, HD], I32)
        is_minus = m.sb("is_minus", [P, HD], I32)
        plus = m.sb("plus", [P, HD])
        minus = m.sb("minus", [P, HD])
        clean = m.sb("clean", [P, HD])
        res = [m.sb(f"res{u}", [P, HD]) for u in range(UN)]
        ps_x = m.ps("ps_x", [P, 512])
        ps_h = [m.ps(f"ps_h{i}", [P, 512]) for i in range(2)]
        ps_t = [m.ps(f"ps_t{i}", [P, 512]) for i in range(2)]
        ps_y = [m.ps(f"ps_y{i}", [P, 512]) for i in range(2)]

        entry_in = [m.sem(f"entry_in{u}") for u in range(UN)]
        row_in = [m.sem(f"row_in{u}") for u in range(UN)]
        res_out = [m.sem(f"res_out{u}") for u in range(UN)]
        const_ready, turns, turns_v = m.sem("const_ready"), m.sem("turns"), m.sem("turns_v")
        token_ready, px_ready, xnt_ready = m.sem("token_ready"), m.sem("px_ready"), m.sem("xnt_ready")
        h_ready, pre_ready, t_ready, hid_ready = (
            m.sem("h_ready"), m.sem("pre_ready"), m.sem("t_ready"), m.sem("hid_ready"))
        y_ready, y_read, y_scaled, masks_ready, clean_step, res_ready = (
            m.sem("y_ready"), m.sem("y_read"), m.sem("y_scaled"), m.sem("masks_ready"), m.sem("clean_step"),
            m.sem("res_ready"))
        block = ctx.enter_context(nc.Block())

        def steps(eng, step):
            run_steps(eng, step, -3, 2 * UN, (NT - UN) // UN * UN, NT + 1, UN)

        @block.sync
        def _(sp):
            def step(t, u, q):
                if there(t + 3, NT):
                    w = (u + 3) % UN
                    at_least(sp, res_ready, t)
                    sp.dma_start(entry[w][:], slots[bass.ds((t + 3) * P, P), :]).then_inc(entry_in[w], 16)

            steps(sp, step)

        @block.gpsimd
        def _(pool):
            def step(t, u, q):
                w = (u + 2) % UN
                if there(t + 2, NT):
                    pool.wait_ge(token_ready, t + 3)
                    at_least(pool, res_ready, t - 1)
                    pool.sem_inc(turns, 1)
                    nc.gpsimd.indirect_dma_start(
                        out=row[w][:].rearrange("p a d -> p (a d)"), out_offset=None, in_=token_rows,
                        in_offset=bass.IndirectOffsetOnAxis(ap=token[w][:, 0:1], axis=0)).then_inc(row_in[w], 16)
                if there(t - 1, NT):
                    o = (u - 1) % UN
                    pool.wait_ge(res_ready, t)
                    pool.sem_inc(turns, 1)
                    nc.gpsimd.indirect_dma_start(
                        out=out, out_offset=bass.IndirectOffsetOnAxis(ap=token[o][:, 0:1], axis=0),
                        in_=res[o][:], in_offset=None, bounds_check=N - 1, oob_is_err=False).then_inc(res_out[o], 16)

            steps(pool, step)
            for u in range(UN):
                pool.wait_ge(res_out[u], 16 * len(range(u, NT, UN)))

        @block.tensor
        def _(pe):
            def step(t, u, q):
                w = (u + 1) % UN
                w2 = (u + 2) % UN
                if there(t, NT):
                    pe.wait_ge(pre_ready, 2 * (t + 1))
                    at_least(pe, hid_ready, 2 * t)
                    for c in range(FC):
                        ins = nc.tensor.transpose(ps_t[c // 4][:, (c % 4) * P:(c % 4 + 1) * P],
                                                  pre[:, c * P:(c + 1) * P], ident[:])
                        if c % 4 == 3:
                            ins.then_inc(t_ready, 1)
                if there(t + 1, NT):
                    x = pe.value_load(tile_expert[0:1, bass.ds(t + 1, 1)], min_val=0, max_val=X - 1)
                    pe.wait_ge(xnt_ready, t + 2)
                    at_least(pe, pre_ready, 2 * (t + 1))
                    for i in range(2):
                        for k in range(KC):
                            ins = nc.tensor.matmul(ps_h[i][:], xnt[w][:, k, :],
                                                   w1s[:, bass.ds(x * (KC * F) + (k * F + i * HB), HB)],
                                                   start=(k == 0), stop=(k == KC - 1))
                        ins.then_inc(h_ready, 1)
                if there(t, NT):
                    x = pe.value_load(tile_expert[0:1, bass.ds(t, 1)], min_val=0, max_val=X - 1)
                    pe.wait_ge(hid_ready, 2 * (t + 1))
                    at_least(pe, y_read, t)
                    for c in range(FC):
                        ins = nc.tensor.matmul(ps_y[0][:, 0:HD], hid[:, c, :],
                                               w2s[:, bass.ds(x * (FC * HD) + c * HD, HD)],
                                               start=(c == 0), stop=(c == FC - 1))
                    ins.then_inc(y_ready, 1)
                if there(t + 2, NT):
                    pe.wait_ge(row_in[w2], 16 * (q + (u + 2) // UN + 1))
                    at_least(pe, xnt_ready, t + 2)
                    for k in range(KC):
                        ins = nc.tensor.transpose(ps_x[:, k * P:(k + 1) * P], row[w2][:, 0, k * P:(k + 1) * P],
                                                  ident[:])
                    ins.then_inc(px_ready, 1)

            steps(pe, step)

        @block.scalar
        def _(act):
            def step(t, u, q):
                w2 = (u + 2) % UN
                if there(t, NT):
                    for i in range(2):
                        act.wait_ge(t_ready, 2 * t + i + 1)
                        at_least(act, y_ready, t)
                        nc.scalar.activation(hid[:, 4 * i:4 * (i + 1), :],
                                             ps_t[i][:].rearrange("p (c t) -> p c t", c=4),
                                             ACT.Relu).then_inc(hid_ready, 1)
                if there(t + 2, NT):
                    act.wait_ge(px_ready, t + 3)
                    at_least(act, h_ready, 2 * (t - 1))
                    nc.scalar.copy(xnt[w2][:], ps_x[:, 0:HD].rearrange("p (k t) -> p k t", k=KC)).then_inc(
                        xnt_ready, 1)

            steps(act, step)

        @block.vector
        def _(dve):
            v = nc.vector
            v.memset(plus[:], 1e4).then_inc(const_ready, 1)
            v.memset(minus[:], -1e4).then_inc(const_ready, 1)
            dve.wait_ge(const_ready, 2)

            def step(t, u, q):
                w = (u + 1) % UN
                w2 = (u + 2) % UN
                if there(t + 2, NT):
                    n = q + (u + 2) // UN
                    dve.wait_ge(entry_in[w2], 16 * (n + 1))
                    at_least(dve, res_out[w2], 16 * n)
                    v.tensor_copy(token[w2][:], entry[w2][:, 0:1]).then_inc(token_ready, 1)
                if there(t + 1, NT):
                    x = dve.value_load(tile_expert[0:1, bass.ds(t + 1, 1)], min_val=0, max_val=X - 1)
                    for i in range(2):
                        dve.wait_ge(h_ready, 2 * (t + 1) + i + 1)
                        at_least(dve, t_ready, 2 * t + 2)
                        v.tensor_tensor(pre[:, i * HB:(i + 1) * HB], ps_h[i][:],
                                        b1r[:, bass.ds(x * F + i * HB, HB)], ALU.add).then_inc(pre_ready, 1)
                if there(t, NT):
                    x = dve.value_load(tile_expert[0:1, bass.ds(t, 1)], min_val=0, max_val=X - 1)
                    dve.wait_ge(y_ready, t + 1)
                    v.tensor_tensor(y[:], ps_y[0][:, 0:HD], b2r[:, bass.ds(x * HD, HD)],
                                    ALU.add).then_inc(y_read, 1)
                    dve.wait_ge(y_read, t + 1)
                    v.tensor_scalar(scaled[:], y[:], entry[u][:, 1:2], None, ALU.mult).then_inc(y_scaled, 1)
                    v.memset(clean[:], 0.0).then_inc(masks_ready, 1)
                    dve.wait_ge(y_scaled, t + 1)
                    v.tensor_tensor(is_number[:], scaled[:], scaled[:], ALU.is_equal).then_inc(masks_ready, 1)
                    v.tensor_scalar(is_plus[:], scaled[:], float("inf"), None, ALU.is_equal).then_inc(masks_ready, 1)
                    v.tensor_scalar(is_minus[:], scaled[:], float("-inf"), None, ALU.is_equal).then_inc(masks_ready, 1)
                    dve.wait_ge(masks_ready, 4 * (t + 1))
                    dve.sem_inc(turns_v, 1)
                    v.copy_predicated(clean[:], is_number[:], scaled[:]).then_inc(clean_step, 1)
                    dve.wait_ge(clean_step, 3 * t + 1)
                    dve.sem_inc(turns_v, 1)
                    v.copy_predicated(clean[:], is_plus[:], plus[:]).then_inc(clean_step, 1)
                    dve.wait_ge(clean_step, 3 * t + 2)
                    dve.sem_inc(turns_v, 1)
                    v.copy_predicated(clean[:], is_minus[:], minus[:]).then_inc(clean_step, 1)
                    dve.wait_ge(row_in[u], 16 * (q + 1))
                    at_least(dve, res_out[u], 16 * q)
                    dve.wait_ge(clean_step, 3 * t + 3)
                    v.tensor_tensor(res[u][:], clean[:], row[u][:, 1, :], ALU.add).then_inc(res_ready, 1)

            steps(dve, step)


def gnn_then_experts(nc, x_pad, w_t, a_src, a_dst, dst_heads, dst_chunks, dst_ext, edge_ends, edge_attr_t, edge_w_t,
                     edge_b, bias, gate_w, gate_b, w1, b1, w2, b2, out):
    src_table = nc.dram_tensor("src_table", (NPAD, ROW), F32, kind="Internal").ap()
    dst_table = nc.dram_tensor("dst_table", (NPAD, 3 * VD), BF16, kind="Internal").ap()
    edge_parts = nc.dram_tensor("edge_parts", (27, EP), BF16, kind="Internal").ap()
    edge_gaps = nc.dram_tensor("edge_gaps", (EP,), F32, kind="Internal").ap()
    token_rows = nc.dram_tensor("token_rows", (NPAD + P, 2 * HD), F32, kind="Internal").ap()
    slots = nc.dram_tensor("slots", ((NT + 1) * P, 2), F32, kind="Internal").ap()
    with ExitStack() as ctx:
        m = Space(nc, ctx, "")
        ident = m.sb("ident", [P, P])
        logits = m.sb("logits", [P, NB * X])
        tile_expert = m.sb("tile_expert", [1, NT], I32)
        node_phase(nc, ident, x_pad, w_t, a_src, a_dst, edge_attr_t, src_table, dst_table, edge_parts)
        with ExitStack() as edges:
            e = Space(nc, edges, "")
            tables = (e.sb("item_edge", [1, NITEM], I32), e.sb("item_block", [1, NITEM], I32),
                      e.sb("neg_node", [P, NITEM]), e.sb("wparts", [KE, HD], BF16))
            setup_phase(nc, ident, tables, dst_heads, dst_chunks, dst_ext, edge_w_t, edge_b, edge_gaps)
            acc = e.sb("acc", [P, NB * ROW])
            edge_phase(nc, ident, tables, acc, edge_ends, dst_ext, edge_gaps, edge_parts, src_table, dst_table)
            combine_phase(nc, ident, acc, (logits,), x_pad, bias, gate_w, gate_b, token_rows)
        weights = (m.sb("w1s", [P, X * KC * F]), m.sb("w2s", [P, X * F // P * HD]), m.sb("b1r", [P, X * F]),
                   m.sb("b2r", [P, X * HD]))
        route_phase(nc, (logits,), (tile_expert,), slots, weights, (w1, w2, b1, b2), token_rows)
        expert_phase(nc, ident, (tile_expert,), weights, slots, token_rows, out)


def kernel(x, src, dst, edge_attr_3, L0_gnn_W, L0_gnn_a_src, L0_gnn_a_dst, L0_gnn_edge_W, L0_gnn_edge_b,
           L0_gnn_bias, L0_ffn_gate_w, L0_ffn_gate_b, L0_ffn_w1, L0_ffn_b1, L0_ffn_w2, L0_ffn_b2):
    import numpy as np
    import concourse.bacc as bacc
    from concourse.bass_utils import run_bass_kernel_spmd

    def padded(a, before, after, fill):
        a = np.asarray(a)
        wide = np.full(a.shape[:-1] + (before + a.shape[-1] + after,), fill, a.dtype)
        wide[..., before:before + a.shape[-1]] = a
        return wide

    dst = np.asarray(dst)
    x = np.asarray(x)
    x_pad = np.zeros((NPAD, IN), x.dtype)
    x_pad[:N] = x
    dst_pad = padded(dst, 0, EP - E, SENTINEL)
    layout = {
        "x_pad": x_pad,
        "w_t": np.asarray(L0_gnn_W).T,
        "a_src": np.asarray(L0_gnn_a_src).reshape(1, HD),
        "a_dst": np.asarray(L0_gnn_a_dst).reshape(1, HD),
        "dst_heads": dst_pad[::P].reshape(1, NCHUNK),
        "dst_chunks": dst_pad.reshape(NCHUNK, P),
        "dst_ext": padded(padded(dst, 1, 0, -1), 0, EP - E, SENTINEL),
        "edge_ends": np.stack([padded(src, 0, EP - E, 0), dst_pad, padded(dst[1:], 0, EP - E + 1, SENTINEL)],
                              axis=1).reshape(EP * 3),
        "edge_attr_t": padded(np.asarray(edge_attr_3).T, 0, EP - E, 0),
        "edge_w_t": np.asarray(L0_gnn_edge_W).T,
        "edge_b": np.asarray(L0_gnn_edge_b).reshape(1, HD),
        "bias": np.asarray(L0_gnn_bias).reshape(1, HD),
        "gate_w": np.asarray(L0_ffn_gate_w),
        "gate_b": np.asarray(L0_ffn_gate_b).reshape(1, X),
        "w1": np.asarray(L0_ffn_w1),
        "b1": np.asarray(L0_ffn_b1).reshape(1, X * F),
        "w2": np.asarray(L0_ffn_w2),
        "b2": np.asarray(L0_ffn_b2).reshape(1, X * HD),
    }
    nc = bacc.Bacc("TRN2", target_bir_lowering=False, num_devices=1)
    arrays, args = {}, {}
    for name, a in layout.items():
        a = np.ascontiguousarray(a)
        arrays["in_" + name] = a
        args[name] = nc.dram_tensor("in_" + name, a.shape, mybir.dt.from_np(a.dtype), kind="ExternalInput").ap()
    out = nc.dram_tensor("out_0", (N, HD), F32, kind="ExternalOutput").ap()
    gnn_then_experts(nc, out=out, **args)
    r = run_bass_kernel_spmd(nc, [arrays], core_ids=[0])
    return r.results[0]["out_0"]
```
